# Optimizing a Trainium2 kernel written in Bass

```python
import numpy as np
import jax
import jax.numpy as jnp

def _softmax(x, axis=-1):
    return jax.nn.softmax(x, axis=axis)

def _gelu(x):
    return jax.nn.gelu(x, approximate=True)

def _silu(x):
    return jax.nn.silu(x)

def _sigmoid(x):
    return jax.nn.sigmoid(x)

def _layernorm(x, axis=-1, eps=1e-05):
    m = jnp.mean(x, axis=axis, keepdims=True)
    v = jnp.var(x, axis=axis, keepdims=True)
    return (x - m) / jnp.sqrt(v + eps)

def _scatter_add(tgt, idx, src, axis=0):
    return tgt.at[idx].add(src)

def _segment_sum(src, seg, n):
    return jax.ops.segment_sum(src, seg, n)
kernel_name = 'mk_gnn_ffn_d2_gnn_r8_c95619'

def setup_inputs(seed: int=0):
    np.random.seed(seed)
    _w = jnp.asarray

    def _rec_inputs():
        import jax
        import jax.numpy as jnp
        _gk = jax.random.key(seed)
        x = -0.0003713 + 1 * jax.random.normal(jax.random.fold_in(_gk, 1), (6250, 256), jnp.float32)
        _s = jax.random.randint(jax.random.fold_in(_gk, 2), (50000,), 0, 6250, jnp.int32)
        _d = jax.random.randint(jax.random.fold_in(_gk, 3), (50000,), 0, 6250, jnp.int32)
        _loop = jnp.arange(6250, dtype=jnp.int32)
        src = jnp.concatenate([_s, _d, _loop])
        dst = jnp.concatenate([_d, _s, _loop])
        _o = jnp.argsort(dst, stable=True)
        src = src[_o]
        dst = dst[_o]
        return (x, src, dst)
    x, src, dst = _rec_inputs()

    def _L0_gnn_setup():
        import jax, jax.numpy as jnp
        import numpy as np
        N = 6250
        E = 100000
        IN = 256
        HD = 4
        D = 64
        key = jax.random.key(seed)
        k1, k2, k3, k4, k5 = jax.random.split(key, 5)
        h = jax.random.normal(k1, (N, IN), dtype=jnp.float32)
        edge_index = jax.random.randint(k2, (2, E), 0, N)
        W = jax.random.normal(k3, (IN, HD * D), dtype=jnp.float32) * (1.0 / np.sqrt(IN))
        a_src = jax.random.normal(k4, (HD, D), dtype=jnp.float32) * 0.1
        a_dst = jax.random.normal(k5, (HD, D), dtype=jnp.float32) * 0.1
        return {'h': h, 'edge_index': edge_index, 'W': W, 'a_src': a_src, 'a_dst': a_dst}
    _L0_gnn_all = _L0_gnn_setup()
    _L0_gnn_in = {k: v for k, v in _L0_gnn_all.items() if k in ('W', 'a_src', 'a_dst')}
    del _L0_gnn_all

    def _L0_ffn_setup():
        import math
        import jax, jax.numpy as jnp
        import numpy as np
        CAPACITY_FACTOR = 1.25
        TOP_K = 2
        LN_EPS = 1e-05

        def _layer_norm(x, gamma, beta):
            mu = jnp.mean(x, axis=-1, keepdims=True)
            var = jnp.var(x, axis=-1, keepdims=True)
            return (x - mu) * jax.lax.rsqrt(var + LN_EPS) * gamma + beta
        key = jax.random.key(seed)
        ks = jax.random.split(key, 4)
        B, S, D, F, E = (8, 512, 256, 512, 8)
        x = jax.random.normal(ks[0], (B, S, D), dtype=jnp.float32)
        Wr = jax.random.normal(ks[1], (D, E), dtype=jnp.float32) / np.sqrt(D)
        br = jnp.zeros((E,), jnp.float32)
        W1 = jax.random.normal(ks[2], (E, D, F), dtype=jnp.float32) / np.sqrt(D)
        b1 = jnp.zeros((E, F), jnp.float32)
        W2 = jax.random.normal(ks[3], (E, F, D), dtype=jnp.float32) / np.sqrt(F)
        b2 = jnp.zeros((E, D), jnp.float32)
        gamma = jnp.ones((D,), jnp.float32)
        beta = jnp.zeros((D,), jnp.float32)
        return {'x': x, 'Wr': Wr, 'br': br, 'W1': W1, 'b1': b1, 'W2': W2, 'b2': b2, 'gamma': gamma, 'beta': beta}
    _L0_ffn_all = _L0_ffn_setup()
    _L0_ffn_in = {k: v for k, v in _L0_ffn_all.items() if k in ('Wr', 'br', 'W1', 'b1', 'W2', 'b2', 'gamma', 'beta')}
    del _L0_ffn_all

    def _L1_gnn_setup():
        import jax, jax.numpy as jnp
        import numpy as np
        N_NODES = 6250
        N_EDGES = 100000
        IN_CH = 256
        HID_CH = 256
        OUT_CH = 256
        N_LAYERS = 3
        key = jax.random.key(seed)
        ks = jax.random.split(key, 8)
        s_in = 1.0 / np.sqrt(IN_CH)
        s_h = 1.0 / np.sqrt(HID_CH)
        return {'x': jax.random.normal(ks[0], (N_NODES, IN_CH), dtype=jnp.float32), 'W_in': jax.random.normal(ks[1], (IN_CH, HID_CH), dtype=jnp.float32) * s_in, 'b_in': jnp.zeros((HID_CH,), dtype=jnp.float32), 'W_agg': jax.random.normal(ks[2], (N_LAYERS, HID_CH, HID_CH), dtype=jnp.float32) * s_h, 'W_self': jax.random.normal(ks[3], (N_LAYERS, HID_CH, HID_CH), dtype=jnp.float32) * s_h, 'b_hid': jnp.zeros((N_LAYERS, HID_CH), dtype=jnp.float32), 'W_out': jax.random.normal(ks[4], (HID_CH, OUT_CH), dtype=jnp.float32) * s_h, 'b_out': jnp.zeros((OUT_CH,), dtype=jnp.float32), 'edge_index': jax.random.randint(ks[5], (2, N_EDGES), 0, N_NODES, dtype=jnp.int64)}
    _L1_gnn_all = _L1_gnn_setup()
    _L1_gnn_in = {k: v for k, v in _L1_gnn_all.items() if k in ('W_in', 'b_in', 'W_agg', 'W_self', 'b_hid', 'W_out', 'b_out')}
    del _L1_gnn_all

    def _L1_ffn_setup():
        import jax, jax.numpy as jnp
        import numpy as np
        B, N, D = (16, 512, 256)
        NUM_EXPERTS, TOP_K, HEADS = (4, 2, 4)
        N_EDGES = 131072
        LN_EPS = 1e-05

        def _layernorm(x, g, b):
            mu = x.mean(-1, keepdims=True)
            var = ((x - mu) ** 2).mean(-1, keepdims=True)
            return (x - mu) * jax.lax.rsqrt(var + LN_EPS) * g + b

        def _forward(x, edge_index, W_gat, att_src, att_dst, b_gat, ln_gamma, ln_beta, W1, b1, W2, b2):
            Bc, Nc, Dc = x.shape
            M = Bc * Nc
            x_flat = x.reshape(M, Dc)
            h = (x_flat @ W_gat).reshape(M, HEADS, NUM_EXPERTS)
            loops = jnp.arange(M, dtype=edge_index.dtype)
            src = jnp.concatenate([edge_index[0], loops])
            dst = jnp.concatenate([edge_index[1], loops])
            a_src = (h * att_src).sum(-1)
            a_dst = (h * att_dst).sum(-1)
            e = jax.nn.leaky_relu(a_src[src] + a_dst[dst], negative_slope=0.2)
            e_max = jax.ops.segment_max(e, dst, num_segments=M)
            ee = jnp.exp(e - e_max[dst])
            denom = jax.ops.segment_sum(ee, dst, num_segments=M)
            alpha = ee / (denom[dst] + 1e-16)
            msg = h[src] * alpha[:, :, None]
            agg = jax.ops.segment_sum(msg, dst, num_segments=M).reshape(M, HEADS * NUM_EXPERTS) + b_gat
            scores = _layernorm(agg, ln_gamma, ln_beta).reshape(M, HEADS, NUM_EXPERTS).mean(1)
            scores = scores.reshape(Bc, Nc, NUM_EXPERTS)
            topk_s, topk_i = jax.lax.top_k(scores, TOP_K)
            w = jax.nn.softmax(topk_s, axis=-1)
            out = jnp.zeros_like(x)
            for ei in range(NUM_EXPERTS):
                g = jnp.where(topk_i == ei, w, 0.0).sum(-1)
                hh = jax.nn.gelu(x @ W1[ei] + b1[ei], approximate=False)
                out = out + g[..., None] * (hh @ W2[ei] + b2[ei])
            return out
        key = jax.random.key(seed)
        ks = jax.random.split(key, 8)
        s = 0.05
        return {'x': jax.random.normal(ks[0], (B, N, D), jnp.float32), 'W_gat': jax.random.normal(ks[1], (D, HEADS * NUM_EXPERTS), jnp.float32) * s, 'att_src': jax.random.normal(ks[2], (HEADS, NUM_EXPERTS), jnp.float32) * s, 'att_dst': jax.random.normal(ks[3], (HEADS, NUM_EXPERTS), jnp.float32) * s, 'b_gat': jnp.zeros((HEADS * NUM_EXPERTS,), jnp.float32), 'ln_gamma': jnp.ones((HEADS * NUM_EXPERTS,), jnp.float32), 'ln_beta': jnp.zeros((HEADS * NUM_EXPERTS,), jnp.float32), 'W1': jax.random.normal(ks[4], (NUM_EXPERTS, D, 2 * D), jnp.float32) * s, 'b1': jnp.zeros((NUM_EXPERTS, 2 * D), jnp.float32), 'W2': jax.random.normal(ks[5], (NUM_EXPERTS, 2 * D, D), jnp.float32) * s, 'b2': jnp.zeros((NUM_EXPERTS, D), jnp.float32), 'edge_index': jax.random.randint(ks[6], (2, N_EDGES), 0, B * N, jnp.int32)}
    _L1_ffn_all = _L1_ffn_setup()
    _L1_ffn_in = {k: v for k, v in _L1_ffn_all.items() if k in ('W_gat', 'att_src', 'att_dst', 'b_gat', 'ln_gamma', 'ln_beta', 'W1', 'b1', 'W2', 'b2', 'edge_index')}
    del _L1_ffn_all
    return {'x': x, 'src': src, 'dst': dst, 'L0_gnn_W': _L0_gnn_in['W'], 'L0_gnn_a_src': _L0_gnn_in['a_src'], 'L0_gnn_a_dst': _L0_gnn_in['a_dst'], 'L0_ffn_Wr': _L0_ffn_in['Wr'], 'L0_ffn_br': _L0_ffn_in['br'], 'L0_ffn_W1': _L0_ffn_in['W1'], 'L0_ffn_b1': _L0_ffn_in['b1'], 'L0_ffn_W2': _L0_ffn_in['W2'], 'L0_ffn_b2': _L0_ffn_in['b2'], 'L0_ffn_gamma': _L0_ffn_in['gamma'], 'L0_ffn_beta': _L0_ffn_in['beta'], 'L1_gnn_W_in': _L1_gnn_in['W_in'], 'L1_gnn_b_in': _L1_gnn_in['b_in'], 'L1_gnn_W_agg': _L1_gnn_in['W_agg'], 'L1_gnn_W_self': _L1_gnn_in['W_self'], 'L1_gnn_b_hid': _L1_gnn_in['b_hid'], 'L1_gnn_W_out': _L1_gnn_in['W_out'], 'L1_gnn_b_out': _L1_gnn_in['b_out'], 'L1_ffn_W_gat': _L1_ffn_in['W_gat'], 'L1_ffn_att_src': _L1_ffn_in['att_src'], 'L1_ffn_att_dst': _L1_ffn_in['att_dst'], 'L1_ffn_b_gat': _L1_ffn_in['b_gat'], 'L1_ffn_ln_gamma': _L1_ffn_in['ln_gamma'], 'L1_ffn_ln_beta': _L1_ffn_in['ln_beta'], 'L1_ffn_W1': _L1_ffn_in['W1'], 'L1_ffn_b1': _L1_ffn_in['b1'], 'L1_ffn_W2': _L1_ffn_in['W2'], 'L1_ffn_b2': _L1_ffn_in['b2'], 'L1_ffn_edge_index': _L1_ffn_in['edge_index']}

def reference(x, src, dst, L0_gnn_W, L0_gnn_a_src, L0_gnn_a_dst, L0_ffn_Wr, L0_ffn_br, L0_ffn_W1, L0_ffn_b1, L0_ffn_W2, L0_ffn_b2, L0_ffn_gamma, L0_ffn_beta, L1_gnn_W_in, L1_gnn_b_in, L1_gnn_W_agg, L1_gnn_W_self, L1_gnn_b_hid, L1_gnn_W_out, L1_gnn_b_out, L1_ffn_W_gat, L1_ffn_att_src, L1_ffn_att_dst, L1_ffn_b_gat, L1_ffn_ln_gamma, L1_ffn_ln_beta, L1_ffn_W1, L1_ffn_b1, L1_ffn_W2, L1_ffn_b2, L1_ffn_edge_index):
    import jax
    import jax.numpy as jnp

    def _L0_gnn_ref(h, edge_index, W, a_src, a_dst):
        import jax, jax.numpy as jnp
        import numpy as np
        N = 6250
        E = 100000
        IN = 256
        HD = 4
        D = 64
        n = h.shape[0]
        src, dst = (edge_index[0], edge_index[1])
        hp = (h @ W).reshape(n, HD, D)
        e_src = jnp.einsum('ehd,hd->eh', hp[src], a_src)
        e_dst = jnp.einsum('ehd,hd->eh', hp[dst], a_dst)
        e = jax.nn.leaky_relu(e_src + e_dst, negative_slope=0.2)
        e_max = jax.ops.segment_max(e, dst, num_segments=n)
        ex = jnp.exp(e - e_max[dst])
        e_sum = jax.ops.segment_sum(ex, dst, num_segments=n)
        alpha = ex / (e_sum[dst] + 1e-16)
        msg = hp[src] * alpha[..., None]
        out = jax.ops.segment_sum(msg, dst, num_segments=n)
        return out.reshape(n, HD * D)

    def _L0_ffn_ref(x, Wr, br, W1, b1, W2, b2, gamma, beta):
        import math
        import jax, jax.numpy as jnp
        import numpy as np
        CAPACITY_FACTOR = 1.25
        TOP_K = 2
        LN_EPS = 1e-05

        def _layer_norm(x, gamma, beta):
            mu = jnp.mean(x, axis=-1, keepdims=True)
            var = jnp.var(x, axis=-1, keepdims=True)
            return (x - mu) * jax.lax.rsqrt(var + LN_EPS) * gamma + beta
        B, S, D = x.shape
        E = Wr.shape[1]
        N = B * S
        K = TOP_K
        logits = jnp.mean(x, axis=1) @ Wr + br
        routing_weights = jax.nn.softmax(logits, axis=-1)
        capacity = float(math.ceil(N * CAPACITY_FACTOR / E))
        expected_loads = routing_weights.sum(axis=0) * (N / B)
        scale = jnp.where(expected_loads > capacity, capacity / expected_loads, 1.0)
        routing_weights = jax.nn.softmax(routing_weights * scale, axis=-1)
        rw_tok = jnp.broadcast_to(routing_weights[:, None, :], (B, S, E)).reshape(N, E)
        top_w, top_i = jax.lax.top_k(rw_tok, K)
        top_w = jax.nn.softmax(top_w, axis=-1)
        xf = x.reshape(N, D)
        h = jax.nn.gelu(jnp.einsum('nd,edf->enf', xf, W1) + b1[:, None, :], approximate=False)
        y = jnp.einsum('enf,efd->end', h, W2) + b2[:, None, :]
        w_dense = jnp.zeros((N, E), x.dtype).at[jnp.arange(N)[:, None], top_i].add(top_w)
        out = jnp.einsum('ne,end->nd', w_dense, y).reshape(B, S, D)
        out = _layer_norm(out + x, gamma, beta)
        return out

    def _L1_gnn_ref(x, W_in, b_in, W_agg, W_self, b_hid, W_out, b_out, edge_index):
        import jax, jax.numpy as jnp
        import numpy as np
        N_NODES = 6250
        N_EDGES = 100000
        IN_CH = 256
        HID_CH = 256
        OUT_CH = 256
        N_LAYERS = 3
        n = x.shape[0]
        dst = edge_index[0]
        src = edge_index[1]
        n_layers = W_agg.shape[0]
        h = x @ W_in + b_in
        deg = jax.ops.segment_sum(jnp.ones_like(dst, dtype=h.dtype), dst, num_segments=n)
        deg = jnp.maximum(deg, 1.0)[:, None]
        for l in range(n_layers):
            agg = jax.ops.segment_sum(h[src], dst, num_segments=n) / deg
            h = jax.nn.relu(agg @ W_agg[l] + h @ W_self[l] + b_hid[l])
        return h @ W_out + b_out

    def _L1_ffn_ref(x, W_gat, att_src, att_dst, b_gat, ln_gamma, ln_beta, W1, b1, W2, b2, edge_index):
        import jax, jax.numpy as jnp
        import numpy as np
        B, N, D = (16, 512, 256)
        NUM_EXPERTS, TOP_K, HEADS = (4, 2, 4)
        N_EDGES = 131072
        LN_EPS = 1e-05

        def _layernorm(x, g, b):
            mu = x.mean(-1, keepdims=True)
            var = ((x - mu) ** 2).mean(-1, keepdims=True)
            return (x - mu) * jax.lax.rsqrt(var + LN_EPS) * g + b

        def _forward(x, edge_index, W_gat, att_src, att_dst, b_gat, ln_gamma, ln_beta, W1, b1, W2, b2):
            Bc, Nc, Dc = x.shape
            M = Bc * Nc
            x_flat = x.reshape(M, Dc)
            h = (x_flat @ W_gat).reshape(M, HEADS, NUM_EXPERTS)
            loops = jnp.arange(M, dtype=edge_index.dtype)
            src = jnp.concatenate([edge_index[0], loops])
            dst = jnp.concatenate([edge_index[1], loops])
            a_src = (h * att_src).sum(-1)
            a_dst = (h * att_dst).sum(-1)
            e = jax.nn.leaky_relu(a_src[src] + a_dst[dst], negative_slope=0.2)
            e_max = jax.ops.segment_max(e, dst, num_segments=M)
            ee = jnp.exp(e - e_max[dst])
            denom = jax.ops.segment_sum(ee, dst, num_segments=M)
            alpha = ee / (denom[dst] + 1e-16)
            msg = h[src] * alpha[:, :, None]
            agg = jax.ops.segment_sum(msg, dst, num_segments=M).reshape(M, HEADS * NUM_EXPERTS) + b_gat
            scores = _layernorm(agg, ln_gamma, ln_beta).reshape(M, HEADS, NUM_EXPERTS).mean(1)
            scores = scores.reshape(Bc, Nc, NUM_EXPERTS)
            topk_s, topk_i = jax.lax.top_k(scores, TOP_K)
            w = jax.nn.softmax(topk_s, axis=-1)
            out = jnp.zeros_like(x)
            for ei in range(NUM_EXPERTS):
                g = jnp.where(topk_i == ei, w, 0.0).sum(-1)
                hh = jax.nn.gelu(x @ W1[ei] + b1[ei], approximate=False)
                out = out + g[..., None] * (hh @ W2[ei] + b2[ei])
            return out
        return _forward(x, edge_index, W_gat, att_src, att_dst, b_gat, ln_gamma, ln_beta, W1, b1, W2, b2)
    edge_index = jnp.stack([src, dst])
    x = x + _L0_gnn_ref(_layernorm(x, axis=-1), edge_index, L0_gnn_W, L0_gnn_a_src, L0_gnn_a_dst)
    x = x + _L0_ffn_ref(_layernorm(x, axis=-1)[None], L0_ffn_Wr, L0_ffn_br, L0_ffn_W1, L0_ffn_b1, L0_ffn_W2, L0_ffn_b2, L0_ffn_gamma, L0_ffn_beta)[0]
    x = x + _L1_gnn_ref(_layernorm(x, axis=-1), L1_gnn_W_in, L1_gnn_b_in, L1_gnn_W_agg, L1_gnn_W_self, L1_gnn_b_hid, L1_gnn_W_out, L1_gnn_b_out, edge_index)
    x = x + _L1_ffn_ref(_layernorm(x, axis=-1)[None], L1_ffn_W_gat, L1_ffn_att_src, L1_ffn_att_dst, L1_ffn_b_gat, L1_ffn_ln_gamma, L1_ffn_ln_beta, L1_ffn_W1, L1_ffn_b1, L1_ffn_W2, L1_ffn_b2, L1_ffn_edge_index)[0]
    return x

_drawn_inputs = setup_inputs


def setup_inputs(seed=0):
    import zlib

    import numpy as np

    out = dict(_drawn_inputs(seed))
    spreads = {'L0_ffn_br': (0.0, 0.8),
     'L0_ffn_b1': (0.0, 0.281),
     'L0_ffn_b2': (0.0, 0.1),
     'L0_ffn_gamma': (1.0, 0.2),
     'L0_ffn_beta': (0.0, 0.1),
     'L1_gnn_b_in': (0.0, 0.1),
     'L1_gnn_b_hid': (0.0, 0.1),
     'L1_gnn_b_out': (0.0, 0.1),
     'L1_ffn_b_gat': (0.0, 0.1),
     'L1_ffn_ln_gamma': (1.0, 0.2),
     'L1_ffn_ln_beta': (0.0, 0.1),
     'L1_ffn_b1': (0.0, 0.274),
     'L1_ffn_b2': (0.0, 0.1)}
    factors = {'L0_ffn_Wr': 64.0, 'L1_ffn_att_src': 3.188, 'L1_ffn_att_dst': 5.198}
    for name, (base, spread) in spreads.items():
        noise = np.random.default_rng([zlib.crc32(name.encode()), seed]).standard_normal(out[name].shape)
        drawn = base * np.exp(spread * noise) if base else spread * noise
        out[name] = jnp.asarray(drawn.astype(out[name].dtype))
    for name, factor in factors.items():
        out[name] = (out[name] * factor).astype(out[name].dtype)
    return out
```

```python
from contextlib import ExitStack

import numpy as np

import concourse.bass as bass
from concourse import mybir

ALU = mybir.AluOpType
ACT = mybir.ActivationFunctionType
AX = mybir.AxisListType
F32 = mybir.dt.float32
BF16 = mybir.dt.bfloat16
I32 = mybir.dt.int32
U8 = mybir.dt.uint8

P = 128
N = 6250
D = 256
EB = -(-N // P)
NB = EB + 1
NP = NB * P
ACCW = D + 4
FFN_F = 512
IDBITS = 13
IDMASK = (1 << IDBITS) - 1
KEYTOP = 0x40000000
BIG = 1.0e30
GRP = 8

GRAPHS = [dict(c=1024, tq=7, t=880), dict(c=1024, tq=7, t=880), dict(c=2048, tq=9, t=1136)]
for _g in GRAPHS:
    _g["rows"] = _g["c"]
    assert _g["tq"] * P >= _g["t"] and _g["t"] % (2 * GRP) == 0


def host_constants():
    p = np.arange(P)
    sign = lambda r: 1.0 - 2.0 * ((p >> r) & 1)
    flips = np.concatenate([sign(r - 1) * sign(r) for r in range(1, 8)])
    limits = (KEYTOP | (((np.arange(EB) + 1) * P) << IDBITS)).astype(np.int32).view(np.float32)
    every = lambda row: np.broadcast_to(row, (P, len(row)))
    parts = [("ident", np.eye(P)), ("ones", np.ones((P, P))), ("iota", every(p)), ("pcol", p[:, None]),
             ("sign0", sign(0)[:, None]), ("limits", every(limits))]
    for tq in (7, 9):
        parts.append((f"tile{tq}", p[:, None] * tq + np.arange(tq)[None, :]))
    at, where = 0, {}
    for name, a in parts:
        where[name] = (at, at + a.shape[1])
        at += a.shape[1]
    return np.concatenate([np.asarray(a, np.float32) for _, a in parts], 1), where, every(flips).astype(np.float32)


def build_program(nc, A, out, consts, flips, where):
    with ExitStack() as ctx:
        def sb(name, shape, dt=F32):
            return ctx.enter_context(nc.sbuf_tensor(name, shape, dt))

        def sem(name):
            return ctx.enter_context(nc.semaphore(name))

        def dram(name, shape, dt=F32):
            return nc.dram_tensor(name, shape, dt, kind="Internal").ap()

        ncon = consts.shape[1]
        CON = sb("CON", [P, ncon])
        con = lambda name: CON[:, where[name][0]:where[name][1]]
        IDENT, ONES, IOTA, PCOL = con("ident"), con("ones"), con("iota"), con("pcol")
        X = sb("X", [P, NB, D])
        xflat = X[:, :, :].rearrange("p b d -> p (b d)")
        ARENA = sb("ARENA", [P, 36104])
        ACC0, H0, WS0, GR0, S0 = 0, 13000, 25800, 29896, 34056
        ar = lambda a, n: ARENA[:, a:a + n]
        ACCv = ar(ACC0, NB * ACCW).rearrange("p (b w) -> p b w", w=ACCW)
        Hv = ar(H0, NB * D).rearrange("p (b d) -> p b d", d=D)
        Sv = ar(S0, 2 * GRP * P).rearrange("p (h t n) -> p h t n", h=2, t=GRP)
        RELE = sb("RELE", [P, 1152])
        SRCE = sb("SRCE", [P, 1160])
        srce_i = SRCE[:, 0:1152].bitcast(I32)
        BT = sb("BT", [1, 1152], U8)
        IDX = sb("IDX", [P, 2, GRP], I32)
        EDN = sb("EDN", [P, NB, 4])
        ESN = sb("ESN", [P, NB, 4])
        SM = ar(ACC0 + 11000, 420)
        FLIPS = ar(GR0 + 2048, 7 * P)
        LOOPS = sb("LOOPS", [125, 50], I32)
        loops_ready = sem("loops_ready")
        PB = [ctx.enter_context(nc.psum_tensor(f"PB{i}", [P, 512], F32)) for i in range(8)]

        tabD = dram("tabD", (NP, D))
        esD = dram("esD", (NP, 4))
        t20D = dram("t20D", (NP, 20))
        keysD = [dram(f"keysD{g}", (G["rows"], P), I32) for g, G in enumerate(GRAPHS)]
        relD = [dram(f"relD{g}", (1, G["tq"] * P * P), BF16) for g, G in enumerate(GRAPHS)]
        releD = [dram(f"releD{g}", (P, G["tq"] * P)) for g, G in enumerate(GRAPHS)]
        srceD = [dram(f"srceD{g}", (P, G["tq"] * P), I32) for g, G in enumerate(GRAPHS)]
        dstD = [dram(f"dstD{g}", (P, G["tq"] * P)) for g, G in enumerate(GRAPHS)]
        btD = [dram(f"btD{g}", (P, G["tq"]), U8) for g, G in enumerate(GRAPHS)]

        met = sem("met")
        asked, answered = sem("asked"), sem("answered")
        loaded = sem("loaded")
        sp_go = sem("sp_go")
        pool_go, pool_done = sem("pool_go"), sem("pool_done")
        MEETING = 5
        counts = {}

        def nth(name):
            counts[name] = counts.get(name, 0) + 1
            return counts[name]

        def pairs_of(eng, n, body):
            for h in (0, 1):
                body(0, h, True)
            with eng.Fori(1, n) as i:
                for h in (0, 1):
                    body(i, h, False)

        sp_key = sem("sp_key")
        key_room = sem("key_room")
        KA, KB = ar(WS0, 2048), ar(WS0 + 2048, 2048)

        def key_buffers(g):
            C = GRAPHS[g]["c"]
            return KA[:, 0:C].bitcast(I32), KB[:, 0:C].bitcast(I32)

        def key_sources(g):
            if g == 0:
                return A["dst"], A["src"]
            if g == 1:
                return A["src"], A["dst"]
            return A["L1_ffn_edge_index"][1, :], A["L1_ffn_edge_index"][0, :]

        def sort_sync(sp, g):
            dsts, srcs = key_sources(g)
            n = dsts.shape[0]
            rows = 125 if g < 2 else P
            sp.wait_ge(key_room, g + 1)
            for buf, a in zip(key_buffers(g), (dsts, srcs)):
                sp.dma_start(buf[0:rows, 0:n // rows], a.rearrange("(p c) -> p c", p=rows)).then_inc(sp_key, 16)

        def sort_vector(dve, g):
            C = GRAPHS[g]["c"]
            dst_i, src_i = key_buffers(g)
            dve.memset(dst_i, IDMASK)
            dve.memset(src_i, IDMASK)
            dve.drain().then_inc(key_room, 1)
            if g == 2:
                dve.wait_ge(loops_ready, 1)
                dve.tensor_copy(dst_i[0:125, 1024:1074], LOOPS[:, :])
                dve.tensor_copy(src_i[0:125, 1024:1074], LOOPS[:, :])
                dve.drain()
            dve.wait_ge(sp_key, 32 * (g + 1))
            dve.scalar_tensor_tensor(out=dst_i, in0=dst_i, scalar=IDBITS, in1=src_i,
                                     op0=ALU.logical_shift_left, op1=ALU.bitwise_or)
            dve.drain()
            dve.tensor_scalar(dst_i, dst_i, KEYTOP, None, ALU.bitwise_or)
            dve.drain()
            bufs = [KA[:, 0:C], KB[:, 0:C]]
            dve.tensor_scalar(bufs[1], bufs[0], con("sign0"), None, ALU.mult)
            dve.drain()
            cur = 1

            def exchange(lo, hi, olo, ohi):
                dve.tensor_tensor(olo, lo, hi, ALU.min)
                dve.tensor_tensor(ohi, lo, hi, ALU.max)
                dve.drain()

            def step(s):
                nonlocal cur
                v = bufs[cur].rearrange("p (n two s) -> p n two s", two=2, s=s)
                w = bufs[1 - cur].rearrange("p (n two s) -> p n two s", two=2, s=s)
                exchange(v[:, :, 0, :], v[:, :, 1, :], w[:, :, 0, :], w[:, :, 1, :])
                cur = 1 - cur

            def mirror(size):
                nonlocal cur
                v = bufs[cur].rearrange("p (n s) -> p n s", s=size)
                w = bufs[1 - cur].rearrange("p (n s) -> p n s", s=size)
                h = size // 2
                exchange(v[:, :, 0:h], v[:, :, size - 1:h - 1:-1] , w[:, :, 0:h], w[:, :, size - 1:h - 1:-1])
                cur = 1 - cur

            size = 2
            while size <= C:
                if size == 2:
                    step(1)
                else:
                    mirror(size)
                    s = size // 4
                    while s >= 1:
                        step(s)
                        s //= 2
                size *= 2
            for r in range(1, 8):
                turned[g].append(cur)
                dve.drain().then_inc(asked, 1)
                dve.wait_ge(answered, nth("answers"))
                flip = FLIPS[:, (r - 1) * P:r * P]
                for k in range(C // 512):
                    dve.tensor_tensor(bufs[1 - cur][:, k * 512:(k + 1) * 512].rearrange("p (a b) -> p a b", b=P),
                                      PB[4 + k][:, :].rearrange("p (a b) -> p a b", b=P),
                                      flip.rearrange("p (a b) -> p a b", a=1).to_broadcast([P, 4, P]), ALU.mult)
                dve.drain()
                cur = 1 - cur
                s = 1 << (r - 1)
                while s >= 1:
                    step(s)
                    s //= 2
                turned[g].append(cur)
                dve.drain().then_inc(asked, 1)
                dve.wait_ge(answered, nth("answers"))
                for k in range(C // 512):
                    dve.tensor_copy(bufs[1 - cur][:, k * 512:(k + 1) * 512], PB[4 + k][:, :])
                dve.drain()
                cur = 1 - cur
                s = C // 2
                while s >= 1:
                    step(s)
                    s //= 2
            turned[g].append(cur)
            return cur

        def sort_tensor(pe, g):
            C = GRAPHS[g]["c"]
            bufs = [KA, KB]
            for cur in turned[g][:-1]:
                pe.wait_ge(asked, nth("questions"))
                for k in range(C // P):
                    t = pe.transpose(PB[4 + k // 4][:, (k % 4) * P:(k % 4 + 1) * P], bufs[cur][:, k * P:(k + 1) * P], IDENT)
                t.then_inc(answered, 1)

        turned = {g: [] for g in range(3)}

        start_f, nt_f, cum_f, doff_f = SM[:, 0:50], SM[:, 50:100], SM[:, 100:150], SM[:, 150:200]
        cnt_f, re_f = SM[:, 200:250], SM[:, 250:300]
        off_f, bt_f, junk_f, rs_f = SM[:, 300:309], SM[:, 310:319], SM[:, 320:370], SM[:, 370:420]
        ti = sb("ti", [P, 50], I32)
        rowi = [sb(f"rowi{g}", [P, 9], I32) for g in range(3)]
        bt128 = [sb(f"bt128_{g}", [P, 9]) for g in range(3)]
        bt8 = sb("bt8", [P, 9], U8)
        TT0 = ACC0
        RAW = ar(TT0, 1152).bitcast(I32)
        TMPI = ar(TT0 + 1152, 1152).bitcast(I32)
        SRCF, DSTF, RELF = ar(TT0 + 2304, 1152), ar(TT0 + 3456, 1152), ar(TT0 + 4608, 1152)
        RELB = ar(TT0 + 5760, 576).bitcast(BF16)
        TREL = ar(TT0 + 6336, 1152)
        TSRC = ar(TT0 + 7488, 1152).bitcast(I32)
        rows_ready = sem("rows_ready")
        keys_kept = sem("keys_kept")
        raw_sem = [sem(f"raw_sem{g}") for g in range(3)]
        raw_free = sem("raw_free")
        keep_done = sem("keep_done")

        def count_vector(dve, g, cur):
            G = GRAPHS[g]
            C, tq = G["c"], G["tq"]
            keys, junk = (KA, KB) if cur == 0 else (KB, KA)
            dve.drain().then_inc(sp_go, 1)
            dve.memset(cnt_f[:, 0:1], 0.0)
            lim = con("limits")
            with dve.Fori(0, 7) as i:
                for j in range(7):
                    dve.tensor_scalar(junk[:, 0:C], keys[:, 0:C], lim[:, bass.ds(7 * i + j, 1)], None,
                                      ALU.is_lt, ALU.add, accum_out=cnt_f[:, bass.ds(7 * i + j + 1, 1)])
                    dve.drain()
            dve.drain().then_inc(asked, 1)
            dve.wait_ge(answered, nth("answers"))
            dve.tensor_copy(start_f, PB[2][:, 0:50])
            dve.tensor_scalar(re_f, PB[2][:, 0:50], float(P - 1), None, ALU.add)
            dve.drain()
            dve.tensor_copy(ti[:, :], start_f)
            dve.drain()
            dve.tensor_scalar(ti[:, :], ti[:, :], 7, None, ALU.logical_shift_right)
            dve.drain()
            dve.tensor_copy(rs_f, ti[:, :])
            dve.drain()
            dve.tensor_copy(ti[:, :], re_f)
            dve.drain()
            dve.tensor_scalar(ti[:, :], ti[:, :], 7, None, ALU.logical_shift_right)
            dve.drain()
            dve.tensor_copy(re_f, ti[:, :])
            dve.drain()
            dve.tensor_tensor(nt_f[:, 0:EB], re_f[:, 1:NB], rs_f[:, 0:EB], ALU.subtract)
            dve.tensor_tensor(doff_f[:, 0:EB], rs_f[:, 1:NB], rs_f[:, 0:EB], ALU.subtract)
            dve.drain()
            dve.tensor_tensor(doff_f[:, 0:EB], doff_f[:, 0:EB], nt_f[:, 0:EB], ALU.subtract)
            dve.tensor_tensor_scan(cum_f[:, 0:EB], ONES[:, 0:EB], nt_f[:, 0:EB], 0.0, ALU.mult, ALU.add)
            dve.drain()
            tile = con(f"tile{tq}")
            for q in range(tq):
                dve.scalar_tensor_tensor(out=junk_f[:, 0:EB], in0=cum_f[:, 0:EB], scalar=tile[:, q:q + 1], in1=doff_f[:, 0:EB],
                                         op0=ALU.is_le, op1=ALU.mult, accum_out=off_f[:, q:q + 1])
                dve.drain()
                dve.scalar_tensor_tensor(out=junk_f[:, 0:EB], in0=cum_f[:, 0:EB], scalar=tile[:, q:q + 1], in1=ONES[:, 0:EB],
                                         op0=ALU.is_le, op1=ALU.mult, accum_out=bt_f[:, q:q + 1])
                dve.drain()
            dve.tensor_tensor(off_f[:, 0:tq], off_f[:, 0:tq], tile, ALU.add)
            dve.drain()
            dve.tensor_scalar(rowi[g][:, 0:tq], off_f[:, 0:tq], float(G["rows"] - 1), None, ALU.min)
            dve.tensor_scalar(bt128[g][:, 0:tq], bt_f[:, 0:tq], float(P), None, ALU.mult)
            dve.tensor_copy(bt8[:, 0:tq], bt_f[:, 0:tq])
            dve.drain().then_inc(rows_ready, 1)
            dve.wait_ge(keys_kept, 32 * (g + 1))

        def count_tensor(pe, g):
            pe.wait_ge(asked, nth("questions"))
            pe.matmul(PB[2][:, 0:50], ONES, cnt_f, start=True, stop=True).then_inc(answered, 1)

        def count_sync(sp, g):
            C, tq = GRAPHS[g]["c"], GRAPHS[g]["tq"]
            keys = (KA, KB)[turned[g][-1]]
            sp.wait_ge(sp_go, nth("goes"))
            sp.dma_start(keysD[g].rearrange("(p a) b -> p (a b)", p=P), keys[:, 0:C].bitcast(I32)).then_inc(keys_kept, 16)
            sp.wait_ge(rows_ready, g + 1)
            sp.dma_start(btD[g], bt8[:, 0:tq]).then_inc(keys_kept, 16)

        def rows_pool(pool, g):
            tq = GRAPHS[g]["tq"]
            pool.wait_ge(rows_ready, g + 1)
            pool.wait_ge(keys_kept, 32 * (g + 1))
            if g:
                pool.wait_ge(raw_free, g)
            for q in range(tq):
                pool.indirect_dma_start(RAW[:, q * P:(q + 1) * P], None, keysD[g],
                                        bass.IndirectOffsetOnAxis(rowi[g][:, q:q + 1], 0)).then_inc(raw_sem[g], 16)

        def tiles_vector(dve, g):
            tq = GRAPHS[g]["tq"]
            L = tq * P
            dve.wait_ge(raw_sem[g], 16 * tq)
            dve.tensor_scalar(TMPI[:, 0:L], RAW[:, 0:L], IDMASK, None, ALU.bitwise_and)
            dve.drain()
            dve.tensor_scalar(SRCF[:, 0:L], TMPI[:, 0:L], float(N - 1), None, ALU.min)
            dve.drain()
            dve.tensor_scalar(TMPI[:, 0:L], RAW[:, 0:L], IDBITS, IDMASK, ALU.logical_shift_right, ALU.bitwise_and)
            dve.drain()
            dve.tensor_copy(DSTF[:, 0:L], TMPI[:, 0:L])
            dve.drain().then_inc(raw_free, 1)
            for q in range(tq):
                dve.tensor_scalar(RELF[:, q * P:(q + 1) * P], DSTF[:, q * P:(q + 1) * P], bt128[g][:, q:q + 1], None, ALU.subtract)
            dve.drain()
            dve.tensor_scalar(RELF[:, 0:L], RELF[:, 0:L], -1.0, float(P), ALU.max, ALU.min)
            dve.drain()
            dve.tensor_copy(RELB[:, 0:L], RELF[:, 0:L])
            for n0 in range(0, tq, 4):
                n = min(4, tq - n0)
                dve.drain().then_inc(asked, 1)
                dve.wait_ge(answered, nth("answers"))
                for bank, to in ((PB[2], TREL), (PB[3], TSRC)):
                    v = to[:, 0:L].rearrange("e (p q) -> e q p", q=tq)
                    dve.tensor_copy(v[:, n0:n0 + n, :], bank[:, 0:n * P].rearrange("e (q p) -> e q p", p=P))
            dve.drain().then_inc(sp_go, 1)
            dve.wait_ge(keep_done, 64 * (g + 1))

        def tiles_tensor(pe, g):
            tq = GRAPHS[g]["tq"]
            for n0 in range(0, tq, 4):
                pe.wait_ge(asked, nth("questions"))
                for q in range(n0, min(n0 + 4, tq)):
                    pe.transpose(PB[2][:, (q - n0) * P:(q - n0 + 1) * P], RELF[:, q * P:(q + 1) * P], IDENT)
                    t = pe.transpose(PB[3][:, (q - n0) * P:(q - n0 + 1) * P], SRCF[:, q * P:(q + 1) * P], IDENT)
                t.then_inc(answered, 1)

        def tiles_sync(sp, g):
            tq = GRAPHS[g]["tq"]
            L = tq * P
            sp.wait_ge(sp_go, nth("goes"))
            sp.dma_start(relD[g].rearrange("o (p a) -> (o p) a", p=P), RELB[:, 0:L]).then_inc(keep_done, 16)
            sp.dma_start(dstD[g], DSTF[:, 0:L]).then_inc(keep_done, 16)
            sp.dma_start(releD[g], TREL[:, 0:L]).then_inc(keep_done, 16)
            sp.dma_start(srceD[g], TSRC[:, 0:L]).then_inc(keep_done, 16)
            sp.wait_ge(keep_done, 64 * (g + 1))

        def graph_loads(g):
            L = GRAPHS[g]["tq"] * P
            return [(RELE[:, 0:L], releD[g]), (srce_i[:, 0:L], srceD[g]),
                    (BT[:, 0:L], btD[g].rearrange("p (o q) -> o (p q)", o=1))]

        MV = sb("MV", [P, NB, 2])
        RS = sb("RS", [P, NB])
        root = sem("root")
        STATS = sb("STATS", [P, 2, 6])
        MVJ = sb("MVJ", [P, 2, 2])
        roots = dict(asked=0, taken=0)
        root_go = sem("root_go")

        def stats_vector(dve, V):
            with dve.Fori(0, NB // 2) as i:
                for j in range(2):
                    dve.bn_stats(STATS[:, j, :], V[:, bass.ds(2 * i + j, 1), :].rearrange("p a d -> p (a d)"))
                dve.drain()
                for j in range(2):
                    dve.bn_aggr(MVJ[:, j, :], STATS[:, j, :])
                dve.drain()
                dve.tensor_copy(MV[:, bass.ds(2 * i, 2), :], MVJ[:, :, :])
            dve.drain()
            dve.tensor_scalar(RS[:, :], MV[:, :, 1], 1e-5, None, ALU.add)
            dve.drain().then_inc(root_go, 1)
            roots["asked"] += 1
            dve.wait_ge(root, roots["asked"])
            dve.reciprocal(RS[:, :], RS[:, :])
            dve.drain()

        def stats_scalar(act, v):
            roots["taken"] += 1
            act.wait_ge(root_go, roots["taken"])
            act.activation(v, v, ACT.Sqrt).then_inc(root, 1)

        def normalise(dve, to, V, b):
            dve.tensor_scalar(to, V[:, bass.ds(b, 1), :].rearrange("p a d -> p (a d)"),
                              MV[:, bass.ds(b, 1), 0:1].rearrange("p a d -> p (a d)"), RS[:, bass.ds(b, 1)],
                              ALU.subtract, ALU.mult)

        IN = ar(GR0, 1024).rearrange("p (j c) -> p j c", j=2)
        XT = ar(GR0 + 1024, 1024).rearrange("p (j c) -> p j c", j=2)

        class Dense:

            def __init__(self, name, chunks, weight, n):
                self.chunks, self.weight, self.n = chunks, weight, n
                self.rows_in, self.turned, self.cols_in, self.multiplied, self.taken = (
                    sem(f"{name}_{x}") for x in ("rows_in", "turned", "cols_in", "multiplied", "taken"))

            def vector(self, dve, produce, take):
                with dve.Fori(0, NB // 2) as i:
                    for j in range(2):
                        produce(dve, IN[:, j, :], 2 * i + j)
                        dve.drain().then_inc(self.rows_in, 1)
                    for j in range(2):
                        dve.wait_ge(self.multiplied, 2 * i + j + 1)
                        dve.wait_ge(self.multiplied, 1)
                        take(dve, PB[2 + j], 2 * i + j)
                        dve.drain().then_inc(self.taken, 1)

            def scalar(self, act):
                with act.Fori(0, NB // 2) as i:
                    for j in range(2):
                        act.wait_ge(self.turned, 2 * i + j + 1)
                        act.wait_ge(self.turned, 1)
                        act.copy(XT[:, j, 0:P * self.chunks], PB[j][:, 0:P * self.chunks]).then_inc(self.cols_in, 1)

            def tensor(self, pe):
                with pe.Fori(0, NB // 2) as i:
                    for j in range(2):
                        pe.wait_ge(self.rows_in, 2 * i + j + 1)
                        pe.wait_ge(self.rows_in, 1)
                        for k in range(self.chunks):
                            t = pe.transpose(PB[j][:, k * P:(k + 1) * P], IN[:, j, k * P:(k + 1) * P], IDENT)
                        t.then_inc(self.turned, 1)
                    for j in range(2):
                        pe.wait_ge(self.cols_in, 2 * i + j + 1)
                        pe.wait_ge(self.cols_in, 1)
                        for k in range(self.chunks):
                            m = pe.matmul(PB[2 + j][:, 0:self.n], XT[:, j, k * P:(k + 1) * P], self.weight(k),
                                          start=(k == 0), stop=(k == self.chunks - 1))
                        m.then_inc(self.multiplied, 1)

        class Gather:

            def __init__(self, name, g, table, width, pitch):
                self.steps = GRAPHS[g]["t"] // (2 * GRP)
                self.table, self.width = table, width
                self.ring = ar(GR0, 2 * GRP * pitch).rearrange("p (h t w) -> p h t w", h=2, t=GRP)
                self.landed = [sem(f"{name}_landed{h}") for h in (0, 1)]

            def fetch(self, pool, i, h):
                pool.tensor_copy(IDX[:, h, :], srce_i[:, bass.ds((2 * i + h) * GRP, GRP)])
                pool.drain()
                for j in range(GRP):
                    pool.indirect_dma_start(self.ring[:, h, j, 0:self.width], None, self.table,
                                            bass.IndirectOffsetOnAxis(IDX[:, h, j:j + 1], 0)).then_inc(self.landed[h], 16)

        def keep_pool(pool, ga, to):
            n = ga.steps

            def body(i, h, first):
                if not first:
                    pool.wait_ge(ga.landed[h], 16 * GRP * i)
                    pool.wait_ge(ga.landed[h], 16 * GRP)
                    pool.tensor_copy(to(2 * i + h - 2), ga.ring[:, h, :, 0:ga.width])
                    pool.drain()
                ga.fetch(pool, i, h)
            pairs_of(pool, n, body)
            for h in (0, 1):
                pool.wait_ge(ga.landed[h], 16 * GRP * n)
                pool.tensor_copy(to(2 * n + h - 2), ga.ring[:, h, :, 0:ga.width])
            pool.drain()

        class Sums:

            def __init__(self, name, g, gather, width, weights=None, rows=None, acc=(ACC0, ACCW)):
                self.acc0, self.accw = acc
                self.steps = GRAPHS[g]["t"] // (2 * GRP)
                self.gather, self.width, self.weights, self.rows = gather, width, weights, rows
                self.prepared, self.multiplied, self.added = (
                    sem(f"{name}_{x}") for x in ("prepared", "multiplied", "added"))

            def pool(self, pool):
                def body(i, h, first):
                    if not first:
                        pool.wait_ge(self.multiplied, GRP * (2 * i + h - 1))
                        pool.wait_ge(self.multiplied, 1)
                    self.gather.fetch(pool, i, h)
                pairs_of(pool, self.steps, body)

            def prepare(self, dve, g, h, i):
                dve.tensor_tensor(Sv[:, h, :, :], IOTA.rearrange("p (a b) -> p a b", a=1).to_broadcast([P, GRP, P]),
                                  RELE[:, bass.ds(g * GRP, GRP)].rearrange("p (a b) -> p a b", b=1).to_broadcast([P, GRP, P]),
                                  ALU.is_equal)
                if self.weights is not None:
                    ring = self.gather.ring
                    dve.wait_ge(self.gather.landed[h], 16 * GRP * (i + 1))
                    dve.wait_ge(self.gather.landed[h], 16 * GRP)
                    self.weights(dve, ring[:, h, :, :], g)
                dve.drain().then_inc(self.prepared, 1)

            def add(self, dve, g):
                blocks = [dve.value_load(BT[0:1, bass.ds(g * GRP + j, 1)], min_val=0, max_val=NB - 1) for j in range(GRP)]
                for j in range(GRP):
                    dve.drain()
                    dve.wait_ge(self.multiplied, GRP * g + j + 1)
                    dve.wait_ge(self.multiplied, 1)
                    acc = self.acc(blocks[j])
                    dve.tensor_tensor(acc, acc, PB[j][:, 0:self.width], ALU.add).then_inc(self.added, 1)

            def acc(self, b):
                return ar(self.acc0, NB * self.accw)[:, bass.ds(b * self.accw, self.width)]

            def vector(self, dve):
                n = self.steps
                self.prepare(dve, 0, 0, 0)
                with dve.Fori(0, n - 1) as i:
                    self.prepare(dve, 2 * i + 1, 1, i)
                    self.add(dve, 2 * i)
                    self.prepare(dve, 2 * i + 2, 0, i + 1)
                    self.add(dve, 2 * i + 1)
                self.prepare(dve, 2 * n - 1, 1, n - 1)
                self.add(dve, 2 * n - 2)
                self.add(dve, 2 * n - 1)
                dve.drain()

            def tensor(self, pe):
                def group(g, h, first, i):
                    pe.wait_ge(self.prepared, g + 1)
                    pe.wait_ge(self.prepared, 1)
                    if self.gather is not None:
                        pe.wait_ge(self.gather.landed[h], 16 * GRP * (i + 1))
                        pe.wait_ge(self.gather.landed[h], 16 * GRP)
                    for j in range(GRP):
                        if not first:
                            pe.wait_ge(self.added, GRP * (g - 1) + j + 1)
                            pe.wait_ge(self.added, 1)
                        rows = self.rows(g, h, j)
                        pe.matmul(PB[j][:, 0:self.width], Sv[:, h, j, :], rows, start=True, stop=True).then_inc(self.multiplied, 1)
                n = self.steps
                group(0, 0, True, 0)
                with pe.Fori(0, n - 1) as i:
                    group(2 * i + 1, 1, False, i)
                    group(2 * i + 2, 0, False, i + 1)
                group(2 * n - 1, 1, False, n - 1)


        class Spread:

            def __init__(self, name, g):
                self.g, self.steps = g, GRAPHS[g]["t"] // (2 * GRP)
                self.rel_in = [sem(f"{name}_rel_in{h}") for h in (0, 1)]
                self.marked, self.multiplied, self.kept = (sem(f"{name}_{x}") for x in ("marked", "multiplied", "kept"))
                self.REL = ar(GR0 + 1024, 1024).bitcast(BF16).rearrange("p (h c) -> p h c", h=2)

            def sync(self, sp):
                def body(i, h, first):
                    if not first:
                        sp.wait_ge(self.marked, 2 * i + h - 1)
                        sp.wait_ge(self.marked, 1)
                    src = relD[self.g][0:1, bass.ds((2 * i + h) * GRP * P, GRP * P)].to_broadcast([P, GRP * P])
                    sp.dma_start(self.REL[:, h, :], src).then_inc(self.rel_in[h], 16)
                pairs_of(sp, self.steps, body)

            def vector(self, dve):
                def body(i, h, first):
                    dve.wait_ge(self.rel_in[h], 16 * (i + 1))
                    dve.wait_ge(self.rel_in[h], 16)
                    if not first:
                        dve.wait_ge(self.multiplied, 2 * i + h - 1)
                        dve.wait_ge(self.multiplied, 1)
                    dve.tensor_scalar(Sv[:, h, :, :].rearrange("p t n -> p (t n)"), self.REL[:, h, :], PCOL, None,
                                      ALU.is_equal).then_inc(self.marked, 1)
                pairs_of(dve, self.steps, body)

            def tensor(self, pe):
                def body(i, h, first):
                    g = 2 * i + h
                    blocks = [pe.value_load(BT[0:1, bass.ds(g * GRP + j, 1)], min_val=0, max_val=NB - 1) for j in range(GRP)]
                    pe.wait_ge(self.marked, g + 1)
                    pe.wait_ge(self.marked, 1)
                    if not first:
                        pe.wait_ge(self.kept, g - 1)
                        pe.wait_ge(self.kept, 1)
                    flat = EDN[:, :, :].rearrange("p b h -> p (b h)")
                    for j in range(GRP):
                        m = pe.matmul(PB[h][:, 4 * j:4 * j + 4], Sv[:, h, j, :], flat[:, bass.ds(blocks[j] * 4, 4)],
                                      start=True, stop=True)
                    m.then_inc(self.multiplied, 1)
                pairs_of(pe, self.steps, body)

            def scalar(self, act, ed):
                def body(i, h, first):
                    act.wait_ge(self.multiplied, 2 * i + h + 1)
                    act.wait_ge(self.multiplied, 1)
                    act.copy(ed[:, bass.ds((2 * i + h) * 4 * GRP, 4 * GRP)], PB[h][:, 0:4 * GRP]).then_inc(self.kept, 1)
                pairs_of(act, self.steps, body)

        edge_tmp = ARENA[0:4, S0 + 800:S0 + 800 + P]
        edge4 = sb("edge4", [P, 16])
        row4 = ARENA[0:4, S0:S0 + 6 * P]
        exp_go, exp_done = sem("exp_go"), sem("exp_done")

        class Weights:

            def __init__(self, g, es, ed, te, dst, pen):
                G = GRAPHS[g]
                self.g, self.tq, self.t = g, G["tq"], G["t"]
                self.L = self.tq * P
                self.es, self.ed, self.dst, self.pen = es, ed, dst, pen
                self.te = te.rearrange("p (h l) -> p h l", h=4)

            def part(self, v, h, q):
                return v.rearrange("e (p q) h -> e q p h", q=self.tq)[:, q, :, h]

            def groups(self):
                return [(h, n0, min(4, self.tq - n0)) for h in range(4) for n0 in range(0, self.tq, 4)]

            def carry(self, dve, back):
                end = 0 if back else self.L - 1
                dve.tensor_copy(edge4[:, 0:4], self.te[:, :, end])
                dve.drain().then_inc(asked, 1)
                dve.wait_ge(answered, nth("answers"))
                first, last, val = row4[:, 0:P], row4[:, P:2 * P], row4[:, 2 * P:3 * P]
                d0, d1, c = row4[:, 3 * P:4 * P], row4[:, 4 * P:5 * P], row4[:, 5 * P:6 * P]
                dve.tensor_copy(row4[:, 0:3 * P], PB[2][0:4, 0:3 * P])
                dve.memset(d0, -BIG)
                dve.memset(d1, -BIG)
                dve.drain()
                n = P - 1
                x, y = (slice(0, n), slice(1, P)) if back else (slice(1, P), slice(0, n))
                near, far = (last, first) if back else (first, last)
                dve.tensor_tensor(c[:, x], near[:, x], far[:, y], ALU.not_equal)
                dve.drain()
                dve.tensor_scalar(c[:, x], c[:, x], -BIG, None, ALU.mult)
                dve.tensor_tensor(d0[:, y], first[:, y], last[:, y], ALU.not_equal)
                dve.drain()
                dve.scalar_tensor_tensor(out=edge_tmp[:, x], in0=d0[:, y], scalar=-BIG, in1=c[:, x], op0=ALU.mult, op1=ALU.add)
                dve.tensor_tensor(d1[:, x], val[:, y], c[:, x], ALU.add)
                dve.drain()
                dve.memset(d0, -BIG)
                dve.drain()
                dve.tensor_copy(d0[:, x], edge_tmp[:, x])
                dve.drain()
                turn = slice(None, None, -1) if back else slice(None)
                dve.tensor_tensor_scan(c[:, turn], d0[:, turn], d1[:, turn], -BIG, ALU.add, ALU.max)
                dve.drain().then_inc(asked, 1)
                dve.wait_ge(answered, nth("answers"))
                dve.tensor_copy(edge4[:, 12:16], PB[3][:, 0:4])
                dve.drain()

            def scan(self, dve, back, first):
                L = self.L
                for h in range(4):
                    v = self.te[:, h, ::-1] if back else self.te[:, h, :]
                    pen = self.pen[:, L:0:-1] if back else self.pen[:, 0:L]
                    dve.tensor_tensor_scan(v, pen, v, -BIG if first else edge4[:, 12 + h:13 + h], ALU.add, ALU.max)
                dve.drain()

            def vector(self, dve):
                tq, L, T = self.tq, self.L, self.t
                for h, n0, n in self.groups():
                    dve.drain().then_inc(asked, 1)
                    dve.wait_ge(answered, nth("answers"))
                    dve.tensor_copy(self.te[:, h, n0 * P:(n0 + n) * P], PB[2][:, 0:n * P])
                dve.memset(self.pen[:, 0:L + 1], 0.0)
                dve.drain()
                dve.tensor_tensor(self.pen[:, 1:L], self.dst[:, 1:L], self.dst[:, 0:L - 1], ALU.not_equal)
                for h in range(4):
                    dve.tensor_copy(edge4[:, 4 + h:5 + h], self.dst[:, 0:1])
                    dve.tensor_copy(edge4[:, 8 + h:9 + h], self.dst[:, L - 1:L])
                dve.drain()
                dve.tensor_scalar(self.pen[:, 1:L], self.pen[:, 1:L], -BIG, None, ALU.mult)
                dve.drain()
                for back in (False, True):
                    self.scan(dve, back, True)
                    self.carry(dve, back)
                    self.scan(dve, back, False)
                es, ed = self.es, self.ed
                dve.tensor_tensor(es, es, ed, ALU.add)
                dve.drain()
                dve.scalar_tensor_tensor(out=es, in0=es, scalar=0.2, in1=es, op0=ALU.mult, op1=ALU.max)
                for h, n0, n in self.groups():
                    dve.drain().then_inc(asked, 1)
                    dve.wait_ge(answered, nth("answers"))
                    for q in range(n0, n0 + n):
                        v = self.part(ed, h, q)
                        dve.tensor_tensor(v, PB[2][:, (q - n0) * P:(q - n0 + 1) * P], v, ALU.add)
                dve.drain()
                dve.scalar_tensor_tensor(out=ed, in0=ed, scalar=0.2, in1=ed, op0=ALU.mult, op1=ALU.max)
                dve.drain()
                dve.tensor_tensor(es, es, ed, ALU.subtract)
                dve.drain().then_inc(exp_go, 1)
                dve.wait_ge(exp_done, nth("exponentials"))

            def carry_tensor(self, pe):
                pe.wait_ge(asked, nth("questions"))
                for k, a in enumerate((4, 8, 0)):
                    t = pe.transpose(PB[2][0:4, k * P:(k + 1) * P], edge4[:, a:a + 4], IDENT)
                t.then_inc(answered, 1)
                pe.wait_ge(asked, nth("questions"))
                pe.transpose(PB[3][:, 0:4], row4[:, 5 * P:6 * P], IDENT[0:4, 0:4]).then_inc(answered, 1)

            def tensor(self, pe):
                for h, n0, n in self.groups():
                    pe.wait_ge(asked, nth("questions"))
                    for q in range(n0, n0 + n):
                        t = pe.transpose(PB[2][:, (q - n0) * P:(q - n0 + 1) * P], self.part(self.es, h, q), IDENT)
                    t.then_inc(answered, 1)
                self.carry_tensor(pe)
                self.carry_tensor(pe)
                for h, n0, n in self.groups():
                    pe.wait_ge(asked, nth("questions"))
                    for q in range(n0, n0 + n):
                        t = pe.transpose(PB[2][:, (q - n0) * P:(q - n0 + 1) * P], self.te[:, h, q * P:(q + 1) * P], IDENT)
                    t.then_inc(answered, 1)

        W0 = ACC0
        w1 = lambda e: ar(W0 + 2048 * e, 1024).rearrange("p (k f) -> p k f", k=2)
        w2 = lambda e: ar(W0 + 2048 * e + 1024, 1024).rearrange("p (f d) -> p f d", f=4)
        b1 = lambda e: ar(W0 + 8192 + 4 * e, 4)
        b2 = lambda e: ar(W0 + 8256 + D * e, D)
        GAMMA, BETA = ar(W0 + 9280, D), ar(W0 + 9536, D)
        FXT = ar(GR0, 512).rearrange("p (k n) -> p k n", k=2)
        FHT = ar(GR0 + 512, 2048).rearrange("p (a f n) -> p a f n", a=2, f=4)

        class Experts:

            def __init__(self, name, n, gate, dest):
                self.n, self.gate, self.dest = n, gate, dest
                self.rows_in, self.turned, self.cols_in, self.hidden, self.curved, self.mixed, self.added, self.done = (
                    sem(f"{name}_{x}") for x in ("rows_in", "turned", "cols_in", "hidden", "curved", "mixed", "added", "done"))

            def each(self, eng, body):
                body(0, True, False)
                with eng.Fori(1, NB // 2 - 1) as i:
                    body(i, False, False)
                body(NB // 2 - 1, False, True)

            def turn(self, pe, i):
                pe.wait_ge(self.rows_in, i + 1)
                pe.wait_ge(self.rows_in, 1)
                for j in range(2):
                    for k in range(2):
                        t = pe.transpose(PB[0][:, k * 256 + j * P:k * 256 + (j + 1) * P], XIN[:, j, k * P:(k + 1) * P], IDENT)
                t.then_inc(self.turned, 1)

            def tensor(self, pe):
                n = self.n

                def up(e):
                    for f in range(4):
                        for k in range(2):
                            m = pe.matmul(PB[1 + 2 * (e % 2) + f // 2][:, (f % 2) * 256:(f % 2 + 1) * 256],
                                          w1(e)[:, k, f * P:(f + 1) * P], FXT[:, k, :], start=(k == 0), stop=(k == 1))
                        if f % 2:
                            m.then_inc(self.hidden, 1)

                def body(i, first, last):
                    pe.wait_ge(self.cols_in, i + 1)
                    pe.wait_ge(self.cols_in, 1)
                    up(0)
                    for e in range(n):
                        if e + 1 < n:
                            up(e + 1)
                        elif not last:
                            self.turn(pe, i + 1)
                        pe.wait_ge(self.curved, i * n + e + 1)
                        pe.wait_ge(self.curved, 1)
                        if not (first and e < 2):
                            pe.wait_ge(self.added, i * n + e - 1)
                            pe.wait_ge(self.added, 1)
                        for j in range(2):
                            for f in range(4):
                                m = pe.matmul(PB[5 + e % 2][:, j * D:(j + 1) * D], FHT[:, e % 2, f, j * P:(j + 1) * P],
                                              w2(e)[:, f, :], start=(f == 0), stop=(f == 3))
                        m.then_inc(self.mixed, 1)
                self.turn(pe, 0)
                self.each(pe, body)

            def scalar(self, act):
                n = self.n

                def columns(i):
                    act.wait_ge(self.turned, i + 1)
                    act.wait_ge(self.turned, 1)
                    act.copy(FXT[:, :, :].rearrange("p k n -> p (k n)"), PB[0][:, :]).then_inc(self.cols_in, 1)

                def body(i, first, last):
                    for e in range(n):
                        if not (first and e < 2):
                            act.wait_ge(self.mixed, i * n + e - 1)
                            act.wait_ge(self.mixed, 1)
                        for f in range(4):
                            if f % 2 == 0:
                                act.wait_ge(self.hidden, (i * n + e) * 2 + f // 2 + 1)
                                act.wait_ge(self.hidden, 1)
                            a = act.activation(FHT[:, e % 2, f, :], PB[1 + 2 * (e % 2) + f // 2][:, (f % 2) * 256:(f % 2 + 1) * 256],
                                               ACT.Gelu, bias=b1(e)[:, f:f + 1])
                        a.then_inc(self.curved, 1)
                    if not last:
                        columns(i + 1)
                columns(0)
                self.each(act, body)

            def vector(self, dve):
                n = self.n

                def rows(i):
                    dve.tensor_copy(XIN[:, :, :], Hv[:, bass.ds(2 * i, 2), :])
                    dve.drain().then_inc(self.rows_in, 1)

                def body(i, first, last):
                    for e in range(n):
                        if e == n - 1 and not last:
                            dve.wait_ge(self.turned, i + 1)
                            dve.wait_ge(self.turned, 1)
                            rows(i + 1)
                        dve.wait_ge(self.mixed, i * n + e + 1)
                        dve.wait_ge(self.mixed, 1)
                        for j in range(2):
                            to, g = self.dest(2 * i + j), self.gate(2 * i + j, e)
                            dve.scalar_tensor_tensor(out=to, in0=PB[5 + e % 2][:, j * D:(j + 1) * D], scalar=g, in1=to,
                                                     op0=ALU.mult, op1=ALU.add)
                        dve.drain().then_inc(self.added, 1)
                        for j in range(2):
                            to, g = self.dest(2 * i + j), self.gate(2 * i + j, e)
                            dve.scalar_tensor_tensor(out=to, in0=b2(e), scalar=g, in1=to, op0=ALU.mult, op1=ALU.add)
                        dve.drain()
                    dve.drain().then_inc(self.done, 1)
                rows(0)
                self.each(dve, body)

        XIN = ar(GR0 + 2560, 512).rearrange("p (j d) -> p j d", j=2)

        def serve_exp(act, v):
            act.wait_ge(exp_go, nth("exponentials asked"))
            act.activation(v, v, ACT.Exp).then_inc(exp_done, 1)

        def softmax8(dve, v, tmp):
            dve.drain()
            dve.tensor_reduce(tmp, v, AX.X, ALU.max)
            dve.drain()
            dve.tensor_scalar(v, v, tmp, None, ALU.subtract)
            dve.drain().then_inc(exp_go, 1)
            dve.wait_ge(exp_done, nth("exponentials"))
            dve.tensor_reduce(tmp, v, AX.X, ALU.add)
            dve.drain()
            dve.reciprocal(tmp, tmp)
            dve.drain()
            dve.tensor_scalar(v, v, tmp, None, ALU.mult)
            dve.drain()

        def top2(dve, s, B, E, a, b, m, gates, first_id=None, second_id=None):
            rep = lambda v: v.rearrange("p (b e) -> p b e", e=1).to_broadcast([P, B, E])
            ids = IOTA[:, 0:E].rearrange("p (b e) -> p b e", b=1).to_broadcast([P, B, E])
            m1, m2, i1, d = (m[:, k, :] for k in range(4))

            def winner(v, best, hot, ident):
                dve.tensor_reduce(best, v, AX.X, ALU.max)
                dve.drain()
                dve.tensor_tensor(hot, v, rep(best), ALU.not_equal)
                dve.drain()
                dve.scalar_tensor_tensor(out=hot, in0=hot, scalar=float(E), in1=ids, op0=ALU.mult, op1=ALU.add)
                dve.drain()
                dve.tensor_reduce(ident, hot, AX.X, ALU.min)
                dve.drain()
                dve.tensor_tensor(hot, ids, rep(ident), ALU.is_equal)
                dve.drain()

            winner(s, m1, a, i1)
            if first_id is not None:
                dve.tensor_copy(first_id, i1)
            dve.scalar_tensor_tensor(out=s, in0=a, scalar=-BIG, in1=s, op0=ALU.mult, op1=ALU.add)
            dve.drain()
            winner(s, m2, b, i1)
            if second_id is not None:
                dve.tensor_copy(second_id, i1)
            dve.tensor_tensor(d, m2, m1, ALU.subtract)
            dve.drain().then_inc(exp_go, 1)
            dve.wait_ge(exp_done, nth("exponentials"))
            dve.tensor_scalar(m1, d, 1.0, None, ALU.add)
            dve.drain()
            dve.reciprocal(m1, m1)
            dve.drain()
            dve.tensor_tensor(m2, d, m1, ALU.mult)
            dve.drain()
            dve.tensor_tensor(a, a, rep(m1), ALU.mult)
            dve.tensor_tensor(b, b, rep(m2), ALU.mult)
            dve.drain()
            dve.tensor_tensor(gates, a, b, ALU.add)
            dve.drain()

        def extend(dve, w, n, att, heads, tmp, to):
            dve.tensor_tensor(tmp, w, att, ALU.mult)
            dve.drain()
            dve.tensor_reduce(to, tmp.rearrange("p (h d) -> p h d", h=heads), AX.X, ALU.add)
            dve.drain()

        def block(V, b):
            return V[:, bass.ds(b, 1), :].rearrange("p a d -> p (a d)")

        DSTS = {0: ar(ACC0 + 9000, 896), 2: ar(23040, 1152)}
        SMALL2 = ar(28300, 48).rearrange("p (a n) -> p a n", n=16)
        IDSI = sb("IDSI", [P, 2], I32)

        loads, load_sem, load_total = {}, {}, {}

        def define_load(name, pairs):
            loads[name], load_sem[name], load_total[name] = pairs, sem(f"load_{name}"), 16 * len(pairs)

        def load(sp, name):
            for dst, src in loads[name]:
                sp.dma_start(dst, src, allow_slow_non_contiguous=True).then_inc(load_sem[name], 16)

        row = lambda a: a.rearrange("(o n) -> o n", o=1).to_broadcast([P, a.shape[0]])
        rows_by_chunk = lambda a: a.rearrange("(k p) n -> p k n", p=P)
        WX = ar(WS0, 2 * (D + 8)).rearrange("p (k n) -> p k n", k=2)
        ATT = ar(WS0 + 600, 512).rearrange("p (a n) -> p a n", a=2)
        last = N - (EB - 1) * P
        define_load("start", [(CON[:, :], consts), (FLIPS, flips), (WX[:, :, 0:D], rows_by_chunk(A["L0_gnn_W"])),
                              (ATT[:, 0, :], row(A["L0_gnn_a_src"].rearrange("h d -> (h d)"))),
                              (ATT[:, 1, :], row(A["L0_gnn_a_dst"].rearrange("h d -> (h d)")))])
        define_load("x", [(X[:, 8 * c:8 * c + 8, :], A["x"][8 * c * P:8 * (c + 1) * P, :].rearrange("(b p) d -> p b d", p=P))
                          for c in range(6)])
        define_load("x_end", [(X[0:last, EB - 1, :], A["x"][(EB - 1) * P:N, :])])
        for g in range(3):
            define_load(f"graph{g}", graph_loads(g))
        BIASR = sb("BIASR", [P, D])
        sage_w = lambda m: ar(WS0 + 512 * m, 512).rearrange("p (k n) -> p k n", k=2)
        mats = [A["L1_gnn_W_in"]] + [A[f"L1_gnn_W_{x}"][l] for l in range(3) for x in ("agg", "self")] + [A["L1_gnn_W_out"]]
        define_load("sage", [(sage_w(m), rows_by_chunk(a)) for m, a in enumerate(mats)])
        biases = [A["L1_gnn_b_in"]] + [A["L1_gnn_b_hid"][l] for l in range(3)] + [A["L1_gnn_b_out"]]
        for m, a in enumerate(biases):
            define_load(f"bias{m}", [(BIASR[:, :], row(a))])
        WRT, BRT = ar(W0 + 10800, 16).rearrange("p (k n) -> p k n", k=2), ar(W0 + 10816, 8)
        define_load("router", [(WRT, rows_by_chunk(A["L0_ffn_Wr"])), (BRT, row(A["L0_ffn_br"])),
                               (GAMMA, row(A["L0_ffn_gamma"])), (BETA, row(A["L0_ffn_beta"]))])
        WG = ar(WS0, 48).rearrange("p (k n) -> p k n", k=2)
        SMALL = ar(WS0 + 64, 96).rearrange("p (a n) -> p a n", n=16)
        define_load("gat1", [(WG[:, :, 0:16], rows_by_chunk(A["L1_ffn_W_gat"])),
                             (SMALL[:, 0, :], row(A["L1_ffn_att_src"].rearrange("h d -> (h d)"))),
                             (SMALL[:, 1, :], row(A["L1_ffn_att_dst"].rearrange("h d -> (h d)"))),
                             (SMALL[:, 2, :], row(A["L1_ffn_b_gat"])), (SMALL[:, 3, :], row(A["L1_ffn_ln_gamma"])),
                             (SMALL[:, 4, :], row(A["L1_ffn_ln_beta"]))])
        define_load("experts1", [p for e in range(4) for p in (
            (w1(e), rows_by_chunk(A["L1_ffn_W1"][e])), (w2(e), rows_by_chunk(A["L1_ffn_W2"][e])),
            (b1(e), A["L1_ffn_b1"][e].rearrange("(f p) -> p f", p=P)), (b2(e), row(A["L1_ffn_b2"][e])))])
        define_load("small2", [(SMALL2[:, k, :], row(A[f"L1_ffn_{x}"])) for k, x in enumerate(("b_gat", "ln_gamma", "ln_beta"))])
        for g in (0, 2):
            define_load(f"dst{g}", [(DSTS[g], dstD[g])])

        zeroed = sem("zeroed")
        es_kept = sem("es_kept")
        chosen = sem("chosen")
        chosen_in = sem("chosen_in")
        stored = sem("stored")
        weights_free = sem("weights_free")
        summed = sem("summed")
        finished = sem("finished")

        def chunk_stores(sp, table, V, width, taken, s, base):
            for c in range(5):
                sp.wait_ge(taken, 10 * (c + 1))
                dst = table[10 * c * P:10 * (c + 1) * P, :].rearrange("(b p) d -> p b d", p=P)
                sp.dma_start(dst, V[:, 10 * c:10 * (c + 1), 0:width]).then_inc(s, 16)
            sp.wait_ge(s, base + 80)

        first = Dense("project", 2, lambda k: WX[:, k, :], D + 8)
        es_gather = Gather("es", 0, esD, 4, 4)
        spread0 = Spread("spread0", 0)
        ES0, ED0, TE0 = (ar(H0 + k * 3584, 3584) for k in range(3))
        weights0 = Weights(0, ES0.rearrange("p (t h) -> p t h", h=4), ED0.rearrange("p (t h) -> p t h", h=4),
                           TE0, DSTS[0], ar(ACC0 + 10000, 900))
        hp_gather = Gather("hp", 0, tabD, D, ACCW)

        def weigh(dve, ring, g):
            w = ES0[:, bass.ds(g * GRP * 4, GRP * 4)].rearrange("p (t h) -> p t h", h=4)
            v = ring[:, :, 0:D].rearrange("p t (h d) -> p t h d", h=4)
            dve.tensor_tensor(v, v, w.rearrange("p t (h o) -> p t h o", o=1).to_broadcast([P, GRP, 4, 64]), ALU.mult)
            dve.tensor_copy(ring[:, :, D:D + 4], w)

        sums0 = Sums("sums0", 0, hp_gather, ACCW, weigh, lambda g, h, j: hp_gather.ring[:, h, j, 0:ACCW])
        W12 = ar(W0 + 10830, 2)
        experts0 = Experts("experts0", 2, lambda b, e: W12[:, e:e + 1], lambda b: block(Hv, b))
        enter = Dense("enter", 2, lambda k: sage_w(0)[:, k, :], D)
        hop_gather = [Gather(f"hop{l}", 1, tabD, D, ACCW) for l in range(3)]
        hops = [Sums(f"hops{l}", 1, hop_gather[l], D + 1, None, (lambda ga: lambda g, h, j: ga.ring[:, h, j, 0:D + 1])(hop_gather[l]))
                for l in range(3)]
        mixes = [Dense(f"mix{l}", 4, (lambda l: lambda k: sage_w(1 + 2 * l + k // 2)[:, k % 2, :])(l), D) for l in range(3)]
        leave = Dense("leave", 2, lambda k: sage_w(7)[:, k, :], D)
        T20 = ar(ACC0, NB * 24).rearrange("p (b n) -> p b n", n=24)
        project2 = Dense("project2", 2, lambda k: WG[:, k, :], 24)
        G1 = ar(ACC0, 1152 * 20).rearrange("p (t n) -> p t n", n=20)
        ED2, TE2 = ar(24192, 4608), ar(28800, 4608)
        g1_gather = Gather("g1", 2, t20D, 20, 20)
        spread2 = Spread("spread2", 2)
        weights2 = Weights(2, G1[:, :, 16:20], ED2.rearrange("p (t h) -> p t h", h=4), TE2, DSTS[2], SRCE[:, :])
        ACC2 = ar(24192, NB * 20)
        sums2 = Sums("sums2", 2, None, 20, None,
                     lambda g, h, j: ar(ACC0, 1152 * 20)[:, bass.ds((g * GRP + j) * 20, 20)], acc=(24192, 20))
        experts1 = Experts("experts1", 4, lambda b, e: EDN[:, bass.ds(b, 1), e:e + 1].rearrange("p a e -> p (a e)"),
                           lambda b: block(X, b))

        LOGITS, DIFF0, DIFF1 = ar(W0 + 10840, 8), ar(W0 + 10883, 1), ar(28100 + 3 * NB, NB)

        block_ctx = ctx.enter_context(nc.Block())

        def normalise_all(dve):
            with dve.Fori(0, NB // 2) as i:
                for j in range(2):
                    normalise(dve, block(Hv, 2 * i + j), X, 2 * i + j)
            dve.drain()

        def over_blocks(v):
            return v.rearrange("p (b d) -> p b d", b=1).to_broadcast([P, NB, v.shape[1]])

        @block_ctx.vector
        def _(dve):
            dve.memset(X[:, EB - 1:NB, :], 0.0)
            dve.drain().then_inc(zeroed, 1)
            dve.wait_ge(load_sem["start"], load_total["start"])
            for k in range(2):
                for a in range(2):
                    extend(dve, WX[:, k, 0:D], D, ATT[:, a, :], 4, ar(ACC0, D), WX[:, k, D + 4 * a:D + 4 * a + 4])
            dve.wait_ge(load_sem["x"], load_total["x"])
            dve.wait_ge(load_sem["x_end"], load_total["x_end"])
            stats_vector(dve, X)

            def keep(dve, bank, b):
                dve.tensor_copy(block(Hv, b), bank[:, 0:D])
                dve.tensor_copy(block(ESN, b), bank[:, D:D + 4])
                dve.tensor_copy(block(EDN, b), bank[:, D + 4:D + 8])
            first.vector(dve, lambda dve, to, b: normalise(dve, to[:, 0:D], X, b), keep)
            cur = sort_vector(dve, 0)
            count_vector(dve, 0, cur)
            tiles_vector(dve, 0)
            dve.drain().then_inc(met, 1)
            dve.wait_ge(met, MEETING * 1)

            t = GRAPHS[0]["t"] * 4
            dve.memset(ES0[:, t:3584], 0.0)
            dve.memset(ED0[:, t:3584], 0.0)
            spread0.vector(dve)
            for g in (1, 2):
                cur = sort_vector(dve, g)
                count_vector(dve, g, cur)
            for g in (1, 2):
                tiles_vector(dve, g)
            dve.wait_ge(es_kept, 1)
            dve.wait_ge(spread0.kept, GRAPHS[0]["t"] // GRP)
            dve.wait_ge(load_sem["dst0"], load_total["dst0"])
            weights0.vector(dve)
            dve.memset(ar(ACC0, NB * ACCW), 0.0)
            dve.drain().then_inc(met, 1)
            dve.wait_ge(met, MEETING * 2)

            sums0.vector(dve)
            dve.tensor_scalar(ESN[:, :, :], ACCv[:, :, D:D + 4], 1e-16, None, ALU.add)
            dve.drain()
            dve.reciprocal(ESN[:, :, :], ESN[:, :, :])
            dve.drain()
            v = ACCv[:, :, 0:D].rearrange("p b (h d) -> p b h d", h=4)
            dve.tensor_tensor(v, v, ESN[:, :, :].rearrange("p b (h o) -> p b h o", o=1).to_broadcast([P, NB, 4, 64]), ALU.mult)
            dve.drain()
            dve.tensor_tensor(X[:, :, :], X[:, :, :], ACCv[:, :, 0:D], ALU.add)
            dve.drain()
            dve.drain().then_inc(met, 1)
            dve.wait_ge(met, MEETING * 3)

            stats_vector(dve, X)
            normalise_all(dve)
            dve.wait_ge(load_sem["router"], load_total["router"])
            sumx = ar(W0 + 10000, D)
            mb = ar(W0 + 10300, 2 * P).rearrange("p (k n) -> p k n", k=2)
            lg = LOGITS
            t1, a8, b8 = ar(W0 + 10850, 1), ar(W0 + 10860, 8), ar(W0 + 10870, 8)
            m4, g8, ids = ar(W0 + 10880, 4), ar(W0 + 10890, 8), ar(W0 + 10900, 2)
            c8, d8 = ar(W0 + 10910, 8), ar(W0 + 10920, 8)
            dve.tensor_reduce(sumx, Hv.rearrange("p b d -> p d b"), AX.X, ALU.add)
            dve.drain().then_inc(asked, 1)
            dve.wait_ge(answered, nth("answers"))
            for k in range(2):
                dve.tensor_scalar(mb[:, k, :], ONES, PB[2][:, k:k + 1], 1.0 / N, ALU.mult, ALU.mult)
            dve.drain().then_inc(asked, 1)
            dve.wait_ge(answered, nth("answers"))
            dve.tensor_tensor(lg, PB[3][:, 0:8], BRT, ALU.add)
            softmax8(dve, lg, t1)
            capacity = float(-(-N * 5 // (4 * 8)))
            dve.tensor_scalar(c8, lg, float(N), None, ALU.mult)
            dve.drain()
            dve.tensor_scalar(d8, c8, capacity, None, ALU.max)
            dve.drain()
            dve.reciprocal(d8, d8)
            dve.drain()
            dve.tensor_scalar(d8, d8, capacity, -1.0, ALU.mult, ALU.add)
            dve.tensor_scalar(c8, c8, capacity, None, ALU.is_gt)
            dve.drain()
            dve.tensor_tensor(c8, c8, d8, ALU.mult)
            dve.drain()
            dve.tensor_scalar(c8, c8, 1.0, None, ALU.add)
            dve.drain()
            dve.tensor_tensor(lg, lg, c8, ALU.mult)
            softmax8(dve, lg, t1)
            one = lambda v: v.rearrange("p (b e) -> p b e", b=1)
            top2(dve, one(lg), 1, 8, one(a8), one(b8), m4.rearrange("p (k b) -> p k b", b=1), one(g8),
                 ids[:, 0:1], ids[:, 1:2])
            dve.tensor_copy(W12, m4[:, 0:2])
            dve.tensor_copy(IDSI[:, :], ids)
            dve.drain().then_inc(chosen, 1)
            dve.wait_ge(chosen_in, 16 * 8)
            experts0.vector(dve)
            stats_vector(dve, Hv)
            with dve.Fori(0, NB // 2) as i:
                for j in range(2):
                    normalise(dve, block(Hv, 2 * i + j), Hv, 2 * i + j)
            dve.drain()
            dve.tensor_tensor(Hv, Hv, over_blocks(GAMMA), ALU.mult)
            dve.tensor_tensor(X[:, :, :], X[:, :, :], over_blocks(BETA), ALU.add)
            dve.drain()
            dve.tensor_tensor(X[:, :, :], X[:, :, :], Hv, ALU.add)
            dve.drain()
            stats_vector(dve, X)
            dve.wait_ge(load_sem["sage"], load_total["sage"])
            dve.wait_ge(load_sem["bias0"], load_total["bias0"])

            def enter_take(dve, bank, b):
                dve.tensor_tensor(block(Hv, b), bank[:, 0:D], BIASR[:, :], ALU.add)
            enter.vector(dve, lambda dve, to, b: normalise(dve, to[:, 0:D], X, b), enter_take)

            def room_for_sums(dve, ga):
                dve.memset(ga.ring[:, :, :, D:D + 1], 1.0)
                dve.memset(ar(ACC0, NB * ACCW), 0.0)
            room_for_sums(dve, hop_gather[0])
            dve.drain().then_inc(met, 1)
            dve.wait_ge(met, MEETING * 4)

            for l in range(3):
                hops[l].vector(dve)
                dve.tensor_scalar(RS[:, :], ACCv[:, :, D], 1.0, None, ALU.max)
                dve.drain()
                dve.reciprocal(RS[:, :], RS[:, :])
                dve.drain()
                dve.wait_ge(load_sem[f"bias{l + 1}"], load_total[f"bias{l + 1}"])

                def mix_in(dve, to, b):
                    dve.tensor_scalar(to[:, 0:D], ar(ACC0, NB * ACCW)[:, bass.ds(b * ACCW, D)], RS[:, bass.ds(b, 1)], None, ALU.mult)
                    dve.tensor_copy(to[:, D:2 * D], block(Hv, b))

                def mix_take(dve, bank, b):
                    dve.tensor_tensor(block(Hv, b), bank[:, 0:D], BIASR[:, :], ALU.add)
                    dve.drain()
                    dve.tensor_scalar(block(Hv, b), block(Hv, b), 0.0, None, ALU.max)
                mixes[l].vector(dve, mix_in, mix_take)
                if l < 2:
                    room_for_sums(dve, hop_gather[l + 1])
                    dve.drain().then_inc(met, 1)
                    dve.wait_ge(met, MEETING * (5 + l))
            dve.drain().then_inc(sp_go, 1)
            dve.wait_ge(load_sem["bias4"], load_total["bias4"])

            def leave_take(dve, bank, b):
                dve.tensor_tensor(block(X, b), block(X, b), bank[:, 0:D], ALU.add)
                dve.drain()
                dve.tensor_tensor(block(X, b), block(X, b), BIASR[:, :], ALU.add)
            leave.vector(dve, lambda dve, to, b: dve.tensor_copy(to[:, 0:D], block(Hv, b)), leave_take)
            stats_vector(dve, X)
            dve.drain().then_inc(sp_go, 1)
            dve.wait_ge(load_sem["gat1"], load_total["gat1"])
            for k in range(2):
                for a in range(2):
                    extend(dve, WG[:, k, 0:16], 16, SMALL[:, a, :], 4, SM[:, 0:16], WG[:, k, 16 + 4 * a:20 + 4 * a])
            project2.vector(dve, lambda dve, to, b: normalise(dve, to[:, 0:D], X, b),
                            lambda dve, bank, b: dve.tensor_copy(block(T20, b), bank[:, 0:24]))
            dve.tensor_copy(EDN[:, :, :], T20[:, :, 20:24])
            dve.drain().then_inc(met, 1)
            dve.wait_ge(met, MEETING * 7)

            t = GRAPHS[2]["t"]
            dve.memset(ED2[:, 4 * t:4608], 0.0)
            dve.memset(G1[:, t:1152, :], 0.0)
            spread2.vector(dve)
            dve.wait_ge(es_kept, 2)
            dve.wait_ge(spread2.kept, t // GRP)
            dve.wait_ge(load_sem["dst2"], load_total["dst2"])
            weights2.vector(dve)
            v = G1[:, :, 0:16].rearrange("p t (h e) -> p t h e", h=4)
            dve.tensor_tensor(v, v, G1[:, :, 16:20].rearrange("p t (h o) -> p t h o", o=1).to_broadcast([P, 1152, 4, 4]), ALU.mult)
            dve.memset(ACC2, 0.0)
            dve.drain()
            sums2.vector(dve)
            dve.drain().then_inc(met, 1)
            dve.wait_ge(met, MEETING * 8)

            A16 = ar(25800, NB * 16).rearrange("p (b n) -> p b n", n=16)
            B16 = ar(26600, NB * 16).rearrange("p (b n) -> p b n", n=16)
            mean, rs16 = ar(27400, NB), ar(27450, NB)
            s4, a4, c4, m4 = (ar(27500 + 200 * k, NB * 4) for k in range(4))
            acc2 = ACC2.rearrange("p (b n) -> p b n", n=20)
            v4 = lambda v: v.rearrange("p (b e) -> p b e", e=4)
            rep16 = lambda v: v.rearrange("p (b o) -> p b o", o=1).to_broadcast([P, NB, 16])
            dve.wait_ge(load_sem["small2"], load_total["small2"])
            dve.tensor_scalar(v4(a4), acc2[:, :, 16:20], 1e-16, None, ALU.add)
            dve.drain()
            dve.reciprocal(a4, a4)
            dve.drain()
            for h in range(4):
                dve.tensor_tensor(A16[:, :, 4 * h:4 * h + 4], acc2[:, :, 4 * h:4 * h + 4],
                                  v4(a4)[:, :, h:h + 1].to_broadcast([P, NB, 4]), ALU.mult)
            dve.drain()
            dve.tensor_tensor(A16, A16, over_blocks(SMALL2[:, 0, :]), ALU.add)
            dve.drain()
            dve.tensor_reduce(mean, A16, AX.X, ALU.add)
            dve.drain()
            dve.tensor_scalar(mean, mean, 1.0 / 16, None, ALU.mult)
            dve.drain()
            dve.tensor_tensor(A16, A16, rep16(mean), ALU.subtract)
            dve.drain()
            dve.tensor_tensor(B16, A16, A16, ALU.mult)
            dve.drain()
            dve.tensor_reduce(rs16, B16, AX.X, ALU.add)
            dve.drain()
            dve.tensor_scalar(rs16, rs16, 1.0 / 16, 1e-5, ALU.mult, ALU.add)
            dve.drain().then_inc(root_go, 1)
            roots["asked"] += 1
            dve.wait_ge(root, roots["asked"])
            dve.reciprocal(rs16, rs16)
            dve.drain()
            dve.tensor_tensor(A16, A16, rep16(rs16), ALU.mult)
            dve.drain()
            dve.tensor_tensor(A16, A16, over_blocks(SMALL2[:, 1, :]), ALU.mult)
            dve.drain()
            dve.tensor_tensor(A16, A16, over_blocks(SMALL2[:, 2, :]), ALU.add)
            dve.drain()
            dve.tensor_reduce(v4(s4), A16.rearrange("p b (h e) -> p b e h", h=4), AX.X, ALU.add)
            dve.drain()
            dve.tensor_scalar(s4, s4, 0.25, None, ALU.mult)
            dve.drain()
            top2(dve, v4(s4), NB, 4, v4(a4), v4(c4), m4.rearrange("p (k b) -> p k b", k=4), EDN[:, :, :])
            normalise_all(dve)
            dve.wait_ge(load_sem["experts1"], load_total["experts1"])
            experts1.vector(dve)

        @block_ctx.scalar
        def _(act):
            stats_scalar(act, RS[:, :])
            first.scalar(act)
            act.drain().then_inc(met, 1)
            act.wait_ge(met, MEETING * 1)
            spread0.scalar(act, ED0)
            serve_exp(act, weights0.es)
            act.drain().then_inc(met, 1)
            act.wait_ge(met, MEETING * 2)
            act.drain().then_inc(met, 1)
            act.wait_ge(met, MEETING * 3)
            stats_scalar(act, RS[:, :])
            serve_exp(act, LOGITS)
            serve_exp(act, LOGITS)
            serve_exp(act, DIFF0)
            experts0.scalar(act)
            stats_scalar(act, RS[:, :])
            stats_scalar(act, RS[:, :])
            enter.scalar(act)
            act.drain().then_inc(met, 1)
            act.wait_ge(met, MEETING * 4)
            for l in range(3):
                mixes[l].scalar(act)
                if l < 2:
                    act.drain().then_inc(met, 1)
                    act.wait_ge(met, MEETING * (5 + l))
            leave.scalar(act)
            stats_scalar(act, RS[:, :])
            project2.scalar(act)
            act.drain().then_inc(met, 1)
            act.wait_ge(met, MEETING * 7)
            spread2.scalar(act, ED2)
            serve_exp(act, weights2.es)
            act.drain().then_inc(met, 1)
            act.wait_ge(met, MEETING * 8)
            stats_scalar(act, ar(27450, NB))
            serve_exp(act, DIFF1)
            experts1.scalar(act)

        @block_ctx.tensor
        def _(pe):
            first.tensor(pe)
            sort_tensor(pe, 0)
            count_tensor(pe, 0)
            tiles_tensor(pe, 0)
            pe.drain().then_inc(met, 1)
            pe.wait_ge(met, MEETING * 1)
            spread0.tensor(pe)
            for g in (1, 2):
                sort_tensor(pe, g)
                count_tensor(pe, g)
            for g in (1, 2):
                tiles_tensor(pe, g)
            weights0.tensor(pe)
            pe.drain().then_inc(met, 1)
            pe.wait_ge(met, MEETING * 2)
            sums0.tensor(pe)
            pe.drain().then_inc(met, 1)
            pe.wait_ge(met, MEETING * 3)
            pe.wait_ge(asked, nth("questions"))
            for k in range(2):
                m = pe.matmul(PB[2][:, k:k + 1], ar(W0 + 10000, D)[:, k * P:(k + 1) * P], ONES[:, 0:1], start=True, stop=True)
            m.then_inc(answered, 1)
            pe.wait_ge(asked, nth("questions"))
            for k in range(2):
                m = pe.matmul(PB[3][:, 0:8], ar(W0 + 10300, 2 * P)[:, k * P:(k + 1) * P], WRT[:, k, :], start=(k == 0), stop=(k == 1))
            m.then_inc(answered, 1)
            experts0.tensor(pe)
            enter.tensor(pe)
            pe.drain().then_inc(met, 1)
            pe.wait_ge(met, MEETING * 4)
            for l in range(3):
                hops[l].tensor(pe)
                mixes[l].tensor(pe)
                if l < 2:
                    pe.drain().then_inc(met, 1)
                    pe.wait_ge(met, MEETING * (5 + l))
            leave.tensor(pe)
            project2.tensor(pe)
            pe.drain().then_inc(met, 1)
            pe.wait_ge(met, MEETING * 7)
            spread2.tensor(pe)
            weights2.tensor(pe)
            sums2.tensor(pe)
            pe.drain().then_inc(met, 1)
            pe.wait_ge(met, MEETING * 8)
            experts1.tensor(pe)

        @block_ctx.gpsimd
        def _(pool):
            pool.iota(LOOPS[:, :], [[1, 50]], base=0, channel_multiplier=50)
            pool.drain().then_inc(loops_ready, 1)
            rows_pool(pool, 0)
            pool.drain().then_inc(met, 1)
            pool.wait_ge(met, MEETING * 1)
            keep_pool(pool, es_gather, lambda g: ES0[:, bass.ds(g * 4 * GRP, 4 * GRP)].rearrange("p (t w) -> p t w", w=4))
            pool.drain().then_inc(es_kept, 1)
            rows_pool(pool, 1)
            rows_pool(pool, 2)
            pool.drain().then_inc(met, 1)
            pool.wait_ge(met, MEETING * 2)
            sums0.pool(pool)
            pool.drain().then_inc(met, 1)
            pool.wait_ge(met, MEETING * 3)
            pool.drain().then_inc(met, 1)
            pool.wait_ge(met, MEETING * 4)
            for l in range(3):
                hops[l].pool(pool)
                if l < 2:
                    pool.drain().then_inc(met, 1)
                    pool.wait_ge(met, MEETING * (5 + l))
            pool.drain().then_inc(met, 1)
            pool.wait_ge(met, MEETING * 7)
            keep_pool(pool, g1_gather, lambda g: ar(ACC0, 1152 * 20)[:, bass.ds(g * 20 * GRP, 20 * GRP)].rearrange("p (t w) -> p t w", w=20))
            pool.drain().then_inc(es_kept, 1)
            pool.drain().then_inc(met, 1)
            pool.wait_ge(met, MEETING * 8)

        @block_ctx.sync
        def _(sp):
            load(sp, "start")
            load(sp, "x")
            sp.wait_ge(zeroed, 1)
            load(sp, "x_end")
            chunk_stores(sp, tabD, Hv, D, first.taken, stored, 0)
            sp.dma_start(esD.rearrange("(b p) h -> p b h", p=P), ESN[:, :, :]).then_inc(stored, 16)
            sp.wait_ge(stored, 96)
            sort_sync(sp, 0)
            count_sync(sp, 0)
            tiles_sync(sp, 0)
            load(sp, "graph0")
            load(sp, "dst0")
            sp.wait_ge(load_sem["graph0"], load_total["graph0"])
            sp.wait_ge(load_sem["dst0"], load_total["dst0"])
            sp.drain().then_inc(met, 1)
            sp.wait_ge(met, MEETING * 1)
            spread0.sync(sp)
            for g in (1, 2):
                sort_sync(sp, g)
                count_sync(sp, g)
            for g in (1, 2):
                tiles_sync(sp, g)
            sp.drain().then_inc(met, 1)
            sp.wait_ge(met, MEETING * 2)
            sp.drain().then_inc(met, 1)
            sp.wait_ge(met, MEETING * 3)
            load(sp, "router")
            load(sp, "sage")
            load(sp, "graph1")
            load(sp, "bias0")
            sp.wait_ge(chosen, 1)
            for e in range(2):
                v = sp.value_load(IDSI[0:1, e:e + 1], min_val=0, max_val=7)
                one = lambda a: a[bass.ds(v, 1)]
                sp.dma_start(w1(e), one(A["L0_ffn_W1"]).rearrange("o (k p) n -> p (o k) n", p=P)).then_inc(chosen_in, 16)
                sp.dma_start(w2(e), one(A["L0_ffn_W2"]).rearrange("o (k p) n -> p (o k) n", p=P)).then_inc(chosen_in, 16)
                sp.dma_start(b1(e), one(A["L0_ffn_b1"]).rearrange("o (f p) -> p (o f)", p=P), allow_slow_non_contiguous=True).then_inc(chosen_in, 16)
                sp.dma_start(b2(e), one(A["L0_ffn_b2"]).to_broadcast([P, D])).then_inc(chosen_in, 16)
            sp.wait_ge(load_sem["graph1"], load_total["graph1"])
            chunk_stores(sp, tabD, Hv, D, enter.taken, stored, 96)
            load(sp, "bias1")
            sp.wait_ge(load_sem["bias1"], load_total["bias1"])
            sp.drain().then_inc(met, 1)
            sp.wait_ge(met, MEETING * 4)
            for l in range(2):
                chunk_stores(sp, tabD, Hv, D, mixes[l].taken, stored, 176 + 80 * l)
                load(sp, f"bias{l + 2}")
                sp.wait_ge(load_sem[f"bias{l + 2}"], load_total[f"bias{l + 2}"])
                sp.drain().then_inc(met, 1)
                sp.wait_ge(met, MEETING * (5 + l))
            sp.wait_ge(sp_go, nth("goes"))
            load(sp, "bias4")
            load(sp, "graph2")
            sp.wait_ge(sp_go, nth("goes"))
            load(sp, "gat1")
            chunk_stores(sp, t20D, T20, 20, project2.taken, stored, 336)
            sp.wait_ge(load_sem["graph2"], load_total["graph2"])
            sp.drain().then_inc(met, 1)
            sp.wait_ge(met, MEETING * 7)
            load(sp, "dst2")
            spread2.sync(sp)
            sp.drain().then_inc(met, 1)
            sp.wait_ge(met, MEETING * 8)
            load(sp, "small2")
            load(sp, "experts1")
            for c in range(7):
                last_pair = -(-7 * (c + 1) // 2)
                sp.wait_ge(experts1.done, min(last_pair, NB // 2))
                if c < 6:
                    dst = out[7 * c * P:7 * (c + 1) * P, :].rearrange("(b p) d -> p b d", p=P)
                    sp.dma_start(dst, X[:, 7 * c:7 * c + 7, :]).then_inc(finished, 16)
            dst = out[42 * P:48 * P, :].rearrange("(b p) d -> p b d", p=P)
            sp.dma_start(dst, X[:, 42:48, :]).then_inc(finished, 16)
            sp.dma_start(out[48 * P:N, :], X[0:last, 48, :]).then_inc(finished, 16)
            sp.wait_ge(finished, 16 * 8)


_INS = ["x", "src", "dst", "L0_gnn_W", "L0_gnn_a_src", "L0_gnn_a_dst", "L0_ffn_Wr", "L0_ffn_br", "L0_ffn_W1",
        "L0_ffn_b1", "L0_ffn_W2", "L0_ffn_b2", "L0_ffn_gamma", "L0_ffn_beta", "L1_gnn_W_in", "L1_gnn_b_in",
        "L1_gnn_W_agg", "L1_gnn_W_self", "L1_gnn_b_hid", "L1_gnn_W_out", "L1_gnn_b_out", "L1_ffn_W_gat",
        "L1_ffn_att_src", "L1_ffn_att_dst", "L1_ffn_b_gat", "L1_ffn_ln_gamma", "L1_ffn_ln_beta", "L1_ffn_W1",
        "L1_ffn_b1", "L1_ffn_W2", "L1_ffn_b2", "L1_ffn_edge_index"]


def kernel(**inputs):
    import concourse.bacc as _bacc
    from concourse.bass_utils import run_bass_kernel_spmd as _run

    nc = _bacc.Bacc("TRN2", target_bir_lowering=False, num_devices=1)
    arrays, aps = {}, {}
    consts, where, flips = host_constants()
    for name in _INS + ["consts", "flips"]:
        a = {"consts": consts, "flips": flips}.get(name)
        a = np.ascontiguousarray(inputs[name] if a is None else a)
        arrays[f"in_{name}"] = a
        aps[name] = nc.dram_tensor(f"in_{name}", a.shape, mybir.dt.from_np(a.dtype), kind="ExternalInput").ap()
    out = nc.dram_tensor("out_x", (N, D), F32, kind="ExternalOutput").ap()
    build_program(nc, aps, out, aps["consts"], aps["flips"], where)
    r = _run(nc, [arrays], core_ids=[0])
    return r.results[0]["out_x"]
```

```python
from contextlib import ExitStack

import numpy as np

import concourse.bass as bass
from concourse import mybir

ALU = mybir.AluOpType
ACT = mybir.ActivationFunctionType
AX = mybir.AxisListType
F32 = mybir.dt.float32
BF16 = mybir.dt.bfloat16
I32 = mybir.dt.int32
U8 = mybir.dt.uint8

P = 128
N = 6250
D = 256
EB = -(-N // P)
NB = EB + 1
NP = NB * P
ACCW = D + 4
FFN_F = 512
IDBITS = 13
IDMASK = (1 << IDBITS) - 1
KEYTOP = 0x40000000
BIG = 1.0e30
GRP = 8
QRT = 4
RING = 4 * QRT

GRAPHS = [dict(c=1024, tq=7, t=880), dict(c=1024, tq=7, t=880), dict(c=2048, tq=9, t=1136)]
for _g in GRAPHS:
    _g["rows"] = _g["c"]
    assert _g["tq"] * P >= _g["t"] and _g["t"] % (2 * GRP) == 0


def host_constants():
    p = np.arange(P)
    sign = lambda r: 1.0 - 2.0 * ((p >> r) & 1)
    flips = np.concatenate([sign(r - 1) * sign(r) for r in range(1, 8)])
    limits = (KEYTOP | (((np.arange(EB) + 1) * P) << IDBITS)).astype(np.int32).view(np.float32)
    every = lambda row: np.broadcast_to(row, (P, len(row)))
    parts = [("ident", np.eye(P)), ("ones", np.ones((P, P))), ("iota", every(p)), ("pcol", p[:, None]),
             ("sign0", sign(0)[:, None]), ("limits", every(limits))]
    for tq in (7, 9):
        parts.append((f"tile{tq}", p[:, None] * tq + np.arange(tq)[None, :]))
    at, where = 0, {}
    for name, a in parts:
        where[name] = (at, at + a.shape[1])
        at += a.shape[1]
    return np.concatenate([np.asarray(a, np.float32) for _, a in parts], 1), where, every(flips).astype(np.float32)


def build_program(nc, A, out, consts, flips, where):
    with ExitStack() as ctx:
        def sb(name, shape, dt=F32):
            return ctx.enter_context(nc.sbuf_tensor(name, shape, dt))

        def sem(name):
            return ctx.enter_context(nc.semaphore(name))

        def dram(name, shape, dt=F32):
            return nc.dram_tensor(name, shape, dt, kind="Internal").ap()

        ncon = consts.shape[1]
        CON = sb("CON", [P, ncon])
        con = lambda name: CON[:, where[name][0]:where[name][1]]
        IDENT, ONES, IOTA, PCOL = con("ident"), con("ones"), con("iota"), con("pcol")
        X = sb("X", [P, NB, D])
        xflat = X[:, :, :].rearrange("p b d -> p (b d)")
        ARENA = sb("ARENA", [P, 36104])
        ACC0, H0, WS0, GR0, S0 = 0, 13000, 25800, 29896, 34056
        ar = lambda a, n: ARENA[:, a:a + n]
        ACCv = ar(ACC0, NB * ACCW).rearrange("p (b w) -> p b w", w=ACCW)
        Hv = ar(H0, NB * D).rearrange("p (b d) -> p b d", d=D)
        Sv = ar(S0, 2 * GRP * P).rearrange("p (h t n) -> p h t n", h=2, t=GRP)
        Qv = ar(S0, RING * P).rearrange("p (h t n) -> p h t n", h=4, t=QRT)
        RELE = sb("RELE", [P, 1152])
        SRCE = sb("SRCE", [P, 1160])
        srce_i = SRCE[:, 0:1152].bitcast(I32)
        BT = sb("BT", [1, 1152], U8)
        IDX = sb("IDX", [P, 4, QRT], I32)
        EDN = sb("EDN", [P, NB, 4])
        ESN = sb("ESN", [P, NB, 4])
        SM = ar(ACC0 + 11000, 420)
        FLIPS = ar(GR0 + 2048, 7 * P)
        LOOPS = sb("LOOPS", [125, 50], I32)
        loops_ready = sem("loops_ready")
        PSUM = ctx.enter_context(nc.psum_tensor("PSUM", [P, 8 * 512], F32))
        PB = [PSUM[:, 512 * i:512 * (i + 1)] for i in range(8)]

        tabD = dram("tabD", (NP, D))
        esD = dram("esD", (NP, 4))
        t20D = dram("t20D", (NP, 20))
        keysD = [dram(f"keysD{g}", (G["rows"], P), I32) for g, G in enumerate(GRAPHS)]
        relD = [dram(f"relD{g}", (1, G["tq"] * P * P), BF16) for g, G in enumerate(GRAPHS)]
        releD = [dram(f"releD{g}", (P, G["tq"] * P)) for g, G in enumerate(GRAPHS)]
        srceD = [dram(f"srceD{g}", (P, G["tq"] * P), I32) for g, G in enumerate(GRAPHS)]
        dstD = [dram(f"dstD{g}", (P, G["tq"] * P)) for g, G in enumerate(GRAPHS)]
        btD = [dram(f"btD{g}", (P, G["tq"]), U8) for g, G in enumerate(GRAPHS)]

        met = sem("met")
        asked, answered = sem("asked"), sem("answered")
        loaded = sem("loaded")
        sp_go = sem("sp_go")
        pool_go, pool_done = sem("pool_go"), sem("pool_done")
        MEETING = 5
        counts = {}

        def nth(name):
            counts[name] = counts.get(name, 0) + 1
            return counts[name]

        def pairs_of(eng, n, body):
            for h in (0, 1):
                body(0, h, True)
            with eng.Fori(1, n) as i:
                for h in (0, 1):
                    body(i, h, False)

        sp_key = sem("sp_key")
        key_room = sem("key_room")
        KA, KB = ar(WS0, 2048), ar(WS0 + 2048, 2048)

        def key_buffers(g):
            C = GRAPHS[g]["c"]
            return KA[:, 0:C].bitcast(I32), KB[:, 0:C].bitcast(I32)

        def key_sources(g):
            if g == 0:
                return A["dst"], A["src"]
            if g == 1:
                return A["src"], A["dst"]
            return A["L1_ffn_edge_index"][1, :], A["L1_ffn_edge_index"][0, :]

        def sort_sync(sp, g):
            dsts, srcs = key_sources(g)
            n = dsts.shape[0]
            rows = 125 if g < 2 else P
            sp.wait_ge(key_room, g + 1)
            for buf, a in zip(key_buffers(g), (dsts, srcs)):
                sp.dma_start(buf[0:rows, 0:n // rows], a.rearrange("(p c) -> p c", p=rows)).then_inc(sp_key, 16)

        def sort_vector(dve, g):
            C = GRAPHS[g]["c"]
            dst_i, src_i = key_buffers(g)
            dve.memset(dst_i, IDMASK)
            dve.memset(src_i, IDMASK)
            dve.drain().then_inc(key_room, 1)
            if g == 2:
                dve.wait_ge(loops_ready, 1)
                dve.tensor_copy(dst_i[0:125, 1024:1074], LOOPS[:, :])
                dve.tensor_copy(src_i[0:125, 1024:1074], LOOPS[:, :])
                dve.drain()
            dve.wait_ge(sp_key, 32 * (g + 1))
            dve.scalar_tensor_tensor(out=dst_i, in0=dst_i, scalar=IDBITS, in1=src_i,
                                     op0=ALU.logical_shift_left, op1=ALU.bitwise_or)
            dve.drain()
            dve.tensor_scalar(dst_i, dst_i, KEYTOP, None, ALU.bitwise_or)
            dve.drain()
            bufs = [KA[:, 0:C], KB[:, 0:C]]
            dve.tensor_scalar(bufs[1], bufs[0], con("sign0"), None, ALU.mult)
            dve.drain()
            cur = 1

            def exchange(lo, hi, olo, ohi):
                dve.tensor_tensor(olo, lo, hi, ALU.min)
                dve.tensor_tensor(ohi, lo, hi, ALU.max)
                dve.drain()

            def step(s):
                nonlocal cur
                v = bufs[cur].rearrange("p (n two s) -> p n two s", two=2, s=s)
                w = bufs[1 - cur].rearrange("p (n two s) -> p n two s", two=2, s=s)
                exchange(v[:, :, 0, :], v[:, :, 1, :], w[:, :, 0, :], w[:, :, 1, :])
                cur = 1 - cur

            def mirror(size):
                nonlocal cur
                v = bufs[cur].rearrange("p (n s) -> p n s", s=size)
                w = bufs[1 - cur].rearrange("p (n s) -> p n s", s=size)
                h = size // 2
                exchange(v[:, :, 0:h], v[:, :, size - 1:h - 1:-1] , w[:, :, 0:h], w[:, :, size - 1:h - 1:-1])
                cur = 1 - cur

            size = 2
            while size <= C:
                if size == 2:
                    step(1)
                else:
                    mirror(size)
                    s = size // 4
                    while s >= 1:
                        step(s)
                        s //= 2
                size *= 2
            for r in range(1, 8):
                turned[g].append(cur)
                dve.drain().then_inc(asked, 1)
                dve.wait_ge(answered, nth("answers"))
                flip = FLIPS[:, (r - 1) * P:r * P]
                for k in range(C // 512):
                    dve.tensor_tensor(bufs[1 - cur][:, k * 512:(k + 1) * 512].rearrange("p (a b) -> p a b", b=P),
                                      PB[4 + k][:, :].rearrange("p (a b) -> p a b", b=P),
                                      flip.rearrange("p (a b) -> p a b", a=1).to_broadcast([P, 4, P]), ALU.mult)
                dve.drain()
                cur = 1 - cur
                s = 1 << (r - 1)
                while s >= 1:
                    step(s)
                    s //= 2
                turned[g].append(cur)
                dve.drain().then_inc(asked, 1)
                dve.wait_ge(answered, nth("answers"))
                for k in range(C // 512):
                    dve.tensor_copy(bufs[1 - cur][:, k * 512:(k + 1) * 512], PB[4 + k][:, :])
                dve.drain()
                cur = 1 - cur
                s = C // 2
                while s >= 1:
                    step(s)
                    s //= 2
            turned[g].append(cur)
            return cur

        def sort_tensor(pe, g):
            C = GRAPHS[g]["c"]
            bufs = [KA, KB]
            for cur in turned[g][:-1]:
                pe.wait_ge(asked, nth("questions"))
                for k in range(C // P):
                    t = pe.transpose(PB[4 + k // 4][:, (k % 4) * P:(k % 4 + 1) * P], bufs[cur][:, k * P:(k + 1) * P], IDENT)
                t.then_inc(answered, 1)

        turned = {g: [] for g in range(3)}

        start_f, nt_f, cum_f, doff_f = SM[:, 0:50], SM[:, 50:100], SM[:, 100:150], SM[:, 150:200]
        cnt_f, re_f = SM[:, 200:250], SM[:, 250:300]
        off_f, bt_f, junk_f, rs_f = SM[:, 300:309], SM[:, 310:319], SM[:, 320:370], SM[:, 370:420]
        ti = sb("ti", [P, 50], I32)
        rowi = [sb(f"rowi{g}", [P, 9], I32) for g in range(3)]
        bt128 = [sb(f"bt128_{g}", [P, 9]) for g in range(3)]
        bt8 = sb("bt8", [P, 9], U8)
        TT0 = ACC0
        RAW = ar(TT0, 1152).bitcast(I32)
        TMPI = ar(TT0 + 1152, 1152).bitcast(I32)
        SRCF, DSTF, RELF = ar(TT0 + 2304, 1152), ar(TT0 + 3456, 1152), ar(TT0 + 4608, 1152)
        RELB = ar(TT0 + 5760, 576).bitcast(BF16)
        TREL = ar(TT0 + 6336, 1152)
        TSRC = ar(TT0 + 7488, 1152).bitcast(I32)
        rows_ready = sem("rows_ready")
        keys_kept = sem("keys_kept")
        raw_sem = [sem(f"raw_sem{g}") for g in range(3)]
        raw_free = sem("raw_free")
        keep_done = sem("keep_done")

        def count_vector(dve, g, cur):
            G = GRAPHS[g]
            C, tq = G["c"], G["tq"]
            keys, junk = (KA, KB) if cur == 0 else (KB, KA)
            dve.drain().then_inc(sp_go, 1)
            dve.memset(cnt_f[:, 0:1], 0.0)
            lim = con("limits")
            with dve.Fori(0, 7) as i:
                for j in range(7):
                    dve.tensor_scalar(junk[:, 0:C], keys[:, 0:C], lim[:, bass.ds(7 * i + j, 1)], None,
                                      ALU.is_lt, ALU.add, accum_out=cnt_f[:, bass.ds(7 * i + j + 1, 1)])
                    dve.drain()
            dve.drain().then_inc(asked, 1)
            dve.wait_ge(answered, nth("answers"))
            dve.tensor_copy(start_f, PB[2][:, 0:50])
            dve.tensor_scalar(re_f, PB[2][:, 0:50], float(P - 1), None, ALU.add)
            dve.drain()
            dve.tensor_copy(ti[:, :], start_f)
            dve.drain()
            dve.tensor_scalar(ti[:, :], ti[:, :], 7, None, ALU.logical_shift_right)
            dve.drain()
            dve.tensor_copy(rs_f, ti[:, :])
            dve.drain()
            dve.tensor_copy(ti[:, :], re_f)
            dve.drain()
            dve.tensor_scalar(ti[:, :], ti[:, :], 7, None, ALU.logical_shift_right)
            dve.drain()
            dve.tensor_copy(re_f, ti[:, :])
            dve.drain()
            dve.tensor_tensor(nt_f[:, 0:EB], re_f[:, 1:NB], rs_f[:, 0:EB], ALU.subtract)
            dve.tensor_tensor(doff_f[:, 0:EB], rs_f[:, 1:NB], rs_f[:, 0:EB], ALU.subtract)
            dve.drain()
            dve.tensor_tensor(doff_f[:, 0:EB], doff_f[:, 0:EB], nt_f[:, 0:EB], ALU.subtract)
            dve.tensor_tensor_scan(cum_f[:, 0:EB], ONES[:, 0:EB], nt_f[:, 0:EB], 0.0, ALU.mult, ALU.add)
            dve.drain()
            tile = con(f"tile{tq}")
            for q in range(tq):
                dve.scalar_tensor_tensor(out=junk_f[:, 0:EB], in0=cum_f[:, 0:EB], scalar=tile[:, q:q + 1], in1=doff_f[:, 0:EB],
                                         op0=ALU.is_le, op1=ALU.mult, accum_out=off_f[:, q:q + 1])
                dve.drain()
                dve.scalar_tensor_tensor(out=junk_f[:, 0:EB], in0=cum_f[:, 0:EB], scalar=tile[:, q:q + 1], in1=ONES[:, 0:EB],
                                         op0=ALU.is_le, op1=ALU.mult, accum_out=bt_f[:, q:q + 1])
                dve.drain()
            dve.tensor_tensor(off_f[:, 0:tq], off_f[:, 0:tq], tile, ALU.add)
            dve.drain()
            dve.tensor_scalar(rowi[g][:, 0:tq], off_f[:, 0:tq], float(G["rows"] - 1), None, ALU.min)
            dve.tensor_scalar(bt128[g][:, 0:tq], bt_f[:, 0:tq], float(P), None, ALU.mult)
            dve.tensor_copy(bt8[:, 0:tq], bt_f[:, 0:tq])
            dve.drain().then_inc(rows_ready, 1)
            dve.wait_ge(keys_kept, 32 * (g + 1))

        def count_tensor(pe, g):
            pe.wait_ge(asked, nth("questions"))
            pe.matmul(PB[2][:, 0:50], ONES, cnt_f, start=True, stop=True).then_inc(answered, 1)

        def count_sync(sp, g):
            C, tq = GRAPHS[g]["c"], GRAPHS[g]["tq"]
            keys = (KA, KB)[turned[g][-1]]
            sp.wait_ge(sp_go, nth("goes"))
            sp.dma_start(keysD[g].rearrange("(p a) b -> p (a b)", p=P), keys[:, 0:C].bitcast(I32)).then_inc(keys_kept, 16)
            sp.wait_ge(rows_ready, g + 1)
            sp.dma_start(btD[g], bt8[:, 0:tq]).then_inc(keys_kept, 16)

        def rows_pool(pool, g):
            tq = GRAPHS[g]["tq"]
            pool.wait_ge(rows_ready, g + 1)
            pool.wait_ge(keys_kept, 32 * (g + 1))
            if g:
                pool.wait_ge(raw_free, g)
            for q in range(tq):
                pool.indirect_dma_start(RAW[:, q * P:(q + 1) * P], None, keysD[g],
                                        bass.IndirectOffsetOnAxis(rowi[g][:, q:q + 1], 0)).then_inc(raw_sem[g], 16)

        def tiles_vector(dve, g):
            tq = GRAPHS[g]["tq"]
            L = tq * P
            dve.wait_ge(raw_sem[g], 16 * tq)
            dve.tensor_scalar(TMPI[:, 0:L], RAW[:, 0:L], IDMASK, None, ALU.bitwise_and)
            dve.drain()
            dve.tensor_scalar(SRCF[:, 0:L], TMPI[:, 0:L], float(N - 1), None, ALU.min)
            dve.drain()
            dve.tensor_scalar(TMPI[:, 0:L], RAW[:, 0:L], IDBITS, IDMASK, ALU.logical_shift_right, ALU.bitwise_and)
            dve.drain()
            dve.tensor_copy(DSTF[:, 0:L], TMPI[:, 0:L])
            dve.drain().then_inc(raw_free, 1)
            for q in range(tq):
                dve.tensor_scalar(RELF[:, q * P:(q + 1) * P], DSTF[:, q * P:(q + 1) * P], bt128[g][:, q:q + 1], None, ALU.subtract)
            dve.drain()
            dve.tensor_scalar(RELF[:, 0:L], RELF[:, 0:L], -1.0, float(P), ALU.max, ALU.min)
            dve.drain()
            dve.tensor_copy(RELB[:, 0:L], RELF[:, 0:L])
            for n0 in range(0, tq, 4):
                n = min(4, tq - n0)
                dve.drain().then_inc(asked, 1)
                dve.wait_ge(answered, nth("answers"))
                for bank, to in ((PB[2], TREL), (PB[3], TSRC)):
                    v = to[:, 0:L].rearrange("e (p q) -> e q p", q=tq)
                    dve.tensor_copy(v[:, n0:n0 + n, :], bank[:, 0:n * P].rearrange("e (q p) -> e q p", p=P))
            dve.drain().then_inc(sp_go, 1)
            dve.wait_ge(keep_done, 64 * (g + 1))

        def tiles_tensor(pe, g):
            tq = GRAPHS[g]["tq"]
            for n0 in range(0, tq, 4):
                pe.wait_ge(asked, nth("questions"))
                for q in range(n0, min(n0 + 4, tq)):
                    pe.transpose(PB[2][:, (q - n0) * P:(q - n0 + 1) * P], RELF[:, q * P:(q + 1) * P], IDENT)
                    t = pe.transpose(PB[3][:, (q - n0) * P:(q - n0 + 1) * P], SRCF[:, q * P:(q + 1) * P], IDENT)
                t.then_inc(answered, 1)

        def tiles_sync(sp, g):
            tq = GRAPHS[g]["tq"]
            L = tq * P
            sp.wait_ge(sp_go, nth("goes"))
            sp.dma_start(relD[g].rearrange("o (p a) -> (o p) a", p=P), RELB[:, 0:L]).then_inc(keep_done, 16)
            sp.dma_start(dstD[g], DSTF[:, 0:L]).then_inc(keep_done, 16)
            sp.dma_start(releD[g], TREL[:, 0:L]).then_inc(keep_done, 16)
            sp.dma_start(srceD[g], TSRC[:, 0:L]).then_inc(keep_done, 16)
            sp.wait_ge(keep_done, 64 * (g + 1))

        def graph_loads(g):
            L = GRAPHS[g]["tq"] * P
            return [(RELE[:, 0:L], releD[g]), (srce_i[:, 0:L], srceD[g]),
                    (BT[:, 0:L], btD[g].rearrange("p (o q) -> o (p q)", o=1))]

        MV = sb("MV", [P, NB, 2])
        RS = sb("RS", [P, NB])
        root = sem("root")
        STATS = sb("STATS", [P, 2, 6])
        MVJ = sb("MVJ", [P, 2, 2])
        roots = dict(asked=0, taken=0)
        root_go = sem("root_go")

        def stats_vector(dve, V):
            with dve.Fori(0, NB // 2) as i:
                for j in range(2):
                    dve.bn_stats(STATS[:, j, :], V[:, bass.ds(2 * i + j, 1), :].rearrange("p a d -> p (a d)"))
                dve.drain()
                for j in range(2):
                    dve.bn_aggr(MVJ[:, j, :], STATS[:, j, :])
                dve.drain()
                dve.tensor_copy(MV[:, bass.ds(2 * i, 2), :], MVJ[:, :, :])
            dve.drain()
            dve.tensor_scalar(RS[:, :], MV[:, :, 1], 1e-5, None, ALU.add)
            dve.drain().then_inc(root_go, 1)
            roots["asked"] += 1
            dve.wait_ge(root, roots["asked"])
            dve.reciprocal(RS[:, :], RS[:, :])
            dve.drain()

        def stats_scalar(act, v):
            roots["taken"] += 1
            act.wait_ge(root_go, roots["taken"])
            act.activation(v, v, ACT.Sqrt).then_inc(root, 1)

        def normalise(dve, to, V, b):
            dve.tensor_scalar(to, V[:, bass.ds(b, 1), :].rearrange("p a d -> p (a d)"),
                              MV[:, bass.ds(b, 1), 0:1].rearrange("p a d -> p (a d)"), RS[:, bass.ds(b, 1)],
                              ALU.subtract, ALU.mult)

        IN = ar(GR0, 1024).rearrange("p (j c) -> p j c", j=2)
        XT = ar(GR0 + 1024, 1024).rearrange("p (j c) -> p j c", j=2)

        class Dense:

            def __init__(self, name, chunks, weight, n):
                self.chunks, self.weight, self.n = chunks, weight, n
                self.rows_in, self.turned, self.cols_in, self.multiplied, self.taken = (
                    sem(f"{name}_{x}") for x in ("rows_in", "turned", "cols_in", "multiplied", "taken"))

            def each(self, eng, body):
                for j in range(2):
                    body(j, j, True, False)
                with eng.Fori(1, NB // 2 - 1) as i:
                    for j in range(2):
                        body(2 * i + j, j, False, False)
                for j in range(2):
                    body(NB - 2 + j, j, False, True)

            def vector(self, dve, produce, take):
                def body(b, j, first, last):
                    if not last:
                        dve.wait_ge(self.turned, b + 1)
                        dve.wait_ge(self.turned, 1)
                        produce(dve, IN[:, j, :], b + 2)
                        dve.drain().then_inc(self.rows_in, 1)
                    dve.wait_ge(self.multiplied, b + 1)
                    dve.wait_ge(self.multiplied, 1)
                    take(dve, PB[2 + j], b)
                    dve.drain().then_inc(self.taken, 1)
                for j in range(2):
                    produce(dve, IN[:, j, :], j)
                    dve.drain().then_inc(self.rows_in, 1)
                self.each(dve, body)

            def scalar(self, act):
                def body(b, j, first, last):
                    act.wait_ge(self.turned, b + 1)
                    act.wait_ge(self.turned, 1)
                    if not first:
                        act.wait_ge(self.multiplied, b - 1)
                        act.wait_ge(self.multiplied, 1)
                    act.copy(XT[:, j, 0:P * self.chunks], PB[j][:, 0:P * self.chunks]).then_inc(self.cols_in, 1)
                self.each(act, body)

            def tensor(self, pe):
                def turn(b, j, first):
                    pe.wait_ge(self.rows_in, b + 1)
                    pe.wait_ge(self.rows_in, 1)
                    if not first:
                        pe.wait_ge(self.cols_in, b - 1)
                        pe.wait_ge(self.cols_in, 1)
                    for k in range(self.chunks):
                        t = pe.transpose(PB[j][:, k * P:(k + 1) * P], IN[:, j, k * P:(k + 1) * P], IDENT)
                    t.then_inc(self.turned, 1)

                def body(b, j, first, last):
                    if not (last and j == 1):
                        turn(b + 1, 1 - j, first and j == 0)
                    pe.wait_ge(self.cols_in, b + 1)
                    pe.wait_ge(self.cols_in, 1)
                    if not first:
                        pe.wait_ge(self.taken, b - 1)
                        pe.wait_ge(self.taken, 1)
                    for k in range(self.chunks):
                        m = pe.matmul(PB[2 + j][:, 0:self.n], XT[:, j, k * P:(k + 1) * P], self.weight(k),
                                      start=(k == 0), stop=(k == self.chunks - 1))
                    m.then_inc(self.multiplied, 1)
                turn(0, 0, True)
                self.each(pe, body)

        def quarters_of(eng, n, body):
            for h in range(4):
                body(0, h, True)
            with eng.Fori(1, n) as i:
                for h in range(4):
                    body(i, h, False)

        class Gather:

            def __init__(self, name, g, table, width, pitch):
                self.steps = GRAPHS[g]["t"] // RING
                self.table, self.width = table, width
                self.ring = ar(GR0, RING * pitch).rearrange("p (h t w) -> p h t w", h=4, t=QRT)
                self.landed = [sem(f"{name}_landed{h}") for h in range(4)]
                self.told = sem(f"{name}_told")

            def tell(self, act, i, h, first, used=None):
                if not first:
                    act.wait_ge(self.landed[h], 16 * QRT * i)
                    act.wait_ge(self.landed[h], 16 * QRT)
                    if used:
                        used(i, h)
                act.copy(IDX[:, h, :], srce_i[:, bass.ds((4 * i + h) * QRT, QRT)])
                act.drain().then_inc(self.told, 1)

            def fetch(self, pool, i, h):
                pool.wait_ge(self.told, 4 * i + h + 1)
                if not isinstance(i, int):
                    pool.nop(nofuse=True)
                for j in range(QRT):
                    pool.indirect_dma_start(self.ring[:, h, j, 0:self.width], None, self.table,
                                            bass.IndirectOffsetOnAxis(IDX[:, h, j:j + 1], 0)).then_inc(self.landed[h], 16)

        class Kept(Gather):

            def pool(self, pool):
                quarters_of(pool, self.steps, lambda i, h, first: self.fetch(pool, i, h))

            def scalar(self, act, to):
                def used(i, h):
                    act.copy(to(4 * i + h - 4), self.ring[:, h, :, 0:self.width])
                quarters_of(act, self.steps, lambda i, h, first: self.tell(act, i, h, first, used))
                for h in range(4):
                    act.wait_ge(self.landed[h], 16 * QRT * self.steps)
                    used(self.steps, h)

        BT4 = BT[:, :].bitcast(I32)

        def blocks_of(eng, g, size):
            blocks = []
            for k in range(size // 4):
                word = eng.value_load(BT4[0:1, bass.ds(g * (size // 4) + k, 1)], min_val=0, max_val=(NB - 1) * 0x01010101)
                blocks += [((word >> (8 * j)) & 63).with_bounds(min_val=0, max_val=NB - 1) for j in range(4)]
            return blocks

        class Sums:

            def __init__(self, name, gather, width, weights=None):
                self.gather, self.width, self.weights = gather, width, weights
                self.steps = gather.steps
                self.ready_by_tile = 1 if weights is None else 2
                self.prepared, self.multiplied, self.added, self.columns = (
                    sem(f"{name}_{x}") for x in ("prepared", "multiplied", "added", "columns"))

            def pool(self, pool):
                def body(i, h, first):
                    if not first:
                        pool.wait_ge(self.multiplied, QRT * (4 * i + h - 3))
                        pool.wait_ge(self.multiplied, 1)
                    self.gather.fetch(pool, i, h)
                quarters_of(pool, self.steps, body)

            def scalar(self, act):
                def body(i, h, first):
                    self.gather.tell(act, i, h, first)
                if self.weights is None:
                    quarters_of(act, self.steps, body)
                    return

                def column(i, h):
                    act.wait_ge(self.gather.landed[h], 16 * QRT * (i + 1))
                    act.wait_ge(self.gather.landed[h], 16 * QRT)
                    act.copy(self.gather.ring[:, h, :, D:D + 4], self.weights(4 * i + h)).then_inc(self.columns, 1)
                for h in range(4):
                    body(0, h, True)
                with act.Fori(1, self.steps) as i:
                    for h in range(4):
                        column(i - 1, h)
                        body(i, h, False)
                for h in range(4):
                    column(self.steps - 1, h)

            def prepare(self, dve, i, h, j):
                g = 4 * i + h
                dve.tensor_scalar(Qv[:, h, j, :], IOTA, RELE[:, bass.ds(g * QRT + j, 1)], None, ALU.is_equal).then_inc(self.prepared, 1)
                if self.weights is not None:
                    if j == 0:
                        dve.wait_ge(self.gather.landed[h], 16 * QRT * (i + 1))
                        dve.wait_ge(self.gather.landed[h], 16 * QRT)
                    v = self.gather.ring[:, h, j, 0:D].rearrange("p (h d) -> p h d", h=4)
                    w = self.weights(g)[:, j, :].rearrange("p (h o) -> p h o", o=1).to_broadcast([P, 4, D // 4])
                    dve.tensor_tensor(v, v, w, ALU.mult).then_inc(self.prepared, 1)

            def vector(self, dve):
                def step(i, h, first, last):
                    g = 4 * i + h
                    blocks = blocks_of(dve, g, QRT)
                    ahead = (i, h + 1) if h < 3 else (i + 1, 0)
                    for j in range(QRT):
                        if not (last and h == 3):
                            self.prepare(dve, *ahead, j)
                        dve.wait_ge(self.multiplied, QRT * g + j + 1)
                        dve.wait_ge(self.multiplied, 1)
                        if not (first and h == 0 and j == 0):
                            dve.wait_ge(self.added, QRT * g + j)
                            dve.wait_ge(self.added, 1)
                        acc = ar(ACC0, NB * ACCW)[:, bass.ds(blocks[j] * ACCW, self.width)]
                        dve.tensor_tensor(acc, acc, PB[4 * (h % 2) + j][:, 0:self.width], ALU.add).then_inc(self.added, 1)
                for j in range(QRT):
                    self.prepare(dve, 0, 0, j)
                for h in range(4):
                    step(0, h, True, False)
                with dve.Fori(1, self.steps - 1) as i:
                    for h in range(4):
                        step(i, h, False, False)
                for h in range(4):
                    step(self.steps - 1, h, False, True)
                dve.drain()

            def tensor(self, pe):
                def body(i, h, first):
                    pe.wait_ge(self.gather.landed[h], 16 * QRT * (i + 1))
                    pe.wait_ge(self.gather.landed[h], 16 * QRT)
                    if self.weights is not None:
                        pe.wait_ge(self.columns, 4 * i + h + 1)
                        pe.wait_ge(self.columns, 1)
                    for j in range(QRT):
                        tile = QRT * (4 * i + h) + j
                        pe.wait_ge(self.prepared, self.ready_by_tile * (tile + 1))
                        pe.wait_ge(self.prepared, 1)
                        if not first or h >= 2:
                            pe.wait_ge(self.added, tile - 2 * QRT + 1)
                            pe.wait_ge(self.added, 1)
                        pe.matmul(PB[4 * (h % 2) + j][:, 0:self.width], Qv[:, h, j, :], self.gather.ring[:, h, j, 0:self.width],
                                  start=True, stop=True).then_inc(self.multiplied, 1)
                quarters_of(pe, self.steps, body)

        class NarrowSums:

            def __init__(self, name, g, rows, width, pitch):
                self.steps = GRAPHS[g]["t"] // (2 * GRP)
                self.rows, self.width, self.pitch = rows, width, pitch
                self.prepared, self.multiplied, self.ended = (sem(f"{name}_{x}") for x in ("prepared", "multiplied", "ended"))
                self.banks = -(-NB * pitch // 512)

            def vector(self, dve):
                def body(i, h, first):
                    if not first:
                        dve.wait_ge(self.multiplied, 2 * i + h - 1)
                        dve.wait_ge(self.multiplied, 1)
                    dve.tensor_tensor(Sv[:, h, :, :], IOTA.rearrange("p (a b) -> p a b", a=1).to_broadcast([P, GRP, P]),
                                      RELE[:, bass.ds((2 * i + h) * GRP, GRP)].rearrange("p (a b) -> p a b", b=1).to_broadcast([P, GRP, P]),
                                      ALU.is_equal).then_inc(self.prepared, 1)
                pairs_of(dve, self.steps, body)
                dve.wait_ge(self.ended, 1)

            def tensor(self, pe, zeros):
                for k in range(self.banks):
                    pe.matmul(PB[k], zeros[:, 0:P], zeros, start=True, stop=False, skip_group_check=True)

                def body(i, h, first):
                    g = 2 * i + h
                    blocks = blocks_of(pe, g, GRP)
                    pe.wait_ge(self.prepared, g + 1)
                    pe.wait_ge(self.prepared, 1)
                    for j in range(GRP):
                        m = pe.matmul(PSUM[:, bass.ds(blocks[j] * self.pitch, self.width)], Sv[:, h, j, :], self.rows(g, j),
                                      start=False, stop=False, skip_group_check=True)
                    m.then_inc(self.multiplied, 1)
                pairs_of(pe, self.steps, body)
                pe.drain().then_inc(self.ended, 1)

        class Spread:

            def __init__(self, name, g):
                self.g, self.steps = g, GRAPHS[g]["t"] // (2 * GRP)
                self.rel_in = [sem(f"{name}_rel_in{h}") for h in (0, 1)]
                self.marked, self.multiplied, self.kept = (sem(f"{name}_{x}") for x in ("marked", "multiplied", "kept"))
                self.REL = ar(GR0 + 1024, 1024).bitcast(BF16).rearrange("p (h c) -> p h c", h=2)

            def sync(self, sp):
                def body(i, h, first):
                    if not first:
                        sp.wait_ge(self.marked, 2 * i + h - 1)
                        sp.wait_ge(self.marked, 1)
                    src = relD[self.g][0:1, bass.ds((2 * i + h) * GRP * P, GRP * P)].to_broadcast([P, GRP * P])
                    sp.dma_start(self.REL[:, h, :], src).then_inc(self.rel_in[h], 16)
                pairs_of(sp, self.steps, body)

            def vector(self, dve, ed):
                def keep(g, h):
                    dve.wait_ge(self.multiplied, g + 1)
                    dve.wait_ge(self.multiplied, 1)
                    dve.tensor_copy(ed[:, bass.ds(g * 4 * GRP, 4 * GRP)], PB[h][:, 0:4 * GRP]).then_inc(self.kept, 1)

                def body(i, h, first):
                    dve.wait_ge(self.rel_in[h], 16 * (i + 1))
                    dve.wait_ge(self.rel_in[h], 16)
                    dve.tensor_scalar(Sv[:, h, :, :].rearrange("p t n -> p (t n)"), self.REL[:, h, :], PCOL, None,
                                      ALU.is_equal).then_inc(self.marked, 1)
                    if not (first and h == 0):
                        keep(2 * i + h - 1, 1 - h)
                pairs_of(dve, self.steps, body)
                keep(2 * self.steps - 1, 1)
                dve.drain()

            def tensor(self, pe):
                def body(i, h, first):
                    g = 2 * i + h
                    blocks = blocks_of(pe, g, GRP)
                    pe.wait_ge(self.marked, g + 1)
                    pe.wait_ge(self.marked, 1)
                    if not first:
                        pe.wait_ge(self.kept, g - 1)
                        pe.wait_ge(self.kept, 1)
                    flat = EDN[:, :, :].rearrange("p b h -> p (b h)")
                    for j in range(GRP):
                        m = pe.matmul(PB[h][:, 4 * j:4 * j + 4], Sv[:, h, j, :], flat[:, bass.ds(blocks[j] * 4, 4)],
                                      start=True, stop=True)
                    m.then_inc(self.multiplied, 1)
                pairs_of(pe, self.steps, body)

        edge_tmp = ARENA[0:4, S0 + 800:S0 + 800 + P]
        edge4 = sb("edge4", [P, 16])
        row4 = ARENA[0:4, S0:S0 + 6 * P]
        exp_go, exp_done = sem("exp_go"), sem("exp_done")

        class Weights:

            def __init__(self, g, es, ed, te, dst, pen):
                G = GRAPHS[g]
                self.g, self.tq, self.t = g, G["tq"], G["t"]
                self.L = self.tq * P
                self.es, self.ed, self.dst, self.pen = es, ed, dst, pen
                self.te = te.rearrange("p (h l) -> p h l", h=4)

            def part(self, v, h, q):
                return v.rearrange("e (p q) h -> e q p h", q=self.tq)[:, q, :, h]

            def groups(self):
                return [(h, n0, min(4, self.tq - n0)) for h in range(4) for n0 in range(0, self.tq, 4)]

            def carry(self, dve, back):
                end = 0 if back else self.L - 1
                dve.tensor_copy(edge4[:, 0:4], self.te[:, :, end])
                dve.drain().then_inc(asked, 1)
                dve.wait_ge(answered, nth("answers"))
                first, last, val = row4[:, 0:P], row4[:, P:2 * P], row4[:, 2 * P:3 * P]
                d0, d1, c = row4[:, 3 * P:4 * P], row4[:, 4 * P:5 * P], row4[:, 5 * P:6 * P]
                dve.tensor_copy(row4[:, 0:3 * P], PB[2][0:4, 0:3 * P])
                dve.memset(d0, -BIG)
                dve.memset(d1, -BIG)
                dve.drain()
                n = P - 1
                x, y = (slice(0, n), slice(1, P)) if back else (slice(1, P), slice(0, n))
                near, far = (last, first) if back else (first, last)
                dve.tensor_tensor(c[:, x], near[:, x], far[:, y], ALU.not_equal)
                dve.drain()
                dve.tensor_scalar(c[:, x], c[:, x], -BIG, None, ALU.mult)
                dve.tensor_tensor(d0[:, y], first[:, y], last[:, y], ALU.not_equal)
                dve.drain()
                dve.scalar_tensor_tensor(out=edge_tmp[:, x], in0=d0[:, y], scalar=-BIG, in1=c[:, x], op0=ALU.mult, op1=ALU.add)
                dve.tensor_tensor(d1[:, x], val[:, y], c[:, x], ALU.add)
                dve.drain()
                dve.memset(d0, -BIG)
                dve.drain()
                dve.tensor_copy(d0[:, x], edge_tmp[:, x])
                dve.drain()
                turn = slice(None, None, -1) if back else slice(None)
                dve.tensor_tensor_scan(c[:, turn], d0[:, turn], d1[:, turn], -BIG, ALU.add, ALU.max)
                dve.drain().then_inc(asked, 1)
                dve.wait_ge(answered, nth("answers"))
                dve.tensor_copy(edge4[:, 12:16], PB[3][:, 0:4])
                dve.drain()

            def scan(self, dve, back, first):
                L = self.L
                for h in range(4):
                    v = self.te[:, h, ::-1] if back else self.te[:, h, :]
                    pen = self.pen[:, L:0:-1] if back else self.pen[:, 0:L]
                    dve.tensor_tensor_scan(v, pen, v, -BIG if first else edge4[:, 12 + h:13 + h], ALU.add, ALU.max)
                dve.drain()

            def vector(self, dve):
                tq, L, T = self.tq, self.L, self.t
                for h, n0, n in self.groups():
                    dve.drain().then_inc(asked, 1)
                    dve.wait_ge(answered, nth("answers"))
                    dve.tensor_copy(self.te[:, h, n0 * P:(n0 + n) * P], PB[2][:, 0:n * P])
                dve.memset(self.pen[:, 0:L + 1], 0.0)
                dve.drain()
                dve.tensor_tensor(self.pen[:, 1:L], self.dst[:, 1:L], self.dst[:, 0:L - 1], ALU.not_equal)
                for h in range(4):
                    dve.tensor_copy(edge4[:, 4 + h:5 + h], self.dst[:, 0:1])
                    dve.tensor_copy(edge4[:, 8 + h:9 + h], self.dst[:, L - 1:L])
                dve.drain()
                dve.tensor_scalar(self.pen[:, 1:L], self.pen[:, 1:L], -BIG, None, ALU.mult)
                dve.drain()
                for back in (False, True):
                    self.scan(dve, back, True)
                    self.carry(dve, back)
                    self.scan(dve, back, False)
                es, ed = self.es, self.ed
                dve.tensor_tensor(es, es, ed, ALU.add)
                dve.drain()
                dve.scalar_tensor_tensor(out=es, in0=es, scalar=0.2, in1=es, op0=ALU.mult, op1=ALU.max)
                for h, n0, n in self.groups():
                    dve.drain().then_inc(asked, 1)
                    dve.wait_ge(answered, nth("answers"))
                    for q in range(n0, n0 + n):
                        v = self.part(ed, h, q)
                        dve.tensor_tensor(v, PB[2][:, (q - n0) * P:(q - n0 + 1) * P], v, ALU.add)
                dve.drain()
                dve.scalar_tensor_tensor(out=ed, in0=ed, scalar=0.2, in1=ed, op0=ALU.mult, op1=ALU.max)
                dve.drain()
                dve.tensor_tensor(es, es, ed, ALU.subtract)
                dve.drain().then_inc(exp_go, 1)
                dve.wait_ge(exp_done, nth("exponentials"))

            def carry_tensor(self, pe):
                pe.wait_ge(asked, nth("questions"))
                for k, a in enumerate((4, 8, 0)):
                    t = pe.transpose(PB[2][0:4, k * P:(k + 1) * P], edge4[:, a:a + 4], IDENT)
                t.then_inc(answered, 1)
                pe.wait_ge(asked, nth("questions"))
                pe.transpose(PB[3][:, 0:4], row4[:, 5 * P:6 * P], IDENT[0:4, 0:4]).then_inc(answered, 1)

            def tensor(self, pe):
                for h, n0, n in self.groups():
                    pe.wait_ge(asked, nth("questions"))
                    for q in range(n0, n0 + n):
                        t = pe.transpose(PB[2][:, (q - n0) * P:(q - n0 + 1) * P], self.part(self.es, h, q), IDENT)
                    t.then_inc(answered, 1)
                self.carry_tensor(pe)
                self.carry_tensor(pe)
                for h, n0, n in self.groups():
                    pe.wait_ge(asked, nth("questions"))
                    for q in range(n0, n0 + n):
                        t = pe.transpose(PB[2][:, (q - n0) * P:(q - n0 + 1) * P], self.te[:, h, q * P:(q + 1) * P], IDENT)
                    t.then_inc(answered, 1)

        W0 = ACC0
        w1 = lambda e: ar(W0 + 2048 * e, 1024).rearrange("p (k f) -> p k f", k=2)
        w2 = lambda e: ar(W0 + 2048 * e + 1024, 1024).rearrange("p (f d) -> p f d", f=4)
        b1 = lambda e: ar(W0 + 8192 + 4 * e, 4)
        b2 = lambda e: ar(W0 + 8256 + D * e, D)
        GAMMA, BETA = ar(W0 + 9280, D), ar(W0 + 9536, D)
        FXT = ar(GR0, 512).rearrange("p (k n) -> p k n", k=2)
        FHT = ar(GR0 + 512, 2048).rearrange("p (a f n) -> p a f n", a=2, f=4)

        class Experts:

            def __init__(self, name, n, gate, dest):
                self.n, self.gate, self.dest = n, gate, dest
                self.rows_in, self.turned, self.cols_in, self.hidden, self.curved, self.mixed, self.added, self.done = (
                    sem(f"{name}_{x}") for x in ("rows_in", "turned", "cols_in", "hidden", "curved", "mixed", "added", "done"))

            def each(self, eng, body):
                body(0, True, False)
                with eng.Fori(1, NB // 2 - 1) as i:
                    body(i, False, False)
                body(NB // 2 - 1, False, True)

            def turn(self, pe, i):
                pe.wait_ge(self.rows_in, i + 1)
                pe.wait_ge(self.rows_in, 1)
                for j in range(2):
                    for k in range(2):
                        t = pe.transpose(PB[0][:, k * 256 + j * P:k * 256 + (j + 1) * P], XIN[:, j, k * P:(k + 1) * P], IDENT)
                t.then_inc(self.turned, 1)

            def tensor(self, pe):
                n = self.n

                def up(e):
                    for f in range(4):
                        for k in range(2):
                            m = pe.matmul(PB[1 + 2 * (e % 2) + f // 2][:, (f % 2) * 256:(f % 2 + 1) * 256],
                                          w1(e)[:, k, f * P:(f + 1) * P], FXT[:, k, :], start=(k == 0), stop=(k == 1))
                        if f % 2:
                            m.then_inc(self.hidden, 1)

                def body(i, first, last):
                    pe.wait_ge(self.cols_in, i + 1)
                    pe.wait_ge(self.cols_in, 1)
                    up(0)
                    for e in range(n):
                        if e + 1 < n:
                            up(e + 1)
                        elif not last:
                            self.turn(pe, i + 1)
                        pe.wait_ge(self.curved, i * n + e + 1)
                        pe.wait_ge(self.curved, 1)
                        if not (first and e < 2):
                            pe.wait_ge(self.added, i * n + e - 1)
                            pe.wait_ge(self.added, 1)
                        for j in range(2):
                            for f in range(4):
                                m = pe.matmul(PB[5 + e % 2][:, j * D:(j + 1) * D], FHT[:, e % 2, f, j * P:(j + 1) * P],
                                              w2(e)[:, f, :], start=(f == 0), stop=(f == 3))
                        m.then_inc(self.mixed, 1)
                self.turn(pe, 0)
                self.each(pe, body)

            def scalar(self, act):
                n = self.n

                def columns(i):
                    act.wait_ge(self.turned, i + 1)
                    act.wait_ge(self.turned, 1)
                    act.copy(FXT[:, :, :].rearrange("p k n -> p (k n)"), PB[0][:, :]).then_inc(self.cols_in, 1)

                def body(i, first, last):
                    for e in range(n):
                        if not (first and e < 2):
                            act.wait_ge(self.mixed, i * n + e - 1)
                            act.wait_ge(self.mixed, 1)
                        for f in range(4):
                            if f % 2 == 0:
                                act.wait_ge(self.hidden, (i * n + e) * 2 + f // 2 + 1)
                                act.wait_ge(self.hidden, 1)
                            a = act.activation(FHT[:, e % 2, f, :], PB[1 + 2 * (e % 2) + f // 2][:, (f % 2) * 256:(f % 2 + 1) * 256],
                                               ACT.Gelu, bias=b1(e)[:, f:f + 1])
                        a.then_inc(self.curved, 1)
                    if not last:
                        columns(i + 1)
                columns(0)
                self.each(act, body)

            def vector(self, dve):
                n = self.n

                def rows(i):
                    dve.tensor_copy(XIN[:, :, :], Hv[:, bass.ds(2 * i, 2), :])
                    dve.drain().then_inc(self.rows_in, 1)

                def body(i, first, last):
                    for e in range(n):
                        if e == n - 1 and not last:
                            dve.wait_ge(self.turned, i + 1)
                            dve.wait_ge(self.turned, 1)
                            rows(i + 1)
                        dve.wait_ge(self.mixed, i * n + e + 1)
                        dve.wait_ge(self.mixed, 1)
                        for j in range(2):
                            to, g = self.dest(2 * i + j), self.gate(2 * i + j, e)
                            dve.scalar_tensor_tensor(out=to, in0=PB[5 + e % 2][:, j * D:(j + 1) * D], scalar=g, in1=to,
                                                     op0=ALU.mult, op1=ALU.add)
                        dve.drain().then_inc(self.added, 1)
                        for j in range(2):
                            to, g = self.dest(2 * i + j), self.gate(2 * i + j, e)
                            dve.scalar_tensor_tensor(out=to, in0=b2(e), scalar=g, in1=to, op0=ALU.mult, op1=ALU.add)
                        dve.drain()
                    dve.drain().then_inc(self.done, 1)
                rows(0)
                self.each(dve, body)

        XIN = ar(GR0 + 2560, 512).rearrange("p (j d) -> p j d", j=2)

        def serve_exp(act, v):
            act.wait_ge(exp_go, nth("exponentials asked"))
            act.activation(v, v, ACT.Exp).then_inc(exp_done, 1)

        def softmax8(dve, v, tmp):
            dve.drain()
            dve.tensor_reduce(tmp, v, AX.X, ALU.max)
            dve.drain()
            dve.tensor_scalar(v, v, tmp, None, ALU.subtract)
            dve.drain().then_inc(exp_go, 1)
            dve.wait_ge(exp_done, nth("exponentials"))
            dve.tensor_reduce(tmp, v, AX.X, ALU.add)
            dve.drain()
            dve.reciprocal(tmp, tmp)
            dve.drain()
            dve.tensor_scalar(v, v, tmp, None, ALU.mult)
            dve.drain()

        def top2(dve, s, B, E, a, b, m, gates, first_id=None, second_id=None):
            rep = lambda v: v.rearrange("p (b e) -> p b e", e=1).to_broadcast([P, B, E])
            ids = IOTA[:, 0:E].rearrange("p (b e) -> p b e", b=1).to_broadcast([P, B, E])
            m1, m2, i1, d = (m[:, k, :] for k in range(4))

            def winner(v, best, hot, ident):
                dve.tensor_reduce(best, v, AX.X, ALU.max)
                dve.drain()
                dve.tensor_tensor(hot, v, rep(best), ALU.not_equal)
                dve.drain()
                dve.scalar_tensor_tensor(out=hot, in0=hot, scalar=float(E), in1=ids, op0=ALU.mult, op1=ALU.add)
                dve.drain()
                dve.tensor_reduce(ident, hot, AX.X, ALU.min)
                dve.drain()
                dve.tensor_tensor(hot, ids, rep(ident), ALU.is_equal)
                dve.drain()

            winner(s, m1, a, i1)
            if first_id is not None:
                dve.tensor_copy(first_id, i1)
            dve.scalar_tensor_tensor(out=s, in0=a, scalar=-BIG, in1=s, op0=ALU.mult, op1=ALU.add)
            dve.drain()
            winner(s, m2, b, i1)
            if second_id is not None:
                dve.tensor_copy(second_id, i1)
            dve.tensor_tensor(d, m2, m1, ALU.subtract)
            dve.drain().then_inc(exp_go, 1)
            dve.wait_ge(exp_done, nth("exponentials"))
            dve.tensor_scalar(m1, d, 1.0, None, ALU.add)
            dve.drain()
            dve.reciprocal(m1, m1)
            dve.drain()
            dve.tensor_tensor(m2, d, m1, ALU.mult)
            dve.drain()
            dve.tensor_tensor(a, a, rep(m1), ALU.mult)
            dve.tensor_tensor(b, b, rep(m2), ALU.mult)
            dve.drain()
            dve.tensor_tensor(gates, a, b, ALU.add)
            dve.drain()

        def extend(dve, w, n, att, heads, tmp, to):
            dve.tensor_tensor(tmp, w, att, ALU.mult)
            dve.drain()
            dve.tensor_reduce(to, tmp.rearrange("p (h d) -> p h d", h=heads), AX.X, ALU.add)
            dve.drain()

        def block(V, b):
            return V[:, bass.ds(b, 1), :].rearrange("p a d -> p (a d)")

        DSTS = {0: ar(ACC0 + 9000, 896), 2: ar(23040, 1152)}
        SMALL2 = ar(28300, 48).rearrange("p (a n) -> p a n", n=16)
        IDSI = sb("IDSI", [P, 2], I32)

        loads, load_sem, load_total = {}, {}, {}

        def define_load(name, pairs):
            loads[name], load_sem[name], load_total[name] = pairs, sem(f"load_{name}"), 16 * len(pairs)

        def load(sp, name):
            for dst, src in loads[name]:
                sp.dma_start(dst, src, allow_slow_non_contiguous=True).then_inc(load_sem[name], 16)

        row = lambda a: a.rearrange("(o n) -> o n", o=1).to_broadcast([P, a.shape[0]])
        rows_by_chunk = lambda a: a.rearrange("(k p) n -> p k n", p=P)
        WX = ar(WS0, 2 * (D + 8)).rearrange("p (k n) -> p k n", k=2)
        ATT = ar(WS0 + 600, 512).rearrange("p (a n) -> p a n", a=2)
        last = N - (EB - 1) * P
        define_load("start", [(CON[:, :], consts), (FLIPS, flips), (WX[:, :, 0:D], rows_by_chunk(A["L0_gnn_W"])),
                              (ATT[:, 0, :], row(A["L0_gnn_a_src"].rearrange("h d -> (h d)"))),
                              (ATT[:, 1, :], row(A["L0_gnn_a_dst"].rearrange("h d -> (h d)")))])
        define_load("x", [(X[:, 8 * c:8 * c + 8, :], A["x"][8 * c * P:8 * (c + 1) * P, :].rearrange("(b p) d -> p b d", p=P))
                          for c in range(6)])
        define_load("x_end", [(X[0:last, EB - 1, :], A["x"][(EB - 1) * P:N, :])])
        for g in range(3):
            define_load(f"graph{g}", graph_loads(g))
        BIASR = sb("BIASR", [P, D])
        sage_w = lambda m: ar(WS0 + 512 * m, 512).rearrange("p (k n) -> p k n", k=2)
        mats = [A["L1_gnn_W_in"]] + [A[f"L1_gnn_W_{x}"][l] for l in range(3) for x in ("agg", "self")] + [A["L1_gnn_W_out"]]
        define_load("sage", [(sage_w(m), rows_by_chunk(a)) for m, a in enumerate(mats)])
        biases = [A["L1_gnn_b_in"]] + [A["L1_gnn_b_hid"][l] for l in range(3)] + [A["L1_gnn_b_out"]]
        for m, a in enumerate(biases):
            define_load(f"bias{m}", [(BIASR[:, :], row(a))])
        WRT, BRT = ar(W0 + 10800, 16).rearrange("p (k n) -> p k n", k=2), ar(W0 + 10816, 8)
        define_load("router", [(WRT, rows_by_chunk(A["L0_ffn_Wr"])), (BRT, row(A["L0_ffn_br"])),
                               (GAMMA, row(A["L0_ffn_gamma"])), (BETA, row(A["L0_ffn_beta"]))])
        WG = ar(WS0, 48).rearrange("p (k n) -> p k n", k=2)
        SMALL = ar(WS0 + 64, 96).rearrange("p (a n) -> p a n", n=16)
        define_load("gat1", [(WG[:, :, 0:16], rows_by_chunk(A["L1_ffn_W_gat"])),
                             (SMALL[:, 0, :], row(A["L1_ffn_att_src"].rearrange("h d -> (h d)"))),
                             (SMALL[:, 1, :], row(A["L1_ffn_att_dst"].rearrange("h d -> (h d)"))),
                             (SMALL[:, 2, :], row(A["L1_ffn_b_gat"])), (SMALL[:, 3, :], row(A["L1_ffn_ln_gamma"])),
                             (SMALL[:, 4, :], row(A["L1_ffn_ln_beta"]))])
        define_load("experts1", [p for e in range(4) for p in (
            (w1(e), rows_by_chunk(A["L1_ffn_W1"][e])), (w2(e), rows_by_chunk(A["L1_ffn_W2"][e])),
            (b1(e), A["L1_ffn_b1"][e].rearrange("(f p) -> p f", p=P)), (b2(e), row(A["L1_ffn_b2"][e])))])
        define_load("small2", [(SMALL2[:, k, :], row(A[f"L1_ffn_{x}"])) for k, x in enumerate(("b_gat", "ln_gamma", "ln_beta"))])
        for g in (0, 2):
            define_load(f"dst{g}", [(DSTS[g], dstD[g])])

        zeroed = sem("zeroed")
        es_kept = sem("es_kept")
        chosen = sem("chosen")
        chosen_in = sem("chosen_in")
        stored = sem("stored")
        weighted = sem("weighted")
        finished = sem("finished")

        def chunk_stores(sp, table, V, width, taken, s, base):
            for c in range(5):
                sp.wait_ge(taken, 10 * (c + 1))
                dst = table[10 * c * P:10 * (c + 1) * P, :].rearrange("(b p) d -> p b d", p=P)
                sp.dma_start(dst, V[:, 10 * c:10 * (c + 1), 0:width]).then_inc(s, 16)
            sp.wait_ge(s, base + 80)

        first = Dense("project", 2, lambda k: WX[:, k, :], D + 8)
        es_gather = Kept("es", 0, esD, 4, 4)
        spread0 = Spread("spread0", 0)
        ES0, ED0, TE0 = (ar(H0 + k * 3584, 3584) for k in range(3))
        weights0 = Weights(0, ES0.rearrange("p (t h) -> p t h", h=4), ED0.rearrange("p (t h) -> p t h", h=4),
                           TE0, DSTS[0], ar(ACC0 + 10000, 900))
        hp_gather = Gather("hp", 0, tabD, D, ACCW)

        def edge_weights(g):
            return ES0[:, bass.ds(g * QRT * 4, QRT * 4)].rearrange("p (t h) -> p t h", h=4)

        sums0 = Sums("sums0", hp_gather, ACCW, edge_weights)
        W12 = ar(W0 + 10830, 2)
        experts0 = Experts("experts0", 2, lambda b, e: W12[:, e:e + 1], lambda b: block(Hv, b))
        enter = Dense("enter", 2, lambda k: sage_w(0)[:, k, :], D)
        hop_gather = [Gather(f"hop{l}", 1, tabD, D, ACCW) for l in range(3)]
        hops = [Sums(f"hops{l}", hop_gather[l], D + 1) for l in range(3)]
        mixes = [Dense(f"mix{l}", 4, (lambda l: lambda k: sage_w(1 + 2 * l + k // 2)[:, k % 2, :])(l), D) for l in range(3)]
        leave = Dense("leave", 2, lambda k: sage_w(7)[:, k, :], D)
        T20 = ar(ACC0, NB * 24).rearrange("p (b n) -> p b n", n=24)
        project2 = Dense("project2", 2, lambda k: WG[:, k, :], 24)
        G1 = ar(ACC0, 1152 * 20).rearrange("p (t n) -> p t n", n=20)
        ED2, TE2 = ar(24192, 4608), ar(28800, 4608)
        g1_gather = Kept("g1", 2, t20D, 20, 20)
        spread2 = Spread("spread2", 2)
        weights2 = Weights(2, G1[:, :, 16:20], ED2.rearrange("p (t h) -> p t h", h=4), TE2, DSTS[2], SRCE[:, :])
        ACC2 = ar(24192, NB * 20)
        sums2 = NarrowSums("sums2", 2, lambda g, j: ar(ACC0, 1152 * 20)[:, bass.ds((g * GRP + j) * 20, 20)], 20, 32)
        ZEROS = ar(GR0, 512)
        experts1 = Experts("experts1", 4, lambda b, e: EDN[:, bass.ds(b, 1), e:e + 1].rearrange("p a e -> p (a e)"),
                           lambda b: block(X, b))

        LOGITS, DIFF0, DIFF1 = ar(W0 + 10840, 8), ar(W0 + 10883, 1), ar(28100 + 3 * NB, NB)

        block_ctx = ctx.enter_context(nc.Block())

        def normalise_all(dve):
            with dve.Fori(0, NB // 2) as i:
                for j in range(2):
                    normalise(dve, block(Hv, 2 * i + j), X, 2 * i + j)
            dve.drain()

        def over_blocks(v):
            return v.rearrange("p (b d) -> p b d", b=1).to_broadcast([P, NB, v.shape[1]])

        @block_ctx.vector
        def _(dve):
            dve.memset(X[:, EB - 1:NB, :], 0.0)
            dve.drain().then_inc(zeroed, 1)
            dve.wait_ge(load_sem["start"], load_total["start"])
            for k in range(2):
                for a in range(2):
                    extend(dve, WX[:, k, 0:D], D, ATT[:, a, :], 4, ar(ACC0, D), WX[:, k, D + 4 * a:D + 4 * a + 4])
            dve.wait_ge(load_sem["x"], load_total["x"])
            dve.wait_ge(load_sem["x_end"], load_total["x_end"])
            stats_vector(dve, X)

            def keep(dve, bank, b):
                dve.tensor_copy(block(Hv, b), bank[:, 0:D])
                dve.tensor_copy(block(ESN, b), bank[:, D:D + 4])
                dve.tensor_copy(block(EDN, b), bank[:, D + 4:D + 8])
            first.vector(dve, lambda dve, to, b: normalise(dve, to[:, 0:D], X, b), keep)
            cur = sort_vector(dve, 0)
            count_vector(dve, 0, cur)
            tiles_vector(dve, 0)
            dve.drain().then_inc(met, 1)
            dve.wait_ge(met, MEETING * 1)

            t = GRAPHS[0]["t"] * 4
            dve.memset(ES0[:, t:3584], 0.0)
            dve.memset(ED0[:, t:3584], 0.0)
            spread0.vector(dve, ED0)
            for g in (1, 2):
                cur = sort_vector(dve, g)
                count_vector(dve, g, cur)
            for g in (1, 2):
                tiles_vector(dve, g)
            dve.wait_ge(es_kept, 1)
            dve.wait_ge(load_sem["dst0"], load_total["dst0"])
            weights0.vector(dve)
            dve.memset(ar(ACC0, NB * ACCW), 0.0)
            dve.drain().then_inc(met, 1)
            dve.wait_ge(met, MEETING * 2)

            sums0.vector(dve)
            dve.tensor_scalar(ESN[:, :, :], ACCv[:, :, D:D + 4], 1e-16, None, ALU.add)
            dve.drain()
            dve.reciprocal(ESN[:, :, :], ESN[:, :, :])
            dve.drain()
            v = ACCv[:, :, 0:D].rearrange("p b (h d) -> p b h d", h=4)
            dve.tensor_tensor(v, v, ESN[:, :, :].rearrange("p b (h o) -> p b h o", o=1).to_broadcast([P, NB, 4, 64]), ALU.mult)
            dve.drain()
            dve.tensor_tensor(X[:, :, :], X[:, :, :], ACCv[:, :, 0:D], ALU.add)
            dve.drain()
            dve.drain().then_inc(met, 1)
            dve.wait_ge(met, MEETING * 3)

            stats_vector(dve, X)
            normalise_all(dve)
            dve.wait_ge(load_sem["router"], load_total["router"])
            sumx = ar(W0 + 10000, D)
            mb = ar(W0 + 10300, 2 * P).rearrange("p (k n) -> p k n", k=2)
            lg = LOGITS
            t1, a8, b8 = ar(W0 + 10850, 1), ar(W0 + 10860, 8), ar(W0 + 10870, 8)
            m4, g8, ids = ar(W0 + 10880, 4), ar(W0 + 10890, 8), ar(W0 + 10900, 2)
            c8, d8 = ar(W0 + 10910, 8), ar(W0 + 10920, 8)
            dve.tensor_reduce(sumx, Hv.rearrange("p b d -> p d b"), AX.X, ALU.add)
            dve.drain().then_inc(asked, 1)
            dve.wait_ge(answered, nth("answers"))
            for k in range(2):
                dve.tensor_scalar(mb[:, k, :], ONES, PB[2][:, k:k + 1], 1.0 / N, ALU.mult, ALU.mult)
            dve.drain().then_inc(asked, 1)
            dve.wait_ge(answered, nth("answers"))
            dve.tensor_tensor(lg, PB[3][:, 0:8], BRT, ALU.add)
            softmax8(dve, lg, t1)
            capacity = float(-(-N * 5 // (4 * 8)))
            dve.tensor_scalar(c8, lg, float(N), None, ALU.mult)
            dve.drain()
            dve.tensor_scalar(d8, c8, capacity, None, ALU.max)
            dve.drain()
            dve.reciprocal(d8, d8)
            dve.drain()
            dve.tensor_scalar(d8, d8, capacity, -1.0, ALU.mult, ALU.add)
            dve.tensor_scalar(c8, c8, capacity, None, ALU.is_gt)
            dve.drain()
            dve.tensor_tensor(c8, c8, d8, ALU.mult)
            dve.drain()
            dve.tensor_scalar(c8, c8, 1.0, None, ALU.add)
            dve.drain()
            dve.tensor_tensor(lg, lg, c8, ALU.mult)
            softmax8(dve, lg, t1)
            one = lambda v: v.rearrange("p (b e) -> p b e", b=1)
            top2(dve, one(lg), 1, 8, one(a8), one(b8), m4.rearrange("p (k b) -> p k b", b=1), one(g8),
                 ids[:, 0:1], ids[:, 1:2])
            dve.tensor_copy(W12, m4[:, 0:2])
            dve.tensor_copy(IDSI[:, :], ids)
            dve.drain().then_inc(chosen, 1)
            dve.wait_ge(chosen_in, 16 * 8)
            experts0.vector(dve)
            stats_vector(dve, Hv)
            with dve.Fori(0, NB // 2) as i:
                for j in range(2):
                    normalise(dve, block(Hv, 2 * i + j), Hv, 2 * i + j)
            dve.drain()
            dve.tensor_tensor(Hv, Hv, over_blocks(GAMMA), ALU.mult)
            dve.tensor_tensor(X[:, :, :], X[:, :, :], over_blocks(BETA), ALU.add)
            dve.drain()
            dve.tensor_tensor(X[:, :, :], X[:, :, :], Hv, ALU.add)
            dve.drain()
            stats_vector(dve, X)
            dve.wait_ge(load_sem["sage"], load_total["sage"])
            dve.wait_ge(load_sem["bias0"], load_total["bias0"])

            def enter_take(dve, bank, b):
                dve.tensor_tensor(block(Hv, b), bank[:, 0:D], BIASR[:, :], ALU.add)
            enter.vector(dve, lambda dve, to, b: normalise(dve, to[:, 0:D], X, b), enter_take)

            def room_for_sums(dve, ga):
                dve.memset(ga.ring[:, :, :, D:D + 1], 1.0)
                dve.memset(ar(ACC0, NB * ACCW), 0.0)
            room_for_sums(dve, hop_gather[0])
            dve.drain().then_inc(met, 1)
            dve.wait_ge(met, MEETING * 4)

            for l in range(3):
                hops[l].vector(dve)
                dve.tensor_scalar(RS[:, :], ACCv[:, :, D], 1.0, None, ALU.max)
                dve.drain()
                dve.reciprocal(RS[:, :], RS[:, :])
                dve.drain()
                dve.wait_ge(load_sem[f"bias{l + 1}"], load_total[f"bias{l + 1}"])

                def mix_in(dve, to, b):
                    dve.tensor_scalar(to[:, 0:D], ar(ACC0, NB * ACCW)[:, bass.ds(b * ACCW, D)], RS[:, bass.ds(b, 1)], None, ALU.mult)
                    dve.tensor_copy(to[:, D:2 * D], block(Hv, b))

                def mix_take(dve, bank, b):
                    dve.tensor_tensor(block(Hv, b), bank[:, 0:D], BIASR[:, :], ALU.add)
                    dve.drain()
                    dve.tensor_scalar(block(Hv, b), block(Hv, b), 0.0, None, ALU.max)
                mixes[l].vector(dve, mix_in, mix_take)
                if l < 2:
                    room_for_sums(dve, hop_gather[l + 1])
                    dve.drain().then_inc(met, 1)
                    dve.wait_ge(met, MEETING * (5 + l))
            dve.drain().then_inc(sp_go, 1)
            dve.wait_ge(load_sem["bias4"], load_total["bias4"])

            def leave_take(dve, bank, b):
                dve.tensor_tensor(block(X, b), block(X, b), bank[:, 0:D], ALU.add)
                dve.drain()
                dve.tensor_tensor(block(X, b), block(X, b), BIASR[:, :], ALU.add)
            leave.vector(dve, lambda dve, to, b: dve.tensor_copy(to[:, 0:D], block(Hv, b)), leave_take)
            stats_vector(dve, X)
            dve.drain().then_inc(sp_go, 1)
            dve.wait_ge(load_sem["gat1"], load_total["gat1"])
            for k in range(2):
                for a in range(2):
                    extend(dve, WG[:, k, 0:16], 16, SMALL[:, a, :], 4, SM[:, 0:16], WG[:, k, 16 + 4 * a:20 + 4 * a])
            project2.vector(dve, lambda dve, to, b: normalise(dve, to[:, 0:D], X, b),
                            lambda dve, bank, b: dve.tensor_copy(block(T20, b), bank[:, 0:24]))
            dve.tensor_copy(EDN[:, :, :], T20[:, :, 20:24])
            dve.drain().then_inc(met, 1)
            dve.wait_ge(met, MEETING * 7)

            t = GRAPHS[2]["t"]
            dve.memset(ED2[:, 4 * t:4608], 0.0)
            dve.memset(G1[:, t:1152, :], 0.0)
            spread2.vector(dve, ED2)
            dve.wait_ge(es_kept, 2)
            dve.wait_ge(load_sem["dst2"], load_total["dst2"])
            weights2.vector(dve)
            v = G1[:, :, 0:16].rearrange("p t (h e) -> p t h e", h=4)
            dve.tensor_tensor(v, v, G1[:, :, 16:20].rearrange("p t (h o) -> p t h o", o=1).to_broadcast([P, 1152, 4, 4]), ALU.mult)
            dve.memset(ZEROS, 0.0)
            dve.drain().then_inc(weighted, 1)
            sums2.vector(dve)
            dve.tensor_copy(ACC2.rearrange("p (b n) -> p b n", n=20),
                            PSUM[:, 0:NB * 32].rearrange("p (b n) -> p b n", n=32)[:, :, 0:20])
            dve.drain()
            dve.drain().then_inc(met, 1)
            dve.wait_ge(met, MEETING * 8)

            A16 = ar(25800, NB * 16).rearrange("p (b n) -> p b n", n=16)
            B16 = ar(26600, NB * 16).rearrange("p (b n) -> p b n", n=16)
            mean, rs16 = ar(27400, NB), ar(27450, NB)
            s4, a4, c4, m4 = (ar(27500 + 200 * k, NB * 4) for k in range(4))
            acc2 = ACC2.rearrange("p (b n) -> p b n", n=20)
            v4 = lambda v: v.rearrange("p (b e) -> p b e", e=4)
            rep16 = lambda v: v.rearrange("p (b o) -> p b o", o=1).to_broadcast([P, NB, 16])
            dve.wait_ge(load_sem["small2"], load_total["small2"])
            dve.tensor_scalar(v4(a4), acc2[:, :, 16:20], 1e-16, None, ALU.add)
            dve.drain()
            dve.reciprocal(a4, a4)
            dve.drain()
            for h in range(4):
                dve.tensor_tensor(A16[:, :, 4 * h:4 * h + 4], acc2[:, :, 4 * h:4 * h + 4],
                                  v4(a4)[:, :, h:h + 1].to_broadcast([P, NB, 4]), ALU.mult)
            dve.drain()
            dve.tensor_tensor(A16, A16, over_blocks(SMALL2[:, 0, :]), ALU.add)
            dve.drain()
            dve.tensor_reduce(mean, A16, AX.X, ALU.add)
            dve.drain()
            dve.tensor_scalar(mean, mean, 1.0 / 16, None, ALU.mult)
            dve.drain()
            dve.tensor_tensor(A16, A16, rep16(mean), ALU.subtract)
            dve.drain()
            dve.tensor_tensor(B16, A16, A16, ALU.mult)
            dve.drain()
            dve.tensor_reduce(rs16, B16, AX.X, ALU.add)
            dve.drain()
            dve.tensor_scalar(rs16, rs16, 1.0 / 16, 1e-5, ALU.mult, ALU.add)
            dve.drain().then_inc(root_go, 1)
            roots["asked"] += 1
            dve.wait_ge(root, roots["asked"])
            dve.reciprocal(rs16, rs16)
            dve.drain()
            dve.tensor_tensor(A16, A16, rep16(rs16), ALU.mult)
            dve.drain()
            dve.tensor_tensor(A16, A16, over_blocks(SMALL2[:, 1, :]), ALU.mult)
            dve.drain()
            dve.tensor_tensor(A16, A16, over_blocks(SMALL2[:, 2, :]), ALU.add)
            dve.drain()
            dve.tensor_reduce(v4(s4), A16.rearrange("p b (h e) -> p b e h", h=4), AX.X, ALU.add)
            dve.drain()
            dve.tensor_scalar(s4, s4, 0.25, None, ALU.mult)
            dve.drain()
            top2(dve, v4(s4), NB, 4, v4(a4), v4(c4), m4.rearrange("p (k b) -> p k b", k=4), EDN[:, :, :])
            normalise_all(dve)
            dve.wait_ge(load_sem["experts1"], load_total["experts1"])
            experts1.vector(dve)

        @block_ctx.scalar
        def _(act):
            stats_scalar(act, RS[:, :])
            first.scalar(act)
            act.drain().then_inc(met, 1)
            act.wait_ge(met, MEETING * 1)
            es_gather.scalar(act, lambda g: ES0[:, bass.ds(g * 4 * QRT, 4 * QRT)].rearrange("p (t w) -> p t w", w=4))
            act.drain().then_inc(es_kept, 1)
            serve_exp(act, weights0.es)
            act.drain().then_inc(met, 1)
            act.wait_ge(met, MEETING * 2)
            sums0.scalar(act)
            act.drain().then_inc(met, 1)
            act.wait_ge(met, MEETING * 3)
            stats_scalar(act, RS[:, :])
            serve_exp(act, LOGITS)
            serve_exp(act, LOGITS)
            serve_exp(act, DIFF0)
            experts0.scalar(act)
            stats_scalar(act, RS[:, :])
            stats_scalar(act, RS[:, :])
            enter.scalar(act)
            act.drain().then_inc(met, 1)
            act.wait_ge(met, MEETING * 4)
            for l in range(3):
                hops[l].scalar(act)
                mixes[l].scalar(act)
                if l < 2:
                    act.drain().then_inc(met, 1)
                    act.wait_ge(met, MEETING * (5 + l))
            leave.scalar(act)
            stats_scalar(act, RS[:, :])
            project2.scalar(act)
            act.drain().then_inc(met, 1)
            act.wait_ge(met, MEETING * 7)
            g1_gather.scalar(act, lambda g: ar(ACC0, 1152 * 20)[:, bass.ds(g * 20 * QRT, 20 * QRT)].rearrange("p (t w) -> p t w", w=20))
            act.drain().then_inc(es_kept, 1)
            serve_exp(act, weights2.es)
            act.drain().then_inc(met, 1)
            act.wait_ge(met, MEETING * 8)
            stats_scalar(act, ar(27450, NB))
            serve_exp(act, DIFF1)
            experts1.scalar(act)

        @block_ctx.tensor
        def _(pe):
            first.tensor(pe)
            sort_tensor(pe, 0)
            count_tensor(pe, 0)
            tiles_tensor(pe, 0)
            pe.drain().then_inc(met, 1)
            pe.wait_ge(met, MEETING * 1)
            spread0.tensor(pe)
            for g in (1, 2):
                sort_tensor(pe, g)
                count_tensor(pe, g)
            for g in (1, 2):
                tiles_tensor(pe, g)
            weights0.tensor(pe)
            pe.drain().then_inc(met, 1)
            pe.wait_ge(met, MEETING * 2)
            sums0.tensor(pe)
            pe.drain().then_inc(met, 1)
            pe.wait_ge(met, MEETING * 3)
            pe.wait_ge(asked, nth("questions"))
            for k in range(2):
                m = pe.matmul(PB[2][:, k:k + 1], ar(W0 + 10000, D)[:, k * P:(k + 1) * P], ONES[:, 0:1], start=True, stop=True)
            m.then_inc(answered, 1)
            pe.wait_ge(asked, nth("questions"))
            for k in range(2):
                m = pe.matmul(PB[3][:, 0:8], ar(W0 + 10300, 2 * P)[:, k * P:(k + 1) * P], WRT[:, k, :], start=(k == 0), stop=(k == 1))
            m.then_inc(answered, 1)
            experts0.tensor(pe)
            enter.tensor(pe)
            pe.drain().then_inc(met, 1)
            pe.wait_ge(met, MEETING * 4)
            for l in range(3):
                hops[l].tensor(pe)
                mixes[l].tensor(pe)
                if l < 2:
                    pe.drain().then_inc(met, 1)
                    pe.wait_ge(met, MEETING * (5 + l))
            leave.tensor(pe)
            project2.tensor(pe)
            pe.drain().then_inc(met, 1)
            pe.wait_ge(met, MEETING * 7)
            spread2.tensor(pe)
            weights2.tensor(pe)
            pe.wait_ge(weighted, 1)
            sums2.tensor(pe, ZEROS)
            pe.drain().then_inc(met, 1)
            pe.wait_ge(met, MEETING * 8)
            experts1.tensor(pe)

        @block_ctx.gpsimd
        def _(pool):
            pool.iota(LOOPS[:, :], [[1, 50]], base=0, channel_multiplier=50)
            pool.drain().then_inc(loops_ready, 1)
            rows_pool(pool, 0)
            pool.drain().then_inc(met, 1)
            pool.wait_ge(met, MEETING * 1)
            es_gather.pool(pool)
            rows_pool(pool, 1)
            rows_pool(pool, 2)
            pool.drain().then_inc(met, 1)
            pool.wait_ge(met, MEETING * 2)
            sums0.pool(pool)
            pool.drain().then_inc(met, 1)
            pool.wait_ge(met, MEETING * 3)
            pool.drain().then_inc(met, 1)
            pool.wait_ge(met, MEETING * 4)
            for l in range(3):
                hops[l].pool(pool)
                if l < 2:
                    pool.drain().then_inc(met, 1)
                    pool.wait_ge(met, MEETING * (5 + l))
            pool.drain().then_inc(met, 1)
            pool.wait_ge(met, MEETING * 7)
            g1_gather.pool(pool)
            pool.drain().then_inc(met, 1)
            pool.wait_ge(met, MEETING * 8)

        @block_ctx.sync
        def _(sp):
            load(sp, "start")
            load(sp, "x")
            sp.wait_ge(zeroed, 1)
            load(sp, "x_end")
            chunk_stores(sp, tabD, Hv, D, first.taken, stored, 0)
            sp.dma_start(esD.rearrange("(b p) h -> p b h", p=P), ESN[:, :, :]).then_inc(stored, 16)
            sp.wait_ge(stored, 96)
            sort_sync(sp, 0)
            count_sync(sp, 0)
            tiles_sync(sp, 0)
            load(sp, "graph0")
            load(sp, "dst0")
            sp.wait_ge(load_sem["graph0"], load_total["graph0"])
            sp.wait_ge(load_sem["dst0"], load_total["dst0"])
            sp.drain().then_inc(met, 1)
            sp.wait_ge(met, MEETING * 1)
            spread0.sync(sp)
            for g in (1, 2):
                sort_sync(sp, g)
                count_sync(sp, g)
            for g in (1, 2):
                tiles_sync(sp, g)
            sp.drain().then_inc(met, 1)
            sp.wait_ge(met, MEETING * 2)
            sp.drain().then_inc(met, 1)
            sp.wait_ge(met, MEETING * 3)
            load(sp, "router")
            load(sp, "sage")
            load(sp, "graph1")
            load(sp, "bias0")
            sp.wait_ge(chosen, 1)
            for e in range(2):
                v = sp.value_load(IDSI[0:1, e:e + 1], min_val=0, max_val=7)
                one = lambda a: a[bass.ds(v, 1)]
                sp.dma_start(w1(e), one(A["L0_ffn_W1"]).rearrange("o (k p) n -> p (o k) n", p=P)).then_inc(chosen_in, 16)
                sp.dma_start(w2(e), one(A["L0_ffn_W2"]).rearrange("o (k p) n -> p (o k) n", p=P)).then_inc(chosen_in, 16)
                sp.dma_start(b1(e), one(A["L0_ffn_b1"]).rearrange("o (f p) -> p (o f)", p=P), allow_slow_non_contiguous=True).then_inc(chosen_in, 16)
                sp.dma_start(b2(e), one(A["L0_ffn_b2"]).to_broadcast([P, D])).then_inc(chosen_in, 16)
            sp.wait_ge(load_sem["graph1"], load_total["graph1"])
            chunk_stores(sp, tabD, Hv, D, enter.taken, stored, 96)
            load(sp, "bias1")
            sp.wait_ge(load_sem["bias1"], load_total["bias1"])
            sp.drain().then_inc(met, 1)
            sp.wait_ge(met, MEETING * 4)
            for l in range(2):
                chunk_stores(sp, tabD, Hv, D, mixes[l].taken, stored, 176 + 80 * l)
                load(sp, f"bias{l + 2}")
                sp.wait_ge(load_sem[f"bias{l + 2}"], load_total[f"bias{l + 2}"])
                sp.drain().then_inc(met, 1)
                sp.wait_ge(met, MEETING * (5 + l))
            sp.wait_ge(sp_go, nth("goes"))
            load(sp, "bias4")
            load(sp, "graph2")
            sp.wait_ge(sp_go, nth("goes"))
            load(sp, "gat1")
            chunk_stores(sp, t20D, T20, 20, project2.taken, stored, 336)
            sp.wait_ge(load_sem["graph2"], load_total["graph2"])
            sp.drain().then_inc(met, 1)
            sp.wait_ge(met, MEETING * 7)
            load(sp, "dst2")
            spread2.sync(sp)
            sp.drain().then_inc(met, 1)
            sp.wait_ge(met, MEETING * 8)
            load(sp, "small2")
            load(sp, "experts1")
            for c in range(7):
                last_pair = -(-7 * (c + 1) // 2)
                sp.wait_ge(experts1.done, min(last_pair, NB // 2))
                if c < 6:
                    dst = out[7 * c * P:7 * (c + 1) * P, :].rearrange("(b p) d -> p b d", p=P)
                    sp.dma_start(dst, X[:, 7 * c:7 * c + 7, :]).then_inc(finished, 16)
            dst = out[42 * P:48 * P, :].rearrange("(b p) d -> p b d", p=P)
            sp.dma_start(dst, X[:, 42:48, :]).then_inc(finished, 16)
            sp.dma_start(out[48 * P:N, :], X[0:last, 48, :]).then_inc(finished, 16)
            sp.wait_ge(finished, 16 * 8)


_INS = ["x", "src", "dst", "L0_gnn_W", "L0_gnn_a_src", "L0_gnn_a_dst", "L0_ffn_Wr", "L0_ffn_br", "L0_ffn_W1",
        "L0_ffn_b1", "L0_ffn_W2", "L0_ffn_b2", "L0_ffn_gamma", "L0_ffn_beta", "L1_gnn_W_in", "L1_gnn_b_in",
        "L1_gnn_W_agg", "L1_gnn_W_self", "L1_gnn_b_hid", "L1_gnn_W_out", "L1_gnn_b_out", "L1_ffn_W_gat",
        "L1_ffn_att_src", "L1_ffn_att_dst", "L1_ffn_b_gat", "L1_ffn_ln_gamma", "L1_ffn_ln_beta", "L1_ffn_W1",
        "L1_ffn_b1", "L1_ffn_W2", "L1_ffn_b2", "L1_ffn_edge_index"]


def kernel(**inputs):
    import concourse.bacc as _bacc
    from concourse.bass_utils import run_bass_kernel_spmd as _run

    nc = _bacc.Bacc("TRN2", target_bir_lowering=False, num_devices=1)
    arrays, aps = {}, {}
    consts, where, flips = host_constants()
    for name in _INS + ["consts", "flips"]:
        a = {"consts": consts, "flips": flips}.get(name)
        a = np.ascontiguousarray(inputs[name] if a is None else a)
        arrays[f"in_{name}"] = a
        aps[name] = nc.dram_tensor(f"in_{name}", a.shape, mybir.dt.from_np(a.dtype), kind="ExternalInput").ap()
    out = nc.dram_tensor("out_x", (N, D), F32, kind="ExternalOutput").ap()
    build_program(nc, aps, out, aps["consts"], aps["flips"], where)
    r = _run(nc, [arrays], core_ids=[0])
    return r.results[0]["out_x"]
```

```python
from contextlib import ExitStack

import numpy as np

import concourse.bass as bass
from concourse import mybir

ALU = mybir.AluOpType
ACT = mybir.ActivationFunctionType
AX = mybir.AxisListType
F32 = mybir.dt.float32
BF16 = mybir.dt.bfloat16
I32 = mybir.dt.int32
U8 = mybir.dt.uint8

P = 128
N = 6250
D = 256
EB = -(-N // P)
NB = EB + 1
NP = NB * P
ACCW = D + 4
IDBITS = 13
IDMASK = (1 << IDBITS) - 1
KEYTOP = 0x40000000
BIG = 1.0e30
GRP = 8
QRT = 4
RING = 4 * QRT

GRAPHS = [dict(c=1024, tq=7, t=880), dict(c=1024, tq=7, t=880), dict(c=2048, tq=9, t=1136)]
for _g in GRAPHS:
    _g["rows"] = _g["c"]
    assert _g["tq"] * P >= _g["t"] and _g["t"] % (2 * GRP) == 0


def host_constants():
    p = np.arange(P)
    sign = lambda r: 1.0 - 2.0 * ((p >> r) & 1)
    flips = np.concatenate([sign(r - 1) * sign(r) for r in range(1, 8)])
    every = lambda row: np.broadcast_to(row, (P, len(row)))
    parts = [("ident", np.eye(P)), ("ones", np.ones((P, P))), ("iota", every(p)), ("pcol", p[:, None]),
             ("sign0", sign(0)[:, None])]
    for tq in (7, 9):
        parts.append((f"tile{tq}", p[:, None] * tq + np.arange(tq)[None, :]))
    at, where = 0, {}
    for name, a in parts:
        where[name] = (at, at + a.shape[1])
        at += a.shape[1]
    return np.concatenate([np.asarray(a, np.float32) for _, a in parts], 1), where, every(flips).astype(np.float32)


def build_program(nc, A, out, consts, flips, where):
    with ExitStack() as ctx:
        def sb(name, shape, dt=F32):
            return ctx.enter_context(nc.sbuf_tensor(name, shape, dt))

        def sem(name):
            return ctx.enter_context(nc.semaphore(name))

        def dram(name, shape, dt=F32):
            return nc.dram_tensor(name, shape, dt, kind="Internal").ap()

        ncon = consts.shape[1]
        CON = sb("CON", [P, ncon])
        con = lambda name: CON[:, where[name][0]:where[name][1]]
        IDENT, ONES, IOTA, PCOL = con("ident"), con("ones"), con("iota"), con("pcol")
        X = sb("X", [P, NB, D])
        ARENA = sb("ARENA", [P, 36104])
        ACC0, H0, WS0, GR0, S0 = 0, 13000, 25800, 29896, 34056
        ar = lambda a, n: ARENA[:, a:a + n]
        ACCv = ar(ACC0, NB * ACCW).rearrange("p (b w) -> p b w", w=ACCW)
        Hv = ar(H0, NB * D).rearrange("p (b d) -> p b d", d=D)
        Qv = ar(S0, RING * P).rearrange("p (h t n) -> p h t n", h=4, t=QRT)
        RELE = sb("RELE", [P, 1152])
        SRCE = sb("SRCE", [P, 1160])
        srce_i = SRCE[:, 0:1152].bitcast(I32)
        BT = sb("BT", [1, 1152], U8)
        IDX = sb("IDX", [P, 4, QRT], I32)
        EDN = sb("EDN", [P, NB, 4])
        ESN = sb("ESN", [P, NB, 4])
        SM = ar(ACC0 + 11000, 660)
        FLIPS = ar(GR0 + 2048, 7 * P)
        LOOPS = sb("LOOPS", [125, 50], I32)
        loops_ready = sem("loops_ready")
        PSUM = ctx.enter_context(nc.psum_tensor("PSUM", [P, 8 * 512], F32))
        PB = [PSUM[:, 512 * i:512 * (i + 1)] for i in range(8)]

        tabD = dram("tabD", (NP, D))
        esD = dram("esD", (NP, 4))
        t20D = dram("t20D", (NP, 20))
        keysD = [dram(f"keysD{g}", (G["rows"], P), I32) for g, G in enumerate(GRAPHS)]
        relD = [dram(f"relD{g}", (1, G["tq"] * P * P), BF16) for g, G in enumerate(GRAPHS)]
        releD = [dram(f"releD{g}", (P, G["tq"] * P)) for g, G in enumerate(GRAPHS)]
        srceD = [dram(f"srceD{g}", (P, G["tq"] * P), I32) for g, G in enumerate(GRAPHS)]
        dstD = [dram(f"dstD{g}", (P, G["tq"] * P)) for g, G in enumerate(GRAPHS)]
        btD = [dram(f"btD{g}", (P, G["tq"]), U8) for g, G in enumerate(GRAPHS)]

        met = sem("met")
        asked, answered = sem("asked"), sem("answered")
        sp_go = sem("sp_go")
        MEETING = 5
        counts = {}

        def nth(name):
            counts[name] = counts.get(name, 0) + 1
            return counts[name]


        def pairs_of(eng, n, body, start=0):
            for h in (0, 1):
                body(start, h, start == 0)
            with eng.Fori(start + 1, n) as i:
                for h in (0, 1):
                    body(i, h, False)

        sp_key = sem("sp_key")
        key_room = sem("key_room")
        KA, KB = ar(WS0, 2048), ar(WS0 + 2048, 2048)

        def key_buffers(g):
            C = GRAPHS[g]["c"]
            return KA[:, 0:C].bitcast(I32), KB[:, 0:C].bitcast(I32)

        def key_sources(g):
            if g == 0:
                return A["dst"], A["src"]
            if g == 1:
                return A["src"], A["dst"]
            return A["L1_ffn_edge_index"][1, :], A["L1_ffn_edge_index"][0, :]

        def sort_sync(sp, g):
            dsts, srcs = key_sources(g)
            n = dsts.shape[0]
            rows = 125 if g < 2 else P
            sp.wait_ge(key_room, g + 1)
            for buf, a in zip(key_buffers(g), (dsts, srcs)):
                sp.dma_start(buf[0:rows, 0:n // rows], a.rearrange("(p c) -> p c", p=rows)).then_inc(sp_key, 16)

        def sort_vector(dve, g):
            C = GRAPHS[g]["c"]
            dst_i, src_i = key_buffers(g)
            dve.memset(dst_i, IDMASK)
            dve.memset(src_i, IDMASK)
            dve.drain().then_inc(key_room, 1)
            if g == 2:
                dve.wait_ge(loops_ready, 1)
                dve.tensor_copy(dst_i[0:125, 1024:1074], LOOPS[:, :])
                dve.tensor_copy(src_i[0:125, 1024:1074], LOOPS[:, :])
                dve.drain()
            dve.wait_ge(sp_key, 32 * (g + 1))
            dve.scalar_tensor_tensor(out=dst_i, in0=dst_i, scalar=IDBITS, in1=src_i,
                                     op0=ALU.logical_shift_left, op1=ALU.bitwise_or)
            dve.drain()
            dve.tensor_scalar(dst_i, dst_i, KEYTOP, None, ALU.bitwise_or)
            dve.drain()
            bufs = [KA[:, 0:C], KB[:, 0:C]]
            dve.tensor_scalar(bufs[1], bufs[0], con("sign0"), None, ALU.mult)
            dve.drain()
            cur = 1

            def exchange(lo, hi, olo, ohi):
                dve.tensor_tensor(olo, lo, hi, ALU.min)
                dve.tensor_tensor(ohi, lo, hi, ALU.max)
                dve.drain()

            def step(s):
                nonlocal cur
                v = bufs[cur].rearrange("p (n two s) -> p n two s", two=2, s=s)
                w = bufs[1 - cur].rearrange("p (n two s) -> p n two s", two=2, s=s)
                exchange(v[:, :, 0, :], v[:, :, 1, :], w[:, :, 0, :], w[:, :, 1, :])
                cur = 1 - cur

            def mirror(size):
                nonlocal cur
                v = bufs[cur].rearrange("p (n s) -> p n s", s=size)
                w = bufs[1 - cur].rearrange("p (n s) -> p n s", s=size)
                h = size // 2
                exchange(v[:, :, 0:h], v[:, :, size - 1:h - 1:-1] , w[:, :, 0:h], w[:, :, size - 1:h - 1:-1])
                cur = 1 - cur

            size = 2
            while size <= C:
                if size == 2:
                    step(1)
                else:
                    mirror(size)
                    s = size // 4
                    while s >= 1:
                        step(s)
                        s //= 2
                size *= 2
            for r in range(1, 8):
                turned[g].append(cur)
                dve.drain().then_inc(asked, 1)
                dve.wait_ge(answered, nth("answers"))
                flip = FLIPS[:, (r - 1) * P:r * P]
                for k in range(C // 512):
                    dve.tensor_tensor(bufs[1 - cur][:, k * 512:(k + 1) * 512].rearrange("p (a b) -> p a b", b=P),
                                      PB[4 + k][:, :].rearrange("p (a b) -> p a b", b=P),
                                      flip.rearrange("p (a b) -> p a b", a=1).to_broadcast([P, 4, P]), ALU.mult)
                dve.drain()
                cur = 1 - cur
                s = 1 << (r - 1)
                while s >= 1:
                    step(s)
                    s //= 2
                turned[g].append(cur)
                dve.drain().then_inc(asked, 1)
                dve.wait_ge(answered, nth("answers"))
                for k in range(C // 512):
                    dve.tensor_copy(bufs[1 - cur][:, k * 512:(k + 1) * 512], PB[4 + k][:, :])
                dve.drain()
                cur = 1 - cur
                s = C // 2
                while s >= 1:
                    step(s)
                    s //= 2
            turned[g].append(cur)
            return cur

        def sort_tensor(pe, g):
            C = GRAPHS[g]["c"]
            bufs = [KA, KB]
            for cur in turned[g][:-1]:
                pe.wait_ge(asked, nth("questions"))
                for k in range(C // P):
                    t = pe.transpose(PB[4 + k // 4][:, (k % 4) * P:(k % 4 + 1) * P], bufs[cur][:, k * P:(k + 1) * P], IDENT)
                t.then_inc(answered, 1)

        turned = {g: [] for g in range(3)}

        start_f, nt_f, cum_f, doff_f = SM[:, 0:50], SM[:, 50:100], SM[:, 100:150], SM[:, 150:200]
        re_f = SM[:, 250:300]
        off_f, bt_f, junk_f, rs_f = SM[:, 300:309], SM[:, 310:319], SM[:, 320:370], SM[:, 370:420]
        ti = sb("ti", [P, 50], I32)
        rowi = [sb(f"rowi{g}", [P, 9], I32) for g in range(3)]
        bt128 = [sb(f"bt128_{g}", [P, 9]) for g in range(3)]
        bt8 = sb("bt8", [P, 9], U8)
        TT0 = ACC0
        RAW = ar(TT0, 1152).bitcast(I32)
        TMPI = ar(TT0 + 1152, 1152).bitcast(I32)
        SRCF, DSTF, RELF = ar(TT0 + 2304, 1152), ar(TT0 + 3456, 1152), ar(TT0 + 4608, 1152)
        RELB = ar(TT0 + 5760, 576).bitcast(BF16)
        TREL = ar(TT0 + 6336, 1152)
        TSRC = ar(TT0 + 7488, 1152).bitcast(I32)
        rows_ready = sem("rows_ready")
        keys_kept = sem("keys_kept")
        raw_in = sem("raw_in")
        rows_before = [sum(G["tq"] for G in GRAPHS[:g]) for g in range(3)]
        raw_free = sem("raw_free")
        keep_done = sem("keep_done")

        BLOCKS = ar(TT0 + 6336, 1024).bitcast(BF16)
        began, ended, inside = SM[:, 450:499], SM[:, 500:549], SM[:, 550:575].bitcast(BF16)[:, 0:EB]
        ends, rows_n, parts_n, total = SM[:, 576:578], SM[0:EB, 578:580], SM[0:EB, 580:584], SM[0:EB, 584:585]
        diagonal = SM[0:EB, 600:650]
        limit = SM[0:EB, 650:651]

        def count_vector(dve, g, cur):
            G = GRAPHS[g]
            C, tq = G["c"], G["tq"]
            keys, free = (KA, KB) if cur == 0 else (KB, KA)
            dve.drain().then_inc(sp_go, 1)
            block_i, block_b = free[:, 0:C].bitcast(I32), BLOCKS[:, 0:C]
            dve.tensor_scalar(block_i, keys[:, 0:C].bitcast(I32), IDBITS + 7, 63, ALU.logical_shift_right, ALU.bitwise_and)
            dve.drain()
            dve.tensor_scalar(limit, PCOL[0:EB, :], 1.0, None, ALU.add)
            dve.tensor_copy(block_b, block_i)
            dve.tensor_copy(ends[:, 0:1], block_i[:, 0:1])
            dve.tensor_copy(ends[:, 1:2], block_i[:, C - 1:C])
            dve.drain()
            dve.tensor_scalar(began, IOTA[:, 1:NB], ends[:, 0:1], None, ALU.is_gt)
            dve.tensor_scalar(ended, IOTA[:, 1:NB], ends[:, 1:2], None, ALU.is_gt)
            dve.drain()
            dve.tensor_tensor(began, began, ended, ALU.subtract)
            dve.drain()
            dve.tensor_copy(inside, began)
            dve.drain().then_inc(asked, 1)
            dve.wait_ge(answered, nth("answers"))
            for k in range(C // 512):
                dve.tensor_scalar(free[0:EB, 512 * k:512 * (k + 1)], PB[4 + k][0:EB, :], limit, None, ALU.is_lt, ALU.add,
                                  accum_out=parts_n[:, k:k + 1])
            dve.tensor_copy(rows_n, PB[2][0:EB, 0:2])
            dve.drain()
            dve.tensor_reduce(total, parts_n[:, 0:C // 512], AX.X, ALU.add)
            dve.drain()
            dve.tensor_scalar(total, total, rows_n[:, 1:2], None, ALU.mult)
            dve.drain()
            dve.scalar_tensor_tensor(out=total, in0=rows_n[:, 0:1], scalar=float(C), in1=total, op0=ALU.mult, op1=ALU.add)
            dve.drain()
            dve.memset(diagonal[:, 0:1], 0.0)
            dve.tensor_scalar(diagonal[:, 1:NB], IDENT[0:EB, 0:EB], total, None, ALU.mult)
            dve.drain().then_inc(asked, 1)
            dve.wait_ge(answered, nth("answers"))
            dve.tensor_copy(start_f, PB[2][:, 0:50])
            dve.tensor_scalar(re_f, PB[2][:, 0:50], float(P - 1), None, ALU.add)
            dve.drain()
            dve.tensor_copy(ti[:, :], start_f)
            dve.drain()
            dve.tensor_scalar(ti[:, :], ti[:, :], 7, None, ALU.logical_shift_right)
            dve.drain()
            dve.tensor_copy(rs_f, ti[:, :])
            dve.drain()
            dve.tensor_copy(ti[:, :], re_f)
            dve.drain()
            dve.tensor_scalar(ti[:, :], ti[:, :], 7, None, ALU.logical_shift_right)
            dve.drain()
            dve.tensor_copy(re_f, ti[:, :])
            dve.drain()
            dve.tensor_tensor(nt_f[:, 0:EB], re_f[:, 1:NB], rs_f[:, 0:EB], ALU.subtract)
            dve.tensor_tensor(doff_f[:, 0:EB], rs_f[:, 1:NB], rs_f[:, 0:EB], ALU.subtract)
            dve.drain()
            dve.tensor_tensor(doff_f[:, 0:EB], doff_f[:, 0:EB], nt_f[:, 0:EB], ALU.subtract)
            dve.tensor_tensor_scan(cum_f[:, 0:EB], ONES[:, 0:EB], nt_f[:, 0:EB], 0.0, ALU.mult, ALU.add)
            dve.drain()
            tile = con(f"tile{tq}")
            for q in range(tq):
                dve.scalar_tensor_tensor(out=junk_f[:, 0:EB], in0=cum_f[:, 0:EB], scalar=tile[:, q:q + 1], in1=doff_f[:, 0:EB],
                                         op0=ALU.is_le, op1=ALU.mult, accum_out=off_f[:, q:q + 1])
                dve.drain()
                dve.scalar_tensor_tensor(out=junk_f[:, 0:EB], in0=cum_f[:, 0:EB], scalar=tile[:, q:q + 1], in1=ONES[:, 0:EB],
                                         op0=ALU.is_le, op1=ALU.mult, accum_out=bt_f[:, q:q + 1])
                dve.drain()
            if g == 2:
                dve.tensor_scalar(LAST[:, :], cum_f[0:1, 0:EB], -1.0, None, ALU.add)
            dve.tensor_tensor(off_f[:, 0:tq], off_f[:, 0:tq], tile, ALU.add)
            dve.drain()
            dve.tensor_scalar(rowi[g][:, 0:tq], off_f[:, 0:tq], float(G["rows"] - 1), None, ALU.min)
            dve.tensor_scalar(bt128[g][:, 0:tq], bt_f[:, 0:tq], float(P), None, ALU.mult)
            dve.tensor_copy(bt8[:, 0:tq], bt_f[:, 0:tq])
            dve.drain().then_inc(rows_ready, 1)
            dve.wait_ge(keys_kept, 32 * (g + 1))

        def count_tensor(pe, g):
            C = GRAPHS[g]["c"]
            pe.wait_ge(asked, nth("questions"))
            pe.matmul(PB[2][0:EB, 0:1], ended, ONES[:, 0:1], start=True, stop=True)
            pe.matmul(PB[2][0:EB, 1:2], began, ONES[:, 0:1], start=True, stop=True)
            for k in range(C // 512):
                m = pe.matmul(PB[4 + k][0:EB, :], inside, BLOCKS[:, 512 * k:512 * (k + 1)], start=True, stop=True)
            m.then_inc(answered, 1)
            pe.wait_ge(asked, nth("questions"))
            pe.matmul(PB[2][:, 0:NB], ONES[0:EB, :], diagonal, start=True, stop=True).then_inc(answered, 1)

        def count_sync(sp, g):
            C, tq = GRAPHS[g]["c"], GRAPHS[g]["tq"]
            keys = (KA, KB)[turned[g][-1]]
            sp.wait_ge(sp_go, nth("goes"))
            sp.dma_start(keysD[g].rearrange("(p a) b -> p (a b)", p=P), keys[:, 0:C].bitcast(I32)).then_inc(keys_kept, 16)
            sp.wait_ge(rows_ready, g + 1)
            sp.dma_start(btD[g], bt8[:, 0:tq]).then_inc(keys_kept, 16)

        def rows_pool(pool, g):
            tq = GRAPHS[g]["tq"]
            pool.wait_ge(rows_ready, g + 1)
            pool.wait_ge(keys_kept, 32 * (g + 1))
            if g:
                pool.wait_ge(raw_free, g)
            for q in range(tq):
                pool.indirect_dma_start(RAW[:, q * P:(q + 1) * P], None, keysD[g],
                                        bass.IndirectOffsetOnAxis(rowi[g][:, q:q + 1], 0)).then_inc(raw_in, 16)

        def tiles_vector(dve, g):
            tq = GRAPHS[g]["tq"]
            L = tq * P
            dve.wait_ge(raw_in, 16 * (rows_before[g] + tq))
            dve.tensor_scalar(TMPI[:, 0:L], RAW[:, 0:L], IDMASK, None, ALU.bitwise_and)
            dve.drain()
            dve.tensor_scalar(SRCF[:, 0:L], TMPI[:, 0:L], float(N - 1), None, ALU.min)
            dve.drain()
            dve.tensor_scalar(TMPI[:, 0:L], RAW[:, 0:L], IDBITS, IDMASK, ALU.logical_shift_right, ALU.bitwise_and)
            dve.drain()
            dve.tensor_copy(DSTF[:, 0:L], TMPI[:, 0:L])
            dve.drain().then_inc(raw_free, 1)
            for q in range(tq):
                dve.tensor_scalar(RELF[:, q * P:(q + 1) * P], DSTF[:, q * P:(q + 1) * P], bt128[g][:, q:q + 1], None, ALU.subtract)
            dve.drain()
            dve.tensor_scalar(RELF[:, 0:L], RELF[:, 0:L], -1.0, float(P), ALU.max, ALU.min)
            dve.drain()
            dve.tensor_copy(RELB[:, 0:L], RELF[:, 0:L])
            for n0 in range(0, tq, 4):
                n = min(4, tq - n0)
                dve.drain().then_inc(asked, 1)
                dve.wait_ge(answered, nth("answers"))
                for bank, to in ((PB[2], TREL), (PB[3], TSRC)):
                    v = to[:, 0:L].rearrange("e (p q) -> e q p", q=tq)
                    dve.tensor_copy(v[:, n0:n0 + n, :], bank[:, 0:n * P].rearrange("e (q p) -> e q p", p=P))
            dve.drain().then_inc(sp_go, 1)
            dve.wait_ge(keep_done, 64 * (g + 1))

        def tiles_tensor(pe, g):
            tq = GRAPHS[g]["tq"]
            for n0 in range(0, tq, 4):
                pe.wait_ge(asked, nth("questions"))
                for q in range(n0, min(n0 + 4, tq)):
                    pe.transpose(PB[2][:, (q - n0) * P:(q - n0 + 1) * P], RELF[:, q * P:(q + 1) * P], IDENT)
                    t = pe.transpose(PB[3][:, (q - n0) * P:(q - n0 + 1) * P], SRCF[:, q * P:(q + 1) * P], IDENT)
                t.then_inc(answered, 1)

        def tiles_sync(sp, g):
            tq = GRAPHS[g]["tq"]
            L = tq * P
            sp.wait_ge(sp_go, nth("goes"))
            sp.dma_start(relD[g].rearrange("o (p a) -> (o p) a", p=P), RELB[:, 0:L]).then_inc(keep_done, 16)
            sp.dma_start(dstD[g], DSTF[:, 0:L]).then_inc(keep_done, 16)
            sp.dma_start(releD[g], TREL[:, 0:L]).then_inc(keep_done, 16)
            sp.dma_start(srceD[g], TSRC[:, 0:L]).then_inc(keep_done, 16)
            sp.wait_ge(keep_done, 64 * (g + 1))

        def graph_loads(g):
            L = GRAPHS[g]["tq"] * P
            return [(RELE[:, 0:L], releD[g]), (srce_i[:, 0:L], srceD[g]),
                    (BT[:, 0:L], btD[g].rearrange("p (o q) -> o (p q)", o=1))]

        MV = sb("MV", [P, NB, 2])
        RS = sb("RS", [P, NB])
        root = sem("root")
        SB = 10
        STATS = sb("STATS", [P, SB, 6])
        MVJ = sb("MVJ", [P, SB, 2])
        roots = dict(asked=0, taken=0)
        root_go = sem("root_go")

        def stats_vector(dve, V, before=None):
            with dve.Fori(0, NB // SB) as i:
                if before:
                    for j in range(SB):
                        before(SB * i + j)
                    dve.drain()
                for j in range(SB):
                    dve.bn_stats(STATS[:, j, :], V[:, bass.ds(SB * i + j, 1), :].rearrange("p a d -> p (a d)"))
                dve.drain()
                for j in range(SB):
                    dve.bn_aggr(MVJ[:, j, :], STATS[:, j, :])
                dve.drain()
                dve.tensor_copy(MV[:, bass.ds(SB * i, SB), :], MVJ[:, :, :])
            dve.drain()
            deviations_vector(dve)

        def deviations_vector(dve):
            dve.tensor_scalar(RS[:, :], MV[:, :, 1], 1e-5, None, ALU.add)
            dve.drain().then_inc(root_go, 1)
            roots["asked"] += 1
            dve.wait_ge(root, roots["asked"])
            dve.reciprocal(RS[:, :], RS[:, :])
            dve.drain()

        def stats_scalar(act, v):
            roots["taken"] += 1
            act.wait_ge(root_go, roots["taken"])
            act.activation(v, v, ACT.Sqrt).then_inc(root, 1)

        def normalise(dve, to, V, b):
            dve.tensor_scalar(to, V[:, bass.ds(b, 1), :].rearrange("p a d -> p (a d)"),
                              MV[:, bass.ds(b, 1), 0:1].rearrange("p a d -> p (a d)"), RS[:, bass.ds(b, 1)],
                              ALU.subtract, ALU.mult)

        IN = ar(GR0, 1024).rearrange("p (j c) -> p j c", j=2)
        XT = ar(GR0 + 1024, 1024).rearrange("p (j c) -> p j c", j=2)

        class Dense:

            def __init__(self, name, chunks, weight, n, keep=None):
                self.keep = keep
                self.chunks, self.weight, self.n = chunks, weight, n
                self.rows_in, self.turned, self.cols_in, self.multiplied, self.taken = (
                    sem(f"{name}_{x}") for x in ("rows_in", "turned", "cols_in", "multiplied", "taken"))

            def each(self, eng, body):
                for j in range(2):
                    body(j, j, True, False)
                with eng.Fori(1, NB // 2 - 1) as i:
                    for j in range(2):
                        body(2 * i + j, j, False, False)
                for j in range(2):
                    body(NB - 2 + j, j, False, True)

            def vector(self, dve, produce, take):
                def body(b, j, first, last):
                    if not last:
                        dve.wait_ge(self.turned, b + 1)
                        dve.wait_ge(self.turned, 1)
                        produce(dve, IN[:, j, :], b + 2)
                        dve.drain().then_inc(self.rows_in, 1)
                    if not self.keep:
                        dve.wait_ge(self.multiplied, b + 1)
                        dve.wait_ge(self.multiplied, 1)
                        take(dve, PB[2 + j], b)
                        dve.drain().then_inc(self.taken, 1)
                for j in range(2):
                    produce(dve, IN[:, j, :], j)
                    dve.drain().then_inc(self.rows_in, 1)
                self.each(dve, body)

            def scalar(self, act):
                def body(b, j, first, last):
                    act.wait_ge(self.turned, b + 1)
                    act.wait_ge(self.turned, 1)
                    if not first:
                        act.wait_ge(self.multiplied, b - 1)
                        act.wait_ge(self.multiplied, 1)
                    act.copy(XT[:, j, 0:P * self.chunks], PB[j][:, 0:P * self.chunks]).then_inc(self.cols_in, 1)
                    if self.keep and not (first and j == 0):
                        keep(b - 1, 1 - j)

                def keep(b, j):
                    act.wait_ge(self.multiplied, b + 1)
                    act.wait_ge(self.multiplied, 1)
                    act.nop(nofuse=True)
                    act.activation(block(self.keep[0], b), PB[2 + j][:, 0:self.n], self.keep[3]).then_inc(self.taken, 1)
                self.each(act, body)
                if self.keep:
                    keep(NB - 1, 1)

            def tensor(self, pe):
                def turn(b, j, first):
                    pe.wait_ge(self.rows_in, b + 1)
                    pe.wait_ge(self.rows_in, 1)
                    if not first:
                        pe.wait_ge(self.cols_in, b - 1)
                        pe.wait_ge(self.cols_in, 1)
                    for k in range(self.chunks):
                        t = pe.transpose(PB[j][:, k * P:(k + 1) * P], IN[:, j, k * P:(k + 1) * P], IDENT)
                    t.then_inc(self.turned, 1)

                def body(b, j, first, last):
                    if not (last and j == 1):
                        turn(b + 1, 1 - j, first and j == 0)
                    pe.wait_ge(self.cols_in, b + 1)
                    pe.wait_ge(self.cols_in, 1)
                    if not first:
                        pe.wait_ge(self.taken, b - 1)
                        pe.wait_ge(self.taken, 1)
                    for k in range(self.chunks):
                        m = pe.matmul(PB[2 + j][:, 0:self.n], XT[:, j, k * P:(k + 1) * P], self.weight(k),
                                      start=(k == 0), stop=(k == self.chunks - 1 and not self.keep))
                    if self.keep and self.keep[1]:
                        m = pe.matmul(PB[2 + j][:, 0:self.n], IDENT, block(self.keep[0], b), start=False, stop=not self.keep[2])
                    if self.keep and self.keep[2]:
                        m = pe.matmul(PB[2 + j][:, 0:self.n], IDENT[:, 0:1].to_broadcast([P, P]), BIASR[:, :], start=False, stop=True)
                    m.then_inc(self.multiplied, 1)
                turn(0, 0, True)
                self.each(pe, body)

        def quarters_of(eng, n, body):
            for h in range(4):
                body(0, h, True)
            with eng.Fori(1, n) as i:
                for h in range(4):
                    body(i, h, False)

        landed = [sem(f"landed{h}") for h in range(4)]
        told = sem("told")
        rounds = [0]

        class Gather:

            def __init__(self, name, g, table, width, pitch):
                self.steps = GRAPHS[g]["t"] // RING
                self.table, self.width = table, width
                self.ring = ar(GR0, RING * pitch).rearrange("p (h t w) -> p h t w", h=4, t=QRT)
                self.before = rounds[0]
                rounds[0] += self.steps

            def tell(self, act, i, h, first, used=None):
                if not first:
                    act.wait_ge(landed[h], 16 * QRT * (i + self.before))
                    act.wait_ge(landed[h], 16 * QRT * (self.before + 1))
                    if used:
                        used(i, h)
                act.copy(IDX[:, h, :], srce_i[:, bass.ds((4 * i + h) * QRT, QRT)])
                act.drain().then_inc(told, 1)

            def fetch(self, pool, i, h):
                pool.wait_ge(told, 4 * (self.before + i) + h + 1)
                if not isinstance(i, int):
                    pool.nop(nofuse=True)
                for j in range(QRT):
                    pool.indirect_dma_start(self.ring[:, h, j, 0:self.width], None, self.table,
                                            bass.IndirectOffsetOnAxis(IDX[:, h, j:j + 1], 0)).then_inc(landed[h], 16)

        class Kept(Gather):

            def pool(self, pool):
                quarters_of(pool, self.steps, lambda i, h, first: self.fetch(pool, i, h))

            def scalar(self, act, to):
                def used(i, h):
                    act.copy(to(4 * i + h - 4), self.ring[:, h, :, 0:self.width])
                quarters_of(act, self.steps, lambda i, h, first: self.tell(act, i, h, first, used))
                for h in range(4):
                    act.wait_ge(landed[h], 16 * QRT * (self.steps + self.before))
                    used(self.steps, h)

        class KeptBySync(Gather):

            def __init__(self, *args):
                super().__init__(*args)
                self.served = [sem(f"served{h}") for h in range(4)]

            def pool(self, pool):
                def body(i, h, first):
                    pool.wait_ge(self.served[h], 32 * i + 16)
                    if not isinstance(i, int):
                        pool.nop(nofuse=True)
                    for j in range(QRT):
                        pool.indirect_dma_start(self.ring[:, h, j, 0:self.width], None, self.table,
                                                bass.IndirectOffsetOnAxis(IDX[:, h, j:j + 1], 0)).then_inc(landed[h], 16)
                quarters_of(pool, self.steps, body)

            def sync(self, sp, to):
                def body(i, h, first):
                    if not first:
                        sp.wait_ge(landed[h], 16 * QRT * (i + self.before))
                        sp.wait_ge(landed[h], 16 * QRT * (self.before + 1))
                        sp.dma_start(to(4 * i + h - 4), self.ring[:, h, :, :].rearrange("p t w -> p (t w)")).then_inc(self.served[h], 16)
                    sp.dma_start(IDX[:, h, :], srce_i[:, bass.ds((4 * i + h) * QRT, QRT)]).then_inc(self.served[h], 16)
                quarters_of(sp, self.steps, body)
                for h in range(4):
                    sp.wait_ge(landed[h], 16 * QRT * (self.steps + self.before))
                    sp.dma_start(to(4 * self.steps + h - 4), self.ring[:, h, :, :].rearrange("p t w -> p (t w)")).then_inc(self.served[h], 16)

            def all_kept(self, dve):
                for h in range(4):
                    dve.wait_ge(self.served[h], 32 * self.steps)

        IOTAB = ar(GR0 + 1700, 64).bitcast(BF16)
        BT4 = BT[:, :].bitcast(I32)

        def blocks_of(eng, g, size):
            blocks = []
            for k in range(size // 4):
                word = eng.value_load(BT4[0:1, bass.ds(g * (size // 4) + k, 1)], min_val=0, max_val=(NB - 1) * 0x01010101)
                blocks += [((word >> (8 * j)) & 63).with_bounds(min_val=0, max_val=NB - 1) for j in range(4)]
            return blocks

        class SelfPart:

            def __init__(self, name, weight):
                self.weight = weight
                self.staged, self.turned, self.copied, self.multiplied, self.taken = (
                    sem(f"{name}_{x}") for x in ("staged", "turned", "copied", "multiplied", "taken"))
                self.T, self.U = Hv[:, NB - 1, :], X[:, NB - 1, :]

            def scalar(self, act, steps, tell):
                def step(i, take, copy, stage, first=False):
                    tell(i, 0, first)
                    if copy:
                        act.wait_ge(self.turned, i - 1)
                        act.wait_ge(self.turned, 1)
                        if take:
                            act.wait_ge(self.multiplied, i - 2)
                            act.wait_ge(self.multiplied, 1)
                        act.copy(self.U, PB[6][:, 0:D]).then_inc(self.copied, 1)
                    if take:
                        act.wait_ge(self.multiplied, i - 2)
                        act.wait_ge(self.multiplied, 1)
                        act.nop(nofuse=True)
                        act.copy(block(Hv, i - 3), PB[7][:, 0:D]).then_inc(self.taken, 1)
                    tell(i, 1, first)
                    if stage:
                        if copy:
                            act.wait_ge(self.turned, i - 1)
                            act.wait_ge(self.turned, 1)
                            act.nop(nofuse=True)
                        act.copy(self.T, block(Hv, i - 1)).then_inc(self.staged, 1)
                    tell(i, 2, first)
                    tell(i, 3, first)
                step(0, False, False, False, True)
                step(1, False, False, True)
                step(2, False, True, True)
                with act.Fori(3, EB + 1) as i:
                    step(i, True, True, True)
                step(EB + 1, True, True, False)
                step(EB + 2, True, False, False)
                with act.Fori(EB + 3, steps) as i:
                    step(i, False, False, False)
                act.drain()

            def tensor(self, pe, steps, products):
                def step(i, multiply, turn, first=False):
                    products(i, 0, first)
                    products(i, 1, first)
                    if multiply:
                        pe.wait_ge(self.copied, i)
                        pe.wait_ge(self.copied, 1)
                        if multiply > 1:
                            pe.wait_ge(self.taken, i - 1)
                            pe.wait_ge(self.taken, 1)
                        for k in range(2):
                            pe.matmul(PB[7][:, 0:D], self.U[:, k * P:(k + 1) * P], self.weight(k), start=(k == 0), stop=False)
                        pe.matmul(PB[7][:, 0:D], IDENT[:, 0:1].to_broadcast([P, P]), BIASR[:, :], start=False, stop=True
                                  ).then_inc(self.multiplied, 1)
                    products(i, 2, first)
                    if turn:
                        pe.wait_ge(self.staged, i + 1)
                        pe.wait_ge(self.staged, 1)
                        if multiply:
                            pe.wait_ge(self.copied, i)
                            pe.wait_ge(self.copied, 1)
                        for k in range(2):
                            t = pe.transpose(PB[6][:, k * P:(k + 1) * P], self.T[:, k * P:(k + 1) * P], IDENT)
                        t.then_inc(self.turned, 1)
                    products(i, 3, first)
                step(0, 0, True, True)
                step(1, 1, True)
                with pe.Fori(2, EB) as i:
                    step(i, 2, True)
                step(EB, 2, False)
                with pe.Fori(EB + 1, steps) as i:
                    step(i, 0, False)

        class Sums:

            def __init__(self, name, gather, width, weights=None, aside=None):
                self.aside = aside
                self.gather, self.width, self.weights = gather, width, weights
                self.steps = gather.steps
                self.ready_by_tile = 1 if weights is None else 2
                self.prepared, self.multiplied, self.added = (
                    sem(f"{name}_{x}") for x in ("prepared", "multiplied", "added"))
                self.columns = sem(f"{name}_columns") if weights else None

            def bank(self, q):
                b = q % 8 if not self.aside else q % 6 if q < 12 else q - 12
                return PB[b][:, 0:self.width]

            def since(self, q):
                return 8 if not self.aside else 4 if q < 4 else 10 if q < 6 else 6

            def pool(self, pool):
                def body(i, h, first):
                    if not first:
                        pool.wait_ge(self.multiplied, QRT * (4 * i + h - 3))
                        pool.wait_ge(self.multiplied, 1)
                    self.gather.fetch(pool, i, h)
                quarters_of(pool, self.steps, body)

            def scalar(self, act):
                def body(i, h, first):
                    self.gather.tell(act, i, h, first)
                if self.aside:
                    self.aside.scalar(act, self.steps, body)
                    return
                if self.weights is None:
                    quarters_of(act, self.steps, body)
                    return

                def column(i, h):
                    act.wait_ge(landed[h], 16 * QRT * (i + 1 + self.gather.before))
                    act.wait_ge(landed[h], 16 * QRT * (self.gather.before + 1))
                    act.copy(self.gather.ring[:, h, :, D:D + 4], self.weights(4 * i + h)).then_inc(self.columns, 1)
                for h in range(4):
                    body(0, h, True)
                with act.Fori(1, self.steps) as i:
                    for h in range(4):
                        column(i - 1, h)
                        body(i, h, False)
                for h in range(4):
                    column(self.steps - 1, h)

            def prepare(self, dve, i, h, j):
                g = 4 * i + h
                dve.tensor_scalar(Qv[:, h, j, :], IOTA, RELE[:, bass.ds(g * QRT + j, 1)], None, ALU.is_equal).then_inc(self.prepared, 1)
                if self.weights is not None:
                    if j == 0:
                        dve.wait_ge(landed[h], 16 * QRT * (i + 1 + self.gather.before))
                        dve.wait_ge(landed[h], 16 * QRT * (self.gather.before + 1))
                    v = self.gather.ring[:, h, j, 0:D].rearrange("p (h d) -> p h d", h=4)
                    w = self.weights(g)[:, j, :].rearrange("p (h o) -> p h o", o=1).to_broadcast([P, 4, D // 4])
                    dve.tensor_tensor(v, v, w, ALU.mult).then_inc(self.prepared, 1)

            def vector(self, dve):
                def step(i, h, first, last):
                    g = 4 * i + h
                    blocks = blocks_of(dve, g, QRT)
                    ahead = (i, h + 1) if h < 3 else (i + 1, 0)
                    for j in range(QRT):
                        if not (last and h == 3):
                            self.prepare(dve, *ahead, j)
                        dve.wait_ge(self.multiplied, QRT * g + j + 1)
                        dve.wait_ge(self.multiplied, 1)
                        if not (first and h == 0 and j == 0):
                            dve.wait_ge(self.added, QRT * g + j)
                            dve.wait_ge(self.added, 1)
                        acc = ar(ACC0, NB * ACCW)[:, bass.ds(blocks[j] * ACCW, self.width)]
                        dve.tensor_tensor(acc, acc, self.bank(4 * h + j), ALU.add).then_inc(self.added, 1)
                for j in range(QRT):
                    self.prepare(dve, 0, 0, j)
                for h in range(4):
                    step(0, h, True, False)
                with dve.Fori(1, self.steps - 1) as i:
                    for h in range(4):
                        step(i, h, False, False)
                for h in range(4):
                    step(self.steps - 1, h, False, True)
                dve.drain()

            def tensor(self, pe):
                def body(i, h, first):
                    pe.wait_ge(landed[h], 16 * QRT * (i + 1 + self.gather.before))
                    pe.wait_ge(landed[h], 16 * QRT * (self.gather.before + 1))
                    if self.weights is not None:
                        pe.wait_ge(self.columns, 4 * i + h + 1)
                        pe.wait_ge(self.columns, 1)
                    for j in range(QRT):
                        tile = QRT * (4 * i + h) + j
                        pe.wait_ge(self.prepared, self.ready_by_tile * (tile + 1))
                        pe.wait_ge(self.prepared, 1)
                        since = self.since(4 * h + j)
                        if not first or 4 * h + j >= 6 + 2 * (not self.aside):
                            pe.wait_ge(self.added, tile - since + 1)
                            pe.wait_ge(self.added, 1)
                        pe.matmul(self.bank(4 * h + j), Qv[:, h, j, :], self.gather.ring[:, h, j, 0:self.width],
                                  start=True, stop=True).then_inc(self.multiplied, 1)

                if self.aside:
                    self.aside.tensor(pe, self.steps, body)
                else:
                    quarters_of(pe, self.steps, body)

        LAST = sb("LAST", [1, EB], I32)

        class NarrowSums:

            def __init__(self, name, g, rows, width, room, marks, blocks, same):
                self.g, self.t = g, GRAPHS[g]["t"]
                self.steps = self.t // (2 * GRP)
                self.rows, self.width, self.blocks, self.same = rows, width, blocks, same
                self.prepared, self.multiplied, self.kept, self.split, self.rest, self.bt_in = (
                    sem(f"{name}_{x}") for x in ("prepared", "multiplied", "kept", "split", "rest", "bt_in"))
                n = GRP * width
                self.left = room[:, 0:2 * n].rearrange("p (h n) -> p h n", h=2)
                self.parts = room[:, 2 * n:5 * n].bitcast(BF16).rearrange("p (h t k w) -> p h t k w", h=2, t=GRP, k=3)
                self.S = marks.bitcast(BF16).rearrange("p (h t n) -> p h t n", h=2, t=GRP)

            def vector(self, dve):
                def body(i, h, first):
                    g = 2 * i + h
                    if not first:
                        dve.wait_ge(self.multiplied, g - 1)
                        dve.wait_ge(self.multiplied, 1)
                    left = self.left[:, h, :].rearrange("p (t w) -> p t w", t=GRP)
                    rows = self.rows(g).rearrange("p (t w) -> p t w", t=GRP)

                    def marks(j0):
                        for j in range(j0, j0 + 4):
                            m = dve.tensor_scalar(self.S[:, h, j, :], IOTAB, RELE[:, bass.ds(g * GRP + j, 1)], None, ALU.is_equal)
                        m.then_inc(self.prepared, 1)
                    dve.wait_ge(self.split, 3 * g + 1)
                    dve.wait_ge(self.split, 1)
                    dve.tensor_tensor(left, rows, self.parts[:, h, :, 0, :], ALU.subtract).then_inc(self.rest, 1)
                    marks(0)
                    dve.wait_ge(self.split, 3 * g + 2)
                    dve.wait_ge(self.split, 1)
                    dve.tensor_tensor(left, left, self.parts[:, h, :, 1, :], ALU.subtract).then_inc(self.rest, 1)
                    marks(4)
                pairs_of(dve, self.steps, body)

            def add_tiles(self, dve, tiles, out):
                dve.wait_ge(self.bt_in, 16)
                dve.memset(self.same[:, 0:1], 0.0)
                dve.tensor_tensor(self.same[:, 1:self.t], self.blocks[:, 1:self.t], self.blocks[:, 0:self.t - 1], ALU.is_equal)
                dve.wait_ge(self.kept, 2 * self.steps)
                dve.drain()
                for c in range(self.width):
                    v = tiles[:, 0:self.t, c]
                    dve.tensor_tensor_scan(v, self.same[:, 0:self.t], v, 0.0, ALU.mult, ALU.add)
                dve.drain()
                flat = tiles.rearrange("p t w -> p (t w)")
                with dve.Fori(0, EB) as b:
                    tile = dve.value_load(LAST[0:1, bass.ds(b, 1)], min_val=0, max_val=self.t - 1)
                    dve.tensor_copy(out[:, bass.ds(b * self.width, self.width)], flat[:, bass.ds(tile * self.width, self.width)])
                dve.memset(out[:, EB * self.width:NB * self.width], 0.0)
                dve.drain()

            def scalar(self, act):
                row = btD[self.g].rearrange("p (o q) -> o (p q)", o=1).to_broadcast([P, GRAPHS[self.g]["tq"] * P])
                act.dma_start(self.blocks, row).then_inc(self.bt_in, 16)

                def keep(g, h):
                    act.wait_ge(self.multiplied, g + 1)
                    act.wait_ge(self.multiplied, 1)
                    act.nop(nofuse=True)
                    act.copy(self.rows(g), PB[h][:, 0:GRP * self.width]).then_inc(self.kept, 1)

                def body(i, h, first):
                    g = 2 * i + h
                    left = self.left[:, h, :].rearrange("p (t w) -> p t w", t=GRP)
                    rows = self.rows(g).rearrange("p (t w) -> p t w", t=GRP)
                    act.copy(self.parts[:, h, :, 0, :], rows).then_inc(self.split, 1)
                    for k in (1, 2):
                        act.wait_ge(self.rest, 2 * g + k)
                        act.wait_ge(self.rest, 1)
                        act.copy(self.parts[:, h, :, k, :], left).then_inc(self.split, 1)
                    if not (first and h == 0):
                        keep(g - 1, 1 - h)
                pairs_of(act, self.steps, body)
                keep(2 * self.steps - 1, 1)

            def tensor(self, pe):
                def body(i, h, first):
                    g = 2 * i + h
                    pe.wait_ge(self.split, 3 * g + 3)
                    pe.wait_ge(self.split, 1)
                    pe.wait_ge(self.prepared, 2 * g + 2)
                    pe.wait_ge(self.prepared, 1)
                    if not first:
                        pe.wait_ge(self.kept, g - 1)
                        pe.wait_ge(self.kept, 1)
                    for j in range(GRP):
                        for k in range(3):
                            m = pe.matmul(PB[h][:, j * self.width:(j + 1) * self.width], self.S[:, h, j, :],
                                          self.parts[:, h, j, k, :], start=(k == 0), stop=(k == 2))
                    m.then_inc(self.multiplied, 1)
                pairs_of(pe, self.steps, body)

        class Spread:

            def __init__(self, name, g, rel, marks, edt, room, rounds):
                self.g, self.t = g, GRAPHS[g]["t"]
                self.steps = self.t // (2 * GRP)
                self.rounds = list(zip(rounds, rounds[1:]))
                self.rel_in = [sem(f"{name}_rel_in{h}") for h in (0, 1)]
                self.marked, self.multiplied, self.kept, self.bt_in = (
                    sem(f"{name}_{x}") for x in ("marked", "multiplied", "kept", "bt_in"))
                self.REL = rel.bitcast(BF16).rearrange("p (h c) -> p h c", h=2)
                self.S = marks.bitcast(BF16).rearrange("p (h t n) -> p h t n", h=2, t=GRP)
                self.edt = edt.bitcast(BF16)
                self.bt = room[0:EB, 0:288].bitcast(U8)
                self.hot = room[0:EB, 288:384].bitcast(BF16)
                self.parts = room[0:EB, 384:1152].bitcast(BF16).rearrange("p (k n) -> p k n", k=3)
                self.left = edt[0:EB, 0:512]

            def chunks(self, start, end):
                t0, t1 = start * 2 * GRP, end * 2 * GRP
                return [(c, min(192, t1 - c)) for c in range(t0, t1, 192)]

            def loads(self, eng):
                row = btD[self.g].rearrange("p (o q) -> o (p q)", o=1).to_broadcast([EB, GRAPHS[self.g]["tq"] * P])
                eng.dma_start(self.bt[:, 0:GRAPHS[self.g]["tq"] * P], row).then_inc(self.bt_in, 16)

                def body(i, h, first):
                    if not first:
                        eng.wait_ge(self.marked, 2 * i + h - 1)
                        eng.wait_ge(self.marked, 1)
                    n = GRP * P
                    eng.dma_start(self.REL[:, h, :], relD[self.g][0:1, bass.ds((2 * i + h) * n, n)].to_broadcast([P, n])
                                  ).then_inc(self.rel_in[h], 16)
                pairs_of(eng, self.steps, body)

            def vector(self, dve, ed):
                dve.drain().then_inc(asked, 1)
                dve.wait_ge(answered, nth("answers"))
                dve.tensor_copy(self.left, PB[6][0:EB, :])
                dve.drain()
                for k in range(3):
                    dve.tensor_copy(self.parts[:, k, :], self.left)
                    dve.drain()
                    if k < 2:
                        dve.tensor_tensor(self.left, self.left, self.parts[:, k, :], ALU.subtract)
                        dve.drain()
                dve.wait_ge(self.bt_in, 16)

                def keep(g, h):
                    dve.wait_ge(self.multiplied, g + 1)
                    dve.wait_ge(self.multiplied, 1)
                    w = 4 * GRP
                    dve.tensor_reduce(ed[:, bass.ds(g * w, w)], PB[h][:, 0:3 * w].rearrange("p (n k) -> p n k", k=3),
                                      AX.X, ALU.add).then_inc(self.kept, 1)

                for start, end in self.rounds:
                    edt = self.edt[:, 0:24 * GRP * (end - start)].rearrange("p (t n) -> p n t", n=12)
                    for c, n in self.chunks(start, end):
                        dve.tensor_scalar(self.hot[:, 0:n], self.bt[:, c:c + n], PCOL[0:EB, :], None, ALU.is_equal)
                        dve.drain().then_inc(asked, 1)
                        dve.wait_ge(answered, nth("answers"))
                        c0 = c - start * 2 * GRP
                        for b in range(6):
                            dve.tensor_copy(edt[:, 2 * b:2 * b + 2, c0:c0 + n],
                                            PB[2 + b][:, 0:2 * n].rearrange("p (a n) -> p a n", a=2))
                    dve.drain().then_inc(laid_out, 1)

                    def body(i, h, first):
                        dve.wait_ge(self.rel_in[h], 16 * (i + 1))
                        dve.wait_ge(self.rel_in[h], 16)
                        dve.tensor_scalar(self.S[:, h, :, :].rearrange("p t n -> p (t n)"), self.REL[:, h, :], PCOL, None,
                                          ALU.is_equal).then_inc(self.marked, 1)
                        if not (isinstance(i, int) and h == 0):
                            keep(2 * i + h - 1, 1 - h)
                    pairs_of(dve, end, body, start)
                    keep(2 * end - 1, 1)
                    dve.drain()

            def tensor(self, pe):
                pe.wait_ge(asked, nth("questions"))
                for h in range(4):
                    t = pe.transpose(PB[6][0:EB, h * P:(h + 1) * P], EDN[:, 0:EB, h], IDENT)
                t.then_inc(answered, 1)
                for start, end in self.rounds:
                    for c, n in self.chunks(start, end):
                        pe.wait_ge(asked, nth("questions"))
                        for a in range(12):
                            h, k = a // 3, a % 3
                            m = pe.matmul(PB[2 + a // 2][:, (a % 2) * n:(a % 2 + 1) * n], self.parts[:, k, h * P:(h + 1) * P],
                                          self.hot[:, 0:n], start=True, stop=True)
                        m.then_inc(answered, 1)
                    pe.wait_ge(laid_out, nth("laid out"))

                    def body(i, h, first):
                        g = 2 * i + h
                        pe.wait_ge(self.marked, g + 1)
                        pe.wait_ge(self.marked, 1)
                        if not first:
                            pe.wait_ge(self.kept, g - 1)
                            pe.wait_ge(self.kept, 1)
                        for j in range(GRP):
                            m = pe.matmul(PB[h][:, 12 * j:12 * j + 12], self.S[:, h, j, :],
                                          self.edt[:, bass.ds(((g - 2 * start) * GRP + j) * 12, 12)], start=True, stop=True)
                        m.then_inc(self.multiplied, 1)
                    pairs_of(pe, end, body, start)

        edge_tmp = ARENA[0:4, S0 + 800:S0 + 800 + P]
        laid_out = sem("laid_out")
        edge4 = sb("edge4", [P, 16])
        row4 = ARENA[0:4, S0:S0 + 6 * P]
        exp_go, exp_done = sem("exp_go"), sem("exp_done")

        class Weights:

            def __init__(self, g, es, ed, te, dst, pen):
                G = GRAPHS[g]
                self.g, self.tq, self.t = g, G["tq"], G["t"]
                self.L = self.tq * P
                self.es, self.ed, self.dst, self.pen = es, ed, dst, pen
                self.te = te.rearrange("p (h l) -> p h l", h=4)

            def part(self, v, h, q):
                return v.rearrange("e (p q) h -> e q p h", q=self.tq)[:, q, :, h]

            def groups(self):
                return [(h, n0, min(4, self.tq - n0)) for h in range(4) for n0 in range(0, self.tq, 4)]

            def carry(self, dve, back):
                end = 0 if back else self.L - 1
                dve.tensor_copy(edge4[:, 0:4], self.te[:, :, end])
                dve.drain().then_inc(asked, 1)
                dve.wait_ge(answered, nth("answers"))
                first, last, val = row4[:, 0:P], row4[:, P:2 * P], row4[:, 2 * P:3 * P]
                d0, d1, c = row4[:, 3 * P:4 * P], row4[:, 4 * P:5 * P], row4[:, 5 * P:6 * P]
                dve.tensor_copy(row4[:, 0:3 * P], PB[2][0:4, 0:3 * P])
                dve.memset(d0, -BIG)
                dve.memset(d1, -BIG)
                dve.drain()
                n = P - 1
                x, y = (slice(0, n), slice(1, P)) if back else (slice(1, P), slice(0, n))
                near, far = (last, first) if back else (first, last)
                dve.tensor_tensor(c[:, x], near[:, x], far[:, y], ALU.not_equal)
                dve.drain()
                dve.tensor_scalar(c[:, x], c[:, x], -BIG, None, ALU.mult)
                dve.tensor_tensor(d0[:, y], first[:, y], last[:, y], ALU.not_equal)
                dve.drain()
                dve.scalar_tensor_tensor(out=edge_tmp[:, x], in0=d0[:, y], scalar=-BIG, in1=c[:, x], op0=ALU.mult, op1=ALU.add)
                dve.tensor_tensor(d1[:, x], val[:, y], c[:, x], ALU.add)
                dve.drain()
                dve.memset(d0, -BIG)
                dve.drain()
                dve.tensor_copy(d0[:, x], edge_tmp[:, x])
                dve.drain()
                turn = slice(None, None, -1) if back else slice(None)
                dve.tensor_tensor_scan(c[:, turn], d0[:, turn], d1[:, turn], -BIG, ALU.add, ALU.max)
                dve.drain().then_inc(asked, 1)
                dve.wait_ge(answered, nth("answers"))
                dve.tensor_copy(edge4[:, 12:16], PB[3][:, 0:4])
                dve.drain()

            def scan(self, dve, back, first):
                L = self.L
                for h in range(4):
                    v = self.te[:, h, ::-1] if back else self.te[:, h, :]
                    pen = self.pen[:, L:0:-1] if back else self.pen[:, 0:L]
                    dve.tensor_tensor_scan(v, pen, v, -BIG if first else edge4[:, 12 + h:13 + h], ALU.add, ALU.max)
                dve.drain()

            def vector(self, dve):
                tq, L, T = self.tq, self.L, self.t
                for h, n0, n in self.groups():
                    dve.drain().then_inc(asked, 1)
                    dve.wait_ge(answered, nth("answers"))
                    dve.tensor_copy(self.te[:, h, n0 * P:(n0 + n) * P], PB[2][:, 0:n * P])
                dve.memset(self.pen[:, 0:L + 1], 0.0)
                dve.drain()
                dve.tensor_tensor(self.pen[:, 1:L], self.dst[:, 1:L], self.dst[:, 0:L - 1], ALU.not_equal)
                for h in range(4):
                    dve.tensor_copy(edge4[:, 4 + h:5 + h], self.dst[:, 0:1])
                    dve.tensor_copy(edge4[:, 8 + h:9 + h], self.dst[:, L - 1:L])
                dve.drain()
                dve.tensor_scalar(self.pen[:, 1:L], self.pen[:, 1:L], -BIG, None, ALU.mult)
                dve.drain()
                for back in (False, True):
                    self.scan(dve, back, True)
                    self.carry(dve, back)
                    self.scan(dve, back, False)
                es, ed = self.es, self.ed
                dve.tensor_tensor(es, es, ed, ALU.add)
                dve.drain()
                dve.scalar_tensor_tensor(out=es, in0=es, scalar=0.2, in1=es, op0=ALU.mult, op1=ALU.max)
                for h, n0, n in self.groups():
                    dve.drain().then_inc(asked, 1)
                    dve.wait_ge(answered, nth("answers"))
                    for q in range(n0, n0 + n):
                        v = self.part(ed, h, q)
                        dve.tensor_tensor(v, PB[2][:, (q - n0) * P:(q - n0 + 1) * P], v, ALU.add)
                dve.drain()
                dve.scalar_tensor_tensor(out=ed, in0=ed, scalar=0.2, in1=ed, op0=ALU.mult, op1=ALU.max)
                dve.drain()
                dve.tensor_tensor(es, es, ed, ALU.subtract)
                dve.drain().then_inc(exp_go, 1)
                dve.wait_ge(exp_done, nth("exponentials"))

            def carry_tensor(self, pe):
                pe.wait_ge(asked, nth("questions"))
                for k, a in enumerate((4, 8, 0)):
                    t = pe.transpose(PB[2][0:4, k * P:(k + 1) * P], edge4[:, a:a + 4], IDENT)
                t.then_inc(answered, 1)
                pe.wait_ge(asked, nth("questions"))
                pe.transpose(PB[3][:, 0:4], row4[:, 5 * P:6 * P], IDENT[0:4, 0:4]).then_inc(answered, 1)

            def tensor(self, pe):
                for h, n0, n in self.groups():
                    pe.wait_ge(asked, nth("questions"))
                    for q in range(n0, n0 + n):
                        t = pe.transpose(PB[2][:, (q - n0) * P:(q - n0 + 1) * P], self.part(self.es, h, q), IDENT)
                    t.then_inc(answered, 1)
                self.carry_tensor(pe)
                self.carry_tensor(pe)
                for h, n0, n in self.groups():
                    pe.wait_ge(asked, nth("questions"))
                    for q in range(n0, n0 + n):
                        t = pe.transpose(PB[2][:, (q - n0) * P:(q - n0 + 1) * P], self.te[:, h, q * P:(q + 1) * P], IDENT)
                    t.then_inc(answered, 1)

        W0 = ACC0
        GAMMA, BETA = ar(W0 + 9280, D), ar(W0 + 9536, D)

        class Experts:

            def __init__(self, name, n, weights_at, bias, fxt, fht, xin):
                self.n = n
                self.rows_in, self.turned, self.cols_in, self.hidden, self.curved, self.mixed, self.added = (
                    sem(f"{name}_{x}") for x in ("rows_in", "turned", "cols_in", "hidden", "curved", "mixed", "added"))
                self.w1 = [ar(a, 1024).rearrange("p (k f) -> p k f", k=2) for a in weights_at]
                self.w2 = [ar(a + 1024, 1024).rearrange("p (f d) -> p f d", f=4) for a in weights_at]
                self.b1 = [bias[:, 4 * e:4 * e + 4] for e in range(n)]
                self.FXT = fxt.rearrange("p (k n) -> p k n", k=2)
                self.FHT = fht.rearrange("p (a f n) -> p a f n", a=2, f=4)
                self.XIN = xin.rearrange("p (j d) -> p j d", j=2)

            def each(self, eng, body):
                body(0, True, False)
                with eng.Fori(1, NB // 2 - 1) as i:
                    body(i, False, False)
                body(NB // 2 - 1, False, True)

            def turn(self, pe, i):
                pe.wait_ge(self.rows_in, i + 1)
                pe.wait_ge(self.rows_in, 1)
                for j in range(2):
                    for k in range(2):
                        t = pe.transpose(PB[0][:, k * 256 + j * P:k * 256 + (j + 1) * P], self.XIN[:, j, k * P:(k + 1) * P], IDENT)
                t.then_inc(self.turned, 1)

            def tensor(self, pe):
                n = self.n

                def up(e):
                    for f in range(4):
                        for k in range(2):
                            m = pe.matmul(PB[1 + 2 * (e % 2) + f // 2][:, (f % 2) * 256:(f % 2 + 1) * 256],
                                          self.w1[e][:, k, f * P:(f + 1) * P], self.FXT[:, k, :], start=(k == 0), stop=(k == 1))
                        if f % 2:
                            m.then_inc(self.hidden, 1)

                def body(i, first, last):
                    pe.wait_ge(self.cols_in, i + 1)
                    pe.wait_ge(self.cols_in, 1)
                    up(0)
                    for e in range(n):
                        if e + 1 < n:
                            up(e + 1)
                        elif not last:
                            self.turn(pe, i + 1)
                        pe.wait_ge(self.curved, i * n + e + 1)
                        pe.wait_ge(self.curved, 1)
                        if not (first and e < 2):
                            pe.wait_ge(self.added, i * n + e - 1)
                            pe.wait_ge(self.added, 1)
                        for j in range(2):
                            for f in range(4):
                                m = pe.matmul(PB[5 + e % 2][:, j * D:(j + 1) * D], self.FHT[:, e % 2, f, j * P:(j + 1) * P],
                                              self.w2[e][:, f, :], start=(f == 0), stop=(f == 3))
                        m.then_inc(self.mixed, 1)
                self.turn(pe, 0)
                self.each(pe, body)

            def scalar(self, act, behind=None):
                n = self.n

                def columns(i):
                    act.wait_ge(self.turned, i + 1)
                    act.wait_ge(self.turned, 1)
                    act.copy(self.FXT[:, :, :].rearrange("p k n -> p (k n)"), PB[0][:, :]).then_inc(self.cols_in, 1)

                def body(i, first, last):
                    for e in range(n):
                        if not (first and e < 2):
                            act.wait_ge(self.mixed, i * n + e - 1)
                            act.wait_ge(self.mixed, 1)
                        for f in range(4):
                            if f % 2 == 0:
                                act.wait_ge(self.hidden, (i * n + e) * 2 + f // 2 + 1)
                                act.wait_ge(self.hidden, 1)
                            a = act.activation(self.FHT[:, e % 2, f, :], PB[1 + 2 * (e % 2) + f // 2][:, (f % 2) * 256:(f % 2 + 1) * 256],
                                               ACT.Gelu, bias=self.b1[e][:, f:f + 1])
                        a.then_inc(self.curved, 1)
                        if e == n - 1 and not last:
                            columns(i + 1)
                        if behind:
                            behind(i, e, first)
                columns(0)
                self.each(act, body)

            def vector(self, dve, rows, take):
                n = self.n

                def put(i):
                    rows(i)
                    dve.drain().then_inc(self.rows_in, 1)

                def body(i, first, last):
                    for e in range(n):
                        if e == n - 1 and not last:
                            dve.wait_ge(self.turned, i + 1)
                            dve.wait_ge(self.turned, 1)
                            put(i + 1)
                        dve.wait_ge(self.mixed, i * n + e + 1)
                        dve.wait_ge(self.mixed, 1)
                        take(i, e, PB[5 + e % 2], first)
                put(0)
                self.each(dve, body)

        def serve_exp(act, v):
            act.wait_ge(exp_go, nth("exponentials asked"))
            act.activation(v, v, ACT.Exp).then_inc(exp_done, 1)

        def softmax8(dve, v, tmp):
            dve.drain()
            dve.tensor_reduce(tmp, v, AX.X, ALU.max)
            dve.drain()
            dve.tensor_scalar(v, v, tmp, None, ALU.subtract)
            dve.drain().then_inc(exp_go, 1)
            dve.wait_ge(exp_done, nth("exponentials"))
            dve.tensor_reduce(tmp, v, AX.X, ALU.add)
            dve.drain()
            dve.reciprocal(tmp, tmp)
            dve.drain()
            dve.tensor_scalar(v, v, tmp, None, ALU.mult)
            dve.drain()

        def top2(dve, s, B, E, a, b, m, gates, first_id=None, second_id=None):
            rep = lambda v: v.rearrange("p (b e) -> p b e", e=1).to_broadcast([P, B, E])
            ids = IOTA[:, 0:E].rearrange("p (b e) -> p b e", b=1).to_broadcast([P, B, E])
            m1, m2, i1, d = (m[:, k, :] for k in range(4))

            def winner(v, best, hot, ident):
                dve.tensor_reduce(best, v, AX.X, ALU.max)
                dve.drain()
                dve.tensor_tensor(hot, v, rep(best), ALU.not_equal)
                dve.drain()
                dve.scalar_tensor_tensor(out=hot, in0=hot, scalar=float(E), in1=ids, op0=ALU.mult, op1=ALU.add)
                dve.drain()
                dve.tensor_reduce(ident, hot, AX.X, ALU.min)
                dve.drain()
                dve.tensor_tensor(hot, ids, rep(ident), ALU.is_equal)
                dve.drain()

            winner(s, m1, a, i1)
            if first_id is not None:
                dve.tensor_copy(first_id, i1)
            dve.scalar_tensor_tensor(out=s, in0=a, scalar=-BIG, in1=s, op0=ALU.mult, op1=ALU.add)
            dve.drain()
            winner(s, m2, b, i1)
            if second_id is not None:
                dve.tensor_copy(second_id, i1)
            dve.tensor_tensor(d, m2, m1, ALU.subtract)
            dve.drain().then_inc(exp_go, 1)
            dve.wait_ge(exp_done, nth("exponentials"))
            dve.tensor_scalar(m1, d, 1.0, None, ALU.add)
            dve.drain()
            dve.reciprocal(m1, m1)
            dve.drain()
            dve.tensor_tensor(m2, d, m1, ALU.mult)
            dve.drain()
            dve.tensor_tensor(a, a, rep(m1), ALU.mult)
            dve.tensor_tensor(b, b, rep(m2), ALU.mult)
            dve.drain()
            dve.tensor_tensor(gates, a, b, ALU.add)
            dve.drain()

        def extend(dve, w, n, att, heads, tmp, to):
            dve.tensor_tensor(tmp, w, att, ALU.mult)
            dve.drain()
            dve.tensor_reduce(to, tmp.rearrange("p (h d) -> p h d", h=heads), AX.X, ALU.add)
            dve.drain()

        def block(V, b):
            return V[:, bass.ds(b, 1), :].rearrange("p a d -> p (a d)")

        DSTS = {0: ar(ACC0 + 9000, 896), 2: ar(23040, 1152)}
        SMALL2 = ar(28300, 48).rearrange("p (a n) -> p a n", n=16)
        IDSI = sb("IDSI", [P, 2], I32)

        loads, load_sem, load_total = {}, {}, {}

        def define_load(name, pairs, behind=None):
            loads[name] = pairs
            load_sem[name] = load_sem[behind] if behind else sem(f"load_{name}")
            load_total[name] = 16 * len(pairs) + (load_total[behind] if behind else 0)

        def load(sp, name):
            for dst, src in loads[name]:
                sp.dma_start(dst, src, allow_slow_non_contiguous=True).then_inc(load_sem[name], 16)

        row = lambda a: a.rearrange("(o n) -> o n", o=1).to_broadcast([P, a.shape[0]])
        rows_by_chunk = lambda a: a.rearrange("(k p) n -> p k n", p=P)
        WX = ar(WS0, 2 * (D + 8)).rearrange("p (k n) -> p k n", k=2)
        ATT = ar(WS0 + 600, 512).rearrange("p (a n) -> p a n", a=2)
        last = N - (EB - 1) * P
        define_load("start", [(CON[:, :], consts), (FLIPS, flips), (WX[:, :, 0:D], rows_by_chunk(A["L0_gnn_W"])),
                              (ATT[:, 0, :], row(A["L0_gnn_a_src"].rearrange("h d -> (h d)"))),
                              (ATT[:, 1, :], row(A["L0_gnn_a_dst"].rearrange("h d -> (h d)")))])
        define_load("x", [(X[:, 8 * c:8 * c + 8, :], A["x"][8 * c * P:8 * (c + 1) * P, :].rearrange("(b p) d -> p b d", p=P))
                          for c in range(6)])
        define_load("x_end", [(X[0:last, EB - 1, :], A["x"][(EB - 1) * P:N, :])])
        for g in range(3):
            define_load(f"graph{g}", graph_loads(g), f"graph{g - 1}" if g else None)
        BIASR = sb("BIASR", [P, D])
        sage_w = lambda m: ar(WS0 + 512 * m, 512).rearrange("p (k n) -> p k n", k=2)
        mats = [A["L1_gnn_W_in"]] + [A[f"L1_gnn_W_{x}"][l] for l in range(3) for x in ("agg", "self")] + [A["L1_gnn_W_out"]]
        define_load("sage", [(sage_w(m), rows_by_chunk(a)) for m, a in enumerate(mats)])
        biases = [A["L1_gnn_b_in"]] + [A["L1_gnn_b_hid"][l] for l in range(3)] + [A["L1_gnn_b_out"]]
        for m, a in enumerate(biases):
            define_load(f"bias{m}", [(BIASR[:, :], row(a))], f"bias{m - 1}" if m else None)
        WRT, BRT = ar(W0 + 10800, 16).rearrange("p (k n) -> p k n", k=2), ar(W0 + 10816, 8)
        define_load("router", [(WRT, rows_by_chunk(A["L0_ffn_Wr"])), (BRT, row(A["L0_ffn_br"])),
                               (GAMMA, row(A["L0_ffn_gamma"])), (BETA, row(A["L0_ffn_beta"]))])
        WG = ar(WS0, 48).rearrange("p (k n) -> p k n", k=2)
        SMALL = ar(WS0 + 64, 96).rearrange("p (a n) -> p a n", n=16)
        define_load("gat1", [(WG[:, :, 0:16], rows_by_chunk(A["L1_ffn_W_gat"])),
                             (SMALL[:, 0, :], row(A["L1_ffn_att_src"].rearrange("h d -> (h d)"))),
                             (SMALL[:, 1, :], row(A["L1_ffn_att_dst"].rearrange("h d -> (h d)"))),
                             (SMALL[:, 2, :], row(A["L1_ffn_b_gat"])), (SMALL[:, 3, :], row(A["L1_ffn_ln_gamma"])),
                             (SMALL[:, 4, :], row(A["L1_ffn_ln_beta"]))])
        define_load("small2", [(SMALL2[:, k, :], row(A[f"L1_ffn_{x}"])) for k, x in enumerate(("b_gat", "ln_gamma", "ln_beta"))])
        for g in (0, 2):
            define_load(f"dst{g}", [(DSTS[g], dstD[g])], "dst0" if g else None)

        zeroed = sem("zeroed")
        es_kept = sem("es_kept")
        chosen = sem("chosen")
        chosen_in = sem("chosen_in")
        stored = sem("stored")
        weighted = sem("weighted")
        finished = sem("finished")

        def chunk_stores(sp, table, V, width, taken, s, base):
            for c in range(5):
                sp.wait_ge(taken, 10 * (c + 1))
                dst = table[10 * c * P:10 * (c + 1) * P, :].rearrange("(b p) d -> p b d", p=P)
                sp.dma_start(dst, V[:, 10 * c:10 * (c + 1), 0:width]).then_inc(s, 16)
            sp.wait_ge(s, base + 80)

        first = Dense("project", 2, lambda k: WX[:, k, :], D + 8)
        es_gather = Kept("es", 0, esD, 4, 4)
        spread0 = Spread("spread0", 0, ar(GR0 + 1024, 1024), ar(S0, 1024), ar(ACC0, GRAPHS[0]["t"] * 6), ar(ACC0 + 5400, 1152), (0, 55))
        ES0, ED0, TE0 = (ar(H0 + k * 3584, 3584) for k in range(3))
        weights0 = Weights(0, ES0.rearrange("p (t h) -> p t h", h=4), ED0.rearrange("p (t h) -> p t h", h=4),
                           TE0, DSTS[0], ar(ACC0 + 10000, 900))
        hp_gather = Gather("hp", 0, tabD, D, ACCW)

        def edge_weights(g):
            return ES0[:, bass.ds(g * QRT * 4, QRT * 4)].rearrange("p (t h) -> p t h", h=4)

        sums0 = Sums("sums0", hp_gather, ACCW, edge_weights)
        W12 = ar(W0 + 10830, 2)
        experts0 = Experts("experts0", 2, (W0, W0 + 2048), ar(W0 + 8192, 8), ar(GR0, 512), ar(GR0 + 512, 2048), ar(GR0 + 2560, 512))
        B2 = ar(W0 + 8256, 2 * D)
        enter = Dense("enter", 2, lambda k: sage_w(0)[:, k, :], D, (Hv, False, True, ACT.Copy))
        hop_gather = [Gather(f"hop{l}", 1, tabD, D, ACCW) for l in range(3)]
        selfs = [SelfPart(f"self{l}", (lambda l: lambda k: sage_w(2 + 2 * l)[:, k, :])(l)) for l in range(3)]
        hops = [Sums(f"hops{l}", hop_gather[l], D + 1, None, selfs[l]) for l in range(3)]
        mixes = [Dense(f"mix{l}", 2, (lambda l: lambda k: sage_w(1 + 2 * l)[:, k, :])(l), D, (Hv, True, False, ACT.Relu)) for l in range(3)]
        leave = Dense("leave", 2, lambda k: sage_w(7)[:, k, :], D, (X, True, True, ACT.Copy))
        T20 = ar(ACC0, NB * 24).rearrange("p (b n) -> p b n", n=24)
        project2 = Dense("project2", 2, lambda k: WG[:, k, :], 24)
        G1 = ar(ACC0, 1152 * 20).rearrange("p (t n) -> p t n", n=20)
        ED2, TE2 = ar(24192, 4608), ar(28800, 4608)
        g1_gather = KeptBySync("g1", 2, t20D, 20, 20)
        spread2 = Spread("spread2", 2, ar(28800, 1024), ar(S0, 1024), ar(30216, 36 * 2 * GRP * 6), ar(23040, 1152), (0, 36, 71))
        weights2 = Weights(2, G1[:, :, 16:20], ED2.rearrange("p (t h) -> p t h", h=4), TE2, DSTS[2], SRCE[:, :])
        ACC2 = ar(24192, NB * 20)
        sums2 = NarrowSums("sums2", 2, lambda g: ar(ACC0, 1152 * 20)[:, bass.ds(g * GRP * 20, GRP * 20)], 20,
                           ar(GR0 + 512, 800), ar(S0, 1024), ar(GR0 + 1400, 288).bitcast(U8), SRCE[:, :])
        experts1 = Experts("experts1", 4, (22720, 24768, 26816, 30216), ESN[:, :, :].rearrange("p b h -> p (b h)"), ar(32264, 512), ar(32776, 2048), ar(34824, 512))
        YS = ar(28864, 1024).rearrange("p (a n) -> p a n", a=2)
        yD = [dram(f"yD{e}", (NP, D)) for e in range(4)]
        y_kept = [sem(f"y_kept{a}") for a in range(2)]
        YB = 5
        YC = [ar(5120 * c, 4 * YB * D).rearrange("p (e b d) -> p e b d", e=4, b=YB) for c in range(4)]
        y_back = [sem(f"y_back{c}") for c in range(4)]
        B24 = [BIASR[:, :]] + [ar(35336 + e * D, D) for e in range(3)]
        x_done = sem("x_done")

        define_load("experts1", [p for e in range(4) for p in (
            (experts1.w1[e], rows_by_chunk(A["L1_ffn_W1"][e])), (experts1.w2[e], rows_by_chunk(A["L1_ffn_W2"][e])),
            (experts1.b1[e], A["L1_ffn_b1"][e].rearrange("(f p) -> p f", p=P)),
            (B24[e], row(A["L1_ffn_b2"][e])))])

        LOGITS, DIFF0, DIFF1 = ar(W0 + 10840, 8), ar(W0 + 10883, 1), ar(28100 + 3 * NB, NB)

        block_ctx = ctx.enter_context(nc.Block())

        def normalise_all(dve):
            with dve.Fori(0, NB // 2) as i:
                for j in range(2):
                    normalise(dve, block(Hv, 2 * i + j), X, 2 * i + j)
            dve.drain()

        def over_blocks(v):
            return v.rearrange("p (b d) -> p b d", b=1).to_broadcast([P, NB, v.shape[1]])

        @block_ctx.vector
        def _(dve):
            dve.memset(X[:, EB - 1:NB, :], 0.0)
            dve.drain().then_inc(zeroed, 1)
            dve.wait_ge(load_sem["start"], load_total["start"])
            for k in range(2):
                for a in range(2):
                    extend(dve, WX[:, k, 0:D], D, ATT[:, a, :], 4, ar(ACC0, D), WX[:, k, D + 4 * a:D + 4 * a + 4])
            dve.wait_ge(load_sem["x"], load_total["x"])
            dve.wait_ge(load_sem["x_end"], load_total["x_end"])
            stats_vector(dve, X)

            def keep(dve, bank, b):
                dve.tensor_copy(block(Hv, b), bank[:, 0:D])
                dve.tensor_copy(block(ESN, b), bank[:, D:D + 4])
                dve.tensor_copy(block(EDN, b), bank[:, D + 4:D + 8])
            first.vector(dve, lambda dve, to, b: normalise(dve, to[:, 0:D], X, b), keep)
            cur = sort_vector(dve, 0)
            count_vector(dve, 0, cur)
            tiles_vector(dve, 0)
            dve.drain().then_inc(met, 1)
            dve.wait_ge(met, MEETING * 1)

            t = GRAPHS[0]["t"] * 4
            dve.memset(ES0[:, t:3584], 0.0)
            dve.memset(ED0[:, t:3584], 0.0)
            spread0.vector(dve, ED0)
            for g in (1, 2):
                cur = sort_vector(dve, g)
                count_vector(dve, g, cur)
            for g in (1, 2):
                tiles_vector(dve, g)
            dve.wait_ge(es_kept, 1)
            dve.wait_ge(load_sem["dst0"], load_total["dst0"])
            weights0.vector(dve)
            dve.memset(ar(ACC0, NB * ACCW), 0.0)
            dve.drain().then_inc(met, 1)
            dve.wait_ge(met, MEETING * 2)

            sums0.vector(dve)
            dve.tensor_scalar(ESN[:, :, :], ACCv[:, :, D:D + 4], 1e-16, None, ALU.add)
            dve.drain()
            dve.reciprocal(ESN[:, :, :], ESN[:, :, :])
            dve.drain()
            v = ACCv[:, :, 0:D].rearrange("p b (h d) -> p b h d", h=4)
            dve.tensor_tensor(v, v, ESN[:, :, :].rearrange("p b (h o) -> p b h o", o=1).to_broadcast([P, NB, 4, 64]), ALU.mult)
            dve.drain()
            dve.tensor_tensor(X[:, :, :], X[:, :, :], ACCv[:, :, 0:D], ALU.add)
            dve.drain()
            dve.drain().then_inc(met, 1)
            dve.wait_ge(met, MEETING * 3)

            stats_vector(dve, X)
            normalise_all(dve)
            dve.wait_ge(load_sem["router"], load_total["router"])
            sumx = ar(W0 + 10000, D)
            mb = ar(W0 + 10300, 2 * P).rearrange("p (k n) -> p k n", k=2)
            lg = LOGITS
            t1, a8, b8 = ar(W0 + 10850, 1), ar(W0 + 10860, 8), ar(W0 + 10870, 8)
            m4, g8, ids = ar(W0 + 10880, 4), ar(W0 + 10890, 8), ar(W0 + 10900, 2)
            c8, d8 = ar(W0 + 10910, 8), ar(W0 + 10920, 8)
            dve.tensor_reduce(sumx, Hv.rearrange("p b d -> p d b"), AX.X, ALU.add)
            dve.drain().then_inc(asked, 1)
            dve.wait_ge(answered, nth("answers"))
            for k in range(2):
                dve.tensor_scalar(mb[:, k, :], ONES, PB[2][:, k:k + 1], 1.0 / N, ALU.mult, ALU.mult)
            dve.drain().then_inc(asked, 1)
            dve.wait_ge(answered, nth("answers"))
            dve.tensor_tensor(lg, PB[3][:, 0:8], BRT, ALU.add)
            softmax8(dve, lg, t1)
            capacity = float(-(-N * 5 // (4 * 8)))
            dve.tensor_scalar(c8, lg, float(N), None, ALU.mult)
            dve.drain()
            dve.tensor_scalar(d8, c8, capacity, None, ALU.max)
            dve.drain()
            dve.reciprocal(d8, d8)
            dve.drain()
            dve.tensor_scalar(d8, d8, capacity, -1.0, ALU.mult, ALU.add)
            dve.tensor_scalar(c8, c8, capacity, None, ALU.is_gt)
            dve.drain()
            dve.tensor_tensor(c8, c8, d8, ALU.mult)
            dve.drain()
            dve.tensor_scalar(c8, c8, 1.0, None, ALU.add)
            dve.drain()
            dve.tensor_tensor(lg, lg, c8, ALU.mult)
            softmax8(dve, lg, t1)
            one = lambda v: v.rearrange("p (b e) -> p b e", b=1)
            top2(dve, one(lg), 1, 8, one(a8), one(b8), m4.rearrange("p (k b) -> p k b", b=1), one(g8),
                 ids[:, 0:1], ids[:, 1:2])
            dve.tensor_copy(W12, m4[:, 0:2])
            dve.tensor_copy(IDSI[:, :], ids)
            dve.drain().then_inc(chosen, 1)
            dve.wait_ge(chosen_in, 16 * 8)

            def add_expert(i, e, bank, first):
                gate = W12[:, e:e + 1]
                for j in range(2):
                    to = block(Hv, 2 * i + j)
                    dve.scalar_tensor_tensor(out=to, in0=bank[:, j * D:(j + 1) * D], scalar=gate, in1=to, op0=ALU.mult, op1=ALU.add)
                dve.drain().then_inc(experts0.added, 1)
                for j in range(2):
                    to = block(Hv, 2 * i + j)
                    dve.scalar_tensor_tensor(out=to, in0=B2[:, e * D:(e + 1) * D], scalar=gate, in1=to, op0=ALU.mult, op1=ALU.add)
                dve.drain()
                if e == 1:
                    for j in range(2):
                        dve.bn_stats(STATS[:, j, :], block(Hv, 2 * i + j))
                    dve.drain()
                    for j in range(2):
                        dve.bn_aggr(MVJ[:, j, :], STATS[:, j, :])
                    dve.drain()
                    dve.tensor_copy(MV[:, bass.ds(2 * i, 2), :], MVJ[:, 0:2, :])
                    for j in range(2):
                        to, x = block(Hv, 2 * i + j), block(X, 2 * i + j)
                        dve.scalar_tensor_tensor(out=to, in0=to, scalar=MVJ[:, j, 0:1], in1=GAMMA, op0=ALU.subtract, op1=ALU.mult)
                        dve.tensor_tensor(x, x, BETA, ALU.add)
                    dve.drain()
            experts0.vector(dve, lambda i: dve.tensor_copy(experts0.XIN[:, :, :], Hv[:, bass.ds(2 * i, 2), :]), add_expert)
            deviations_vector(dve)
            stats_vector(dve, X, lambda b: dve.scalar_tensor_tensor(
                out=block(X, b), in0=block(Hv, b), scalar=RS[:, bass.ds(b, 1)], in1=block(X, b), op0=ALU.mult, op1=ALU.add))
            dve.wait_ge(load_sem["sage"], load_total["sage"])
            dve.wait_ge(load_sem["bias0"], load_total["bias0"])

            enter.vector(dve, lambda dve, to, b: normalise(dve, to[:, 0:D], X, b), None)

            def room_for_sums(dve, ga, dense):
                dve.memset(ar(ACC0, NB * ACCW), 0.0)
                dve.wait_ge(dense.taken, NB)
                dve.memset(ga.ring[:, :, :, D:D + 1], 1.0)
            room_for_sums(dve, hop_gather[0], enter)
            dve.drain().then_inc(met, 1)
            dve.wait_ge(met, MEETING * 4)

            for l in range(3):
                dve.wait_ge(load_sem[f"bias{l + 1}"], load_total[f"bias{l + 1}"])
                hops[l].vector(dve)
                dve.tensor_scalar(RS[:, :], ACCv[:, :, D], 1.0, None, ALU.max)
                dve.drain()
                dve.reciprocal(RS[:, :], RS[:, :])
                dve.drain()

                def mix_in(dve, to, b):
                    dve.tensor_scalar(to[:, 0:D], ar(ACC0, NB * ACCW)[:, bass.ds(b * ACCW, D)], RS[:, bass.ds(b, 1)], None, ALU.mult)

                mixes[l].vector(dve, mix_in, None)
                if l < 2:
                    room_for_sums(dve, hop_gather[l + 1], mixes[l])
                    dve.drain().then_inc(met, 1)
                    dve.wait_ge(met, MEETING * (5 + l))
            dve.wait_ge(mixes[2].taken, NB)
            dve.drain().then_inc(sp_go, 1)
            dve.wait_ge(load_sem["bias4"], load_total["bias4"])

            leave.vector(dve, lambda dve, to, b: dve.tensor_copy(to[:, 0:D], block(Hv, b)), None)
            dve.wait_ge(leave.taken, NB)
            stats_vector(dve, X)
            dve.drain().then_inc(sp_go, 1)
            dve.wait_ge(load_sem["gat1"], load_total["gat1"])
            for k in range(2):
                for a in range(2):
                    extend(dve, WG[:, k, 0:16], 16, SMALL[:, a, :], 4, SM[:, 0:16], WG[:, k, 16 + 4 * a:20 + 4 * a])
            project2.vector(dve, lambda dve, to, b: normalise(dve, to[:, 0:D], X, b),
                            lambda dve, bank, b: dve.tensor_copy(block(T20, b), bank[:, 0:24]))
            dve.tensor_copy(EDN[:, :, :], T20[:, :, 20:24])
            dve.drain().then_inc(met, 1)
            dve.wait_ge(met, MEETING * 7)

            def rows_of_x(i):
                for j in range(2):
                    normalise(dve, experts1.XIN[:, j, :], X, 2 * i + j)

            def keep_result(i, e, bank, first):
                if not (first and e < 2):
                    dve.wait_ge(y_kept[e % 2], 16 * (2 * i + e // 2))
                    dve.wait_ge(y_kept[e % 2], 16)
                bias = B24[e].rearrange("p (o d) -> p o d", o=1).to_broadcast([P, 2, D])
                dve.tensor_tensor(YS[:, e % 2, :].rearrange("p (j d) -> p j d", j=2), bank[:, 0:2 * D].rearrange("p (j d) -> p j d", j=2),
                                  bias, ALU.add)
                dve.drain().then_inc(experts1.added, 1)
            dve.wait_ge(load_sem["experts1"], load_total["experts1"])
            experts1.vector(dve, rows_of_x, keep_result)
            t = GRAPHS[2]["t"]
            dve.memset(ED2[:, 4 * t:4608], 0.0)
            spread2.vector(dve, ED2)
            dve.memset(G1[:, t:1152, :], 0.0)
            g1_gather.all_kept(dve)
            dve.wait_ge(load_sem["dst2"], load_total["dst2"])
            weights2.vector(dve)
            v = G1[:, :, 0:16].rearrange("p t (h e) -> p t h e", h=4)
            dve.tensor_tensor(v, v, G1[:, :, 16:20].rearrange("p t (h o) -> p t h o", o=1).to_broadcast([P, 1152, 4, 4]), ALU.mult)
            dve.tensor_copy(IOTAB, IOTA)
            dve.drain().then_inc(weighted, 1)
            sums2.vector(dve)
            sums2.add_tiles(dve, G1, ACC2)
            dve.drain()
            dve.drain().then_inc(met, 1)
            dve.wait_ge(met, MEETING * 8)

            A16 = ar(25800, NB * 16).rearrange("p (b n) -> p b n", n=16)
            B16 = ar(26600, NB * 16).rearrange("p (b n) -> p b n", n=16)
            mean, rs16 = ar(27400, NB), ar(27450, NB)
            s4, a4, c4, m4 = (ar(27500 + 200 * k, NB * 4) for k in range(4))
            acc2 = ACC2.rearrange("p (b n) -> p b n", n=20)
            v4 = lambda v: v.rearrange("p (b e) -> p b e", e=4)
            rep16 = lambda v: v.rearrange("p (b o) -> p b o", o=1).to_broadcast([P, NB, 16])
            dve.wait_ge(load_sem["small2"], load_total["small2"])
            dve.tensor_scalar(v4(a4), acc2[:, :, 16:20], 1e-16, None, ALU.add)
            dve.drain()
            dve.reciprocal(a4, a4)
            dve.drain()
            for h in range(4):
                dve.tensor_tensor(A16[:, :, 4 * h:4 * h + 4], acc2[:, :, 4 * h:4 * h + 4],
                                  v4(a4)[:, :, h:h + 1].to_broadcast([P, NB, 4]), ALU.mult)
            dve.drain()
            dve.tensor_tensor(A16, A16, over_blocks(SMALL2[:, 0, :]), ALU.add)
            dve.drain()
            dve.tensor_reduce(mean, A16, AX.X, ALU.add)
            dve.drain()
            dve.tensor_scalar(mean, mean, 1.0 / 16, None, ALU.mult)
            dve.drain()
            dve.tensor_tensor(A16, A16, rep16(mean), ALU.subtract)
            dve.drain()
            dve.tensor_tensor(B16, A16, A16, ALU.mult)
            dve.drain()
            dve.tensor_reduce(rs16, B16, AX.X, ALU.add)
            dve.drain()
            dve.tensor_scalar(rs16, rs16, 1.0 / 16, 1e-5, ALU.mult, ALU.add)
            dve.drain().then_inc(root_go, 1)
            roots["asked"] += 1
            dve.wait_ge(root, roots["asked"])
            dve.reciprocal(rs16, rs16)
            dve.drain()
            dve.tensor_tensor(A16, A16, rep16(rs16), ALU.mult)
            dve.drain()
            dve.tensor_tensor(A16, A16, over_blocks(SMALL2[:, 1, :]), ALU.mult)
            dve.drain()
            dve.tensor_tensor(A16, A16, over_blocks(SMALL2[:, 2, :]), ALU.add)
            dve.drain()
            dve.tensor_reduce(v4(s4), A16.rearrange("p b (h e) -> p b e h", h=4), AX.X, ALU.add)
            dve.drain()
            dve.tensor_scalar(s4, s4, 0.25, None, ALU.mult)
            dve.drain()
            top2(dve, v4(s4), NB, 4, v4(a4), v4(c4), m4.rearrange("p (k b) -> p k b", k=4), EDN[:, :, :])

            def add_results(i, slot):
                dve.wait_ge(y_back[slot], 64 * (i + 1))
                dve.wait_ge(y_back[slot], 64)
                b0 = (4 * i + slot) * YB
                for e in range(4):
                    for k in range(YB):
                        to = block(X, b0 + k)
                        gate = EDN[:, bass.ds(b0 + k, 1), e:e + 1].rearrange("p a e -> p (a e)")
                        dve.scalar_tensor_tensor(out=to, in0=YC[slot][:, e, k, :], scalar=gate, in1=to, op0=ALU.mult, op1=ALU.add)
                    dve.drain()
                dve.drain().then_inc(x_done, 1)
            with dve.Fori(0, NB // YB // 4) as i:
                for slot in range(4):
                    add_results(i, slot)
            for slot in range(NB // YB % 4):
                add_results(NB // YB // 4, slot)

        @block_ctx.scalar
        def _(act):
            stats_scalar(act, RS[:, :])
            first.scalar(act)
            act.drain().then_inc(met, 1)
            act.wait_ge(met, MEETING * 1)
            es_gather.scalar(act, lambda g: ES0[:, bass.ds(g * 4 * QRT, 4 * QRT)].rearrange("p (t w) -> p t w", w=4))
            act.drain().then_inc(es_kept, 1)
            serve_exp(act, weights0.es)
            act.drain().then_inc(met, 1)
            act.wait_ge(met, MEETING * 2)
            sums0.scalar(act)
            act.drain().then_inc(met, 1)
            act.wait_ge(met, MEETING * 3)
            stats_scalar(act, RS[:, :])
            serve_exp(act, LOGITS)
            serve_exp(act, LOGITS)
            serve_exp(act, DIFF0)
            experts0.scalar(act)
            stats_scalar(act, RS[:, :])
            stats_scalar(act, RS[:, :])
            enter.scalar(act)
            act.drain().then_inc(met, 1)
            act.wait_ge(met, MEETING * 4)
            for l in range(3):
                hops[l].scalar(act)
                mixes[l].scalar(act)
                if l < 2:
                    act.drain().then_inc(met, 1)
                    act.wait_ge(met, MEETING * (5 + l))
            leave.scalar(act)
            stats_scalar(act, RS[:, :])
            project2.scalar(act)
            act.drain().then_inc(met, 1)
            act.wait_ge(met, MEETING * 7)
            act.wait_ge(load_sem["experts1"], load_total["experts1"])

            def store_result(i, e):
                act.wait_ge(experts1.added, 4 * i + e + 1)
                act.wait_ge(experts1.added, 1)
                dst = yD[e].rearrange("(b p) d -> p b d", p=P)[:, bass.ds(2 * i, 2), :]
                act.dma_start(dst, YS[:, e % 2, :].rearrange("p (j d) -> p j d", j=2)).then_inc(y_kept[e % 2], 16)

            def store_last(i, e, first):
                if e:
                    store_result(i, e - 1)
                elif not first:
                    store_result(i - 1, 3)
            experts1.scalar(act, store_last)
            store_result(NB // 2 - 1, 3)
            for a in range(2):
                act.wait_ge(y_kept[a], 16 * NB)
            act.wait_ge(experts1.mixed, 4 * NB // 2)
            spread2.loads(act)
            act.wait_ge(spread2.multiplied, 2 * spread2.steps)
            load(act, "dst2")
            serve_exp(act, weights2.es)
            act.wait_ge(weighted, 1)
            sums2.scalar(act)
            act.drain().then_inc(met, 1)
            act.wait_ge(met, MEETING * 8)
            stats_scalar(act, ar(27450, NB))
            serve_exp(act, DIFF1)

        @block_ctx.tensor
        def _(pe):
            first.tensor(pe)
            sort_tensor(pe, 0)
            count_tensor(pe, 0)
            tiles_tensor(pe, 0)
            pe.drain().then_inc(met, 1)
            pe.wait_ge(met, MEETING * 1)
            spread0.tensor(pe)
            for g in (1, 2):
                sort_tensor(pe, g)
                count_tensor(pe, g)
            for g in (1, 2):
                tiles_tensor(pe, g)
            weights0.tensor(pe)
            pe.drain().then_inc(met, 1)
            pe.wait_ge(met, MEETING * 2)
            sums0.tensor(pe)
            pe.drain().then_inc(met, 1)
            pe.wait_ge(met, MEETING * 3)
            pe.wait_ge(asked, nth("questions"))
            for k in range(2):
                m = pe.matmul(PB[2][:, k:k + 1], ar(W0 + 10000, D)[:, k * P:(k + 1) * P], ONES[:, 0:1], start=True, stop=True)
            m.then_inc(answered, 1)
            pe.wait_ge(asked, nth("questions"))
            for k in range(2):
                m = pe.matmul(PB[3][:, 0:8], ar(W0 + 10300, 2 * P)[:, k * P:(k + 1) * P], WRT[:, k, :], start=(k == 0), stop=(k == 1))
            m.then_inc(answered, 1)
            experts0.tensor(pe)
            enter.tensor(pe)
            pe.drain().then_inc(met, 1)
            pe.wait_ge(met, MEETING * 4)
            for l in range(3):
                hops[l].tensor(pe)
                mixes[l].tensor(pe)
                if l < 2:
                    pe.drain().then_inc(met, 1)
                    pe.wait_ge(met, MEETING * (5 + l))
            leave.tensor(pe)
            project2.tensor(pe)
            pe.drain().then_inc(met, 1)
            pe.wait_ge(met, MEETING * 7)
            pe.wait_ge(load_sem["experts1"], load_total["experts1"])
            experts1.tensor(pe)
            spread2.tensor(pe)
            weights2.tensor(pe)
            pe.wait_ge(weighted, 1)
            sums2.tensor(pe)
            pe.drain().then_inc(met, 1)
            pe.wait_ge(met, MEETING * 8)

        @block_ctx.gpsimd
        def _(pool):
            pool.iota(LOOPS[:, :], [[1, 50]], base=0, channel_multiplier=50)
            pool.drain().then_inc(loops_ready, 1)
            rows_pool(pool, 0)
            pool.drain().then_inc(met, 1)
            pool.wait_ge(met, MEETING * 1)
            es_gather.pool(pool)
            rows_pool(pool, 1)
            rows_pool(pool, 2)
            pool.drain().then_inc(met, 1)
            pool.wait_ge(met, MEETING * 2)
            sums0.pool(pool)
            pool.drain().then_inc(met, 1)
            pool.wait_ge(met, MEETING * 3)
            pool.drain().then_inc(met, 1)
            pool.wait_ge(met, MEETING * 4)
            for l in range(3):
                hops[l].pool(pool)
                if l < 2:
                    pool.drain().then_inc(met, 1)
                    pool.wait_ge(met, MEETING * (5 + l))
            pool.drain().then_inc(met, 1)
            pool.wait_ge(met, MEETING * 7)
            g1_gather.pool(pool)
            pool.drain().then_inc(met, 1)
            pool.wait_ge(met, MEETING * 8)

        @block_ctx.sync
        def _(sp):
            load(sp, "start")
            load(sp, "x")
            sp.wait_ge(zeroed, 1)
            load(sp, "x_end")
            chunk_stores(sp, tabD, Hv, D, first.taken, stored, 0)
            sp.dma_start(esD.rearrange("(b p) h -> p b h", p=P), ESN[:, :, :]).then_inc(stored, 16)
            sp.wait_ge(stored, 96)
            sort_sync(sp, 0)
            count_sync(sp, 0)
            tiles_sync(sp, 0)
            load(sp, "graph0")
            load(sp, "dst0")
            sp.wait_ge(load_sem["graph0"], load_total["graph0"])
            sp.wait_ge(load_sem["dst0"], load_total["dst0"])
            sp.drain().then_inc(met, 1)
            sp.wait_ge(met, MEETING * 1)
            spread0.loads(sp)
            for g in (1, 2):
                sort_sync(sp, g)
                count_sync(sp, g)
            for g in (1, 2):
                tiles_sync(sp, g)
            sp.drain().then_inc(met, 1)
            sp.wait_ge(met, MEETING * 2)
            sp.drain().then_inc(met, 1)
            sp.wait_ge(met, MEETING * 3)
            load(sp, "router")
            load(sp, "sage")
            load(sp, "graph1")
            load(sp, "bias0")
            sp.wait_ge(chosen, 1)
            for e in range(2):
                v = sp.value_load(IDSI[0:1, e:e + 1], min_val=0, max_val=7)
                one = lambda a: a[bass.ds(v, 1)]
                sp.dma_start(experts0.w1[e], one(A["L0_ffn_W1"]).rearrange("o (k p) n -> p (o k) n", p=P)).then_inc(chosen_in, 16)
                sp.dma_start(experts0.w2[e], one(A["L0_ffn_W2"]).rearrange("o (k p) n -> p (o k) n", p=P)).then_inc(chosen_in, 16)
                sp.dma_start(experts0.b1[e], one(A["L0_ffn_b1"]).rearrange("o (f p) -> p (o f)", p=P), allow_slow_non_contiguous=True).then_inc(chosen_in, 16)
                sp.dma_start(B2[:, e * D:(e + 1) * D], one(A["L0_ffn_b2"]).to_broadcast([P, D])).then_inc(chosen_in, 16)
            sp.wait_ge(load_sem["graph1"], load_total["graph1"])
            chunk_stores(sp, tabD, Hv, D, enter.taken, stored, 96)
            load(sp, "bias1")
            sp.wait_ge(load_sem["bias1"], load_total["bias1"])
            sp.drain().then_inc(met, 1)
            sp.wait_ge(met, MEETING * 4)
            for l in range(2):
                chunk_stores(sp, tabD, Hv, D, mixes[l].taken, stored, 176 + 80 * l)
                load(sp, f"bias{l + 2}")
                sp.wait_ge(load_sem[f"bias{l + 2}"], load_total[f"bias{l + 2}"])
                sp.drain().then_inc(met, 1)
                sp.wait_ge(met, MEETING * (5 + l))
            sp.wait_ge(sp_go, nth("goes"))
            load(sp, "bias4")
            load(sp, "graph2")
            sp.wait_ge(sp_go, nth("goes"))
            load(sp, "gat1")
            chunk_stores(sp, t20D, T20, 20, project2.taken, stored, 336)
            sp.wait_ge(load_sem["graph2"], load_total["graph2"])
            sp.drain().then_inc(met, 1)
            sp.wait_ge(met, MEETING * 7)
            load(sp, "experts1")
            g1_gather.sync(sp, lambda g: ar(ACC0, 1152 * 20)[:, bass.ds(g * 20 * QRT, 20 * QRT)])
            sp.drain().then_inc(met, 1)
            sp.wait_ge(met, MEETING * 8)
            load(sp, "small2")
            def fetch_results(c):
                for e in range(4):
                    src = yD[e][c * YB * P:(c + 1) * YB * P, :].rearrange("(b p) d -> p b d", p=P)
                    sp.dma_start(YC[c % 4][:, e, :, :], src).then_inc(y_back[c % 4], 16)
            for c in range(4):
                fetch_results(c)
            for c in range(NB // YB):
                sp.wait_ge(x_done, c + 1)
                if c + 4 < NB // YB:
                    fetch_results(c + 4)
                b0, b1 = c * YB, min((c + 1) * YB, EB - 1)
                sp.dma_start(out[b0 * P:b1 * P, :].rearrange("(b p) d -> p b d", p=P), X[:, b0:b1, :]).then_inc(finished, 16)
            sp.dma_start(out[(EB - 1) * P:N, :], X[0:last, EB - 1, :]).then_inc(finished, 16)
            sp.wait_ge(finished, 16 * (NB // YB + 1))


_INS = ["x", "src", "dst", "L0_gnn_W", "L0_gnn_a_src", "L0_gnn_a_dst", "L0_ffn_Wr", "L0_ffn_br", "L0_ffn_W1",
        "L0_ffn_b1", "L0_ffn_W2", "L0_ffn_b2", "L0_ffn_gamma", "L0_ffn_beta", "L1_gnn_W_in", "L1_gnn_b_in",
        "L1_gnn_W_agg", "L1_gnn_W_self", "L1_gnn_b_hid", "L1_gnn_W_out", "L1_gnn_b_out", "L1_ffn_W_gat",
        "L1_ffn_att_src", "L1_ffn_att_dst", "L1_ffn_b_gat", "L1_ffn_ln_gamma", "L1_ffn_ln_beta", "L1_ffn_W1",
        "L1_ffn_b1", "L1_ffn_W2", "L1_ffn_b2", "L1_ffn_edge_index"]


def kernel(**inputs):
    import concourse.bacc as _bacc
    from concourse.bass_utils import run_bass_kernel_spmd as _run

    nc = _bacc.Bacc("TRN2", target_bir_lowering=False, num_devices=1)
    arrays, aps = {}, {}
    consts, where, flips = host_constants()
    for name in _INS + ["consts", "flips"]:
        a = {"consts": consts, "flips": flips}.get(name)
        a = np.ascontiguousarray(inputs[name] if a is None else a)
        arrays[f"in_{name}"] = a
        aps[name] = nc.dram_tensor(f"in_{name}", a.shape, mybir.dt.from_np(a.dtype), kind="ExternalInput").ap()
    out = nc.dram_tensor("out_x", (N, D), F32, kind="ExternalOutput").ap()
    build_program(nc, aps, out, aps["consts"], aps["flips"], where)
    r = _run(nc, [arrays], core_ids=[0])
    return r.results[0]["out_x"]
```
